# Optimizing a Trainium2 kernel written in Bass

```python
import numpy as np
import jax
import jax.numpy as jnp

def _softmax(x, axis=-1):
    return jax.nn.softmax(x, axis=axis)

def _gelu(x):
    return jax.nn.gelu(x, approximate=True)

def _silu(x):
    return jax.nn.silu(x)

def _sigmoid(x):
    return jax.nn.sigmoid(x)

def _layernorm(x, axis=-1, eps=1e-05):
    m = jnp.mean(x, axis=axis, keepdims=True)
    v = jnp.var(x, axis=axis, keepdims=True)
    return (x - m) / jnp.sqrt(v + eps)

def _scatter_add(tgt, idx, src, axis=0):
    return tgt.at[idx].add(src)

def _segment_sum(src, seg, n):
    return jax.ops.segment_sum(src, seg, n)
kernel_name = 'mk_audio_tower_d1_tok_audfeat512_r4_205548'

def setup_inputs(seed: int=0):
    np.random.seed(seed)
    _w = jnp.asarray

    def _rec_inputs():
        import jax
        import jax.numpy as jnp
        _rk = jax.random.key(seed)
        x = -0.000356955 + 1 * jax.random.normal(jax.random.fold_in(_rk, 1), (64, 196, 96), jnp.float32)
        return x
    x = _rec_inputs()

    def _L0_tok_setup():
        import jax, jax.numpy as jnp
        import numpy as np
        import itertools
        B, RES, RES_, STRIDE = (64, 14, 7, 2)
        N, N_ = (RES * RES, RES_ * RES_)
        IN_DIM, OUT_DIM = (96, 128)
        H, KD, AR = (12, 32, 2)
        D = AR * KD
        DH = D * H
        NH_KD = KD * H
        KV_H = DH + NH_KD
        EPS = 1e-05

        def _bias_idxs():
            points = list(itertools.product(range(RES), range(RES)))
            points_ = list(itertools.product(range(RES_), range(RES_)))
            offsets, idxs = ({}, [])
            for p1 in points_:
                for p2 in points:
                    off = (abs(p1[0] * STRIDE - p2[0]), abs(p1[1] * STRIDE - p2[1]))
                    if off not in offsets:
                        offsets[off] = len(offsets)
                    idxs.append(offsets[off])
            return (np.array(idxs, dtype=np.int32).reshape(N_, N), len(offsets))

        def linear_bn(x, w, gamma, beta, mean, var):
            s = gamma / jnp.sqrt(var + EPS)
            return jnp.matmul(x, w.T) * s + (beta - mean * s)
        key = jax.random.key(seed)
        ks = jax.random.split(key, 12)
        idxs_np, n_off = _bias_idxs()

        def bn_params(k, dim):
            k1, k2, k3, k4 = jax.random.split(k, 4)
            return (jax.random.normal(k1, (dim,)) * 0.1 + 1.0, jax.random.normal(k2, (dim,)) * 0.1, jax.random.normal(k3, (dim,)) * 0.1, jax.random.uniform(k4, (dim,), minval=0.5, maxval=1.5))
        kv_g, kv_b, kv_m, kv_v = bn_params(ks[1], KV_H)
        q_g, q_b, q_m, q_v = bn_params(ks[3], NH_KD)
        pr_g, pr_b, pr_m, pr_v = bn_params(ks[5], OUT_DIM)
        return {'x': jax.random.normal(ks[0], (B, N, IN_DIM), dtype=jnp.float32), 'kv_w': jax.random.normal(ks[6], (KV_H, IN_DIM), dtype=jnp.float32) * IN_DIM ** (-0.5), 'kv_g': kv_g, 'kv_b': kv_b, 'kv_m': kv_m, 'kv_v': kv_v, 'q_w': jax.random.normal(ks[7], (NH_KD, IN_DIM), dtype=jnp.float32) * IN_DIM ** (-0.5), 'q_g': q_g, 'q_b': q_b, 'q_m': q_m, 'q_v': q_v, 'proj_w': jax.random.normal(ks[8], (OUT_DIM, DH), dtype=jnp.float32) * DH ** (-0.5), 'proj_g': pr_g, 'proj_b': pr_b, 'proj_m': pr_m, 'proj_v': pr_v, 'attention_biases': jax.random.normal(ks[9], (H, n_off), dtype=jnp.float32) * 0.02, 'bias_idxs': jnp.asarray(idxs_np)}
    _L0_tok_all = _L0_tok_setup()
    _L0_tok_in = {k: v for k, v in _L0_tok_all.items() if k in ('kv_w', 'kv_g', 'kv_b', 'kv_m', 'kv_v', 'q_w', 'q_g', 'q_b', 'q_m', 'q_v', 'proj_w', 'proj_g', 'proj_b', 'proj_m', 'proj_v', 'attention_biases', 'bias_idxs')}
    del _L0_tok_all

    def _L0_attn_setup():
        import jax, jax.numpy as jnp
        import numpy as np
        import math
        D_MODEL = 128
        NUM_HEADS = 8
        HEAD_DIM = D_MODEL // NUM_HEADS
        B, L = (2, 512)
        LN_EPS = 1e-05
        DEN_EPS = 1e-05
        key = jax.random.key(seed)
        ks = jax.random.split(key, 6)
        s = 1.0 / math.sqrt(D_MODEL)
        return {'x': jax.random.normal(ks[0], (B, L, D_MODEL), dtype=jnp.float32), 'Wqkv': jax.random.normal(ks[1], (D_MODEL, 3 * D_MODEL), dtype=jnp.float32) * s, 'bqkv': jnp.zeros((3 * D_MODEL,), dtype=jnp.float32), 'Wout': jax.random.normal(ks[2], (D_MODEL, D_MODEL), dtype=jnp.float32) * s, 'bout': jnp.zeros((D_MODEL,), dtype=jnp.float32), 'ln_gamma': jnp.ones((D_MODEL,), dtype=jnp.float32), 'ln_beta': jnp.zeros((D_MODEL,), dtype=jnp.float32), 'decay_logits': jnp.full((NUM_HEADS,), 5.0, dtype=jnp.float32)}
    _L0_attn_all = _L0_attn_setup()
    _L0_attn_in = {k: v for k, v in _L0_attn_all.items() if k in ('Wqkv', 'bqkv', 'Wout', 'bout', 'ln_gamma', 'ln_beta', 'decay_logits')}
    del _L0_attn_all

    def _L0_ffn_setup():
        import jax, jax.numpy as jnp
        import numpy as np
        B, N, DIM = (1, 512, 128)
        DH, H = (64, 8)
        E, FF = (8, 512)

        def _layernorm(x, g, b, eps=1e-05):
            mu = jnp.mean(x, axis=-1, keepdims=True)
            var = jnp.mean(jnp.square(x - mu), axis=-1, keepdims=True)
            return (x - mu) * jax.lax.rsqrt(var + eps) * g + b

        def _l2norm(x, eps=1e-12):
            return x / jnp.sqrt(jnp.sum(jnp.square(x), axis=-1, keepdims=True) + eps)
        key = jax.random.key(seed)
        ks = jax.random.split(key, 12)
        g = lambda k, shape: jax.random.normal(k, shape, jnp.float32) * 0.02
        return {'x': jax.random.normal(ks[0], (B, N, DIM), jnp.float32), 'ln_g': jnp.ones((DIM,), jnp.float32), 'ln_b': jnp.zeros((DIM,), jnp.float32), 'Wq': g(ks[1], (DIM, DIM)), 'Wk': g(ks[2], (DIM, DIM)), 'Wv': g(ks[3], (DIM, DIM)), 'Wo': g(ks[4], (DIM, DIM)), 'qn_g': jnp.ones((DH,), jnp.float32), 'kn_g': jnp.ones((DH,), jnp.float32), 'gate_W': g(ks[5], (DIM, E)), 'gate_b': jnp.zeros((E,), jnp.float32), 'W1': g(ks[6], (E, DIM, FF)), 'b1': jnp.zeros((E, FF), jnp.float32), 'W2': g(ks[7], (E, FF, DIM)), 'b2': jnp.zeros((E, DIM), jnp.float32)}
    _L0_ffn_all = _L0_ffn_setup()
    _L0_ffn_in = {k: v for k, v in _L0_ffn_all.items() if k in ('ln_g', 'ln_b', 'Wq', 'Wk', 'Wv', 'Wo', 'qn_g', 'kn_g', 'gate_W', 'gate_b', 'W1', 'b1', 'W2', 'b2')}
    del _L0_ffn_all
    return {'x': x, 'L0_tok_kv_w': _L0_tok_in['kv_w'], 'L0_tok_kv_g': _L0_tok_in['kv_g'], 'L0_tok_kv_b': _L0_tok_in['kv_b'], 'L0_tok_kv_m': _L0_tok_in['kv_m'], 'L0_tok_kv_v': _L0_tok_in['kv_v'], 'L0_tok_q_w': _L0_tok_in['q_w'], 'L0_tok_q_g': _L0_tok_in['q_g'], 'L0_tok_q_b': _L0_tok_in['q_b'], 'L0_tok_q_m': _L0_tok_in['q_m'], 'L0_tok_q_v': _L0_tok_in['q_v'], 'L0_tok_proj_w': _L0_tok_in['proj_w'], 'L0_tok_proj_g': _L0_tok_in['proj_g'], 'L0_tok_proj_b': _L0_tok_in['proj_b'], 'L0_tok_proj_m': _L0_tok_in['proj_m'], 'L0_tok_proj_v': _L0_tok_in['proj_v'], 'L0_tok_attention_biases': _L0_tok_in['attention_biases'], 'L0_tok_bias_idxs': _L0_tok_in['bias_idxs'], 'L0_attn_Wqkv': _L0_attn_in['Wqkv'], 'L0_attn_bqkv': _L0_attn_in['bqkv'], 'L0_attn_Wout': _L0_attn_in['Wout'], 'L0_attn_bout': _L0_attn_in['bout'], 'L0_attn_ln_gamma': _L0_attn_in['ln_gamma'], 'L0_attn_ln_beta': _L0_attn_in['ln_beta'], 'L0_attn_decay_logits': _L0_attn_in['decay_logits'], 'L0_ffn_ln_g': _L0_ffn_in['ln_g'], 'L0_ffn_ln_b': _L0_ffn_in['ln_b'], 'L0_ffn_Wq': _L0_ffn_in['Wq'], 'L0_ffn_Wk': _L0_ffn_in['Wk'], 'L0_ffn_Wv': _L0_ffn_in['Wv'], 'L0_ffn_Wo': _L0_ffn_in['Wo'], 'L0_ffn_qn_g': _L0_ffn_in['qn_g'], 'L0_ffn_kn_g': _L0_ffn_in['kn_g'], 'L0_ffn_gate_W': _L0_ffn_in['gate_W'], 'L0_ffn_gate_b': _L0_ffn_in['gate_b'], 'L0_ffn_W1': _L0_ffn_in['W1'], 'L0_ffn_b1': _L0_ffn_in['b1'], 'L0_ffn_W2': _L0_ffn_in['W2'], 'L0_ffn_b2': _L0_ffn_in['b2']}

def reference(x, L0_tok_kv_w, L0_tok_kv_g, L0_tok_kv_b, L0_tok_kv_m, L0_tok_kv_v, L0_tok_q_w, L0_tok_q_g, L0_tok_q_b, L0_tok_q_m, L0_tok_q_v, L0_tok_proj_w, L0_tok_proj_g, L0_tok_proj_b, L0_tok_proj_m, L0_tok_proj_v, L0_tok_attention_biases, L0_tok_bias_idxs, L0_attn_Wqkv, L0_attn_bqkv, L0_attn_Wout, L0_attn_bout, L0_attn_ln_gamma, L0_attn_ln_beta, L0_attn_decay_logits, L0_ffn_ln_g, L0_ffn_ln_b, L0_ffn_Wq, L0_ffn_Wk, L0_ffn_Wv, L0_ffn_Wo, L0_ffn_qn_g, L0_ffn_kn_g, L0_ffn_gate_W, L0_ffn_gate_b, L0_ffn_W1, L0_ffn_b1, L0_ffn_W2, L0_ffn_b2):
    import jax
    import jax.numpy as jnp

    def _L0_tok_ref(x, kv_w, kv_g, kv_b, kv_m, kv_v, q_w, q_g, q_b, q_m, q_v, proj_w, proj_g, proj_b, proj_m, proj_v, attention_biases, bias_idxs):
        import jax, jax.numpy as jnp
        import numpy as np
        import itertools
        B, RES, RES_, STRIDE = (64, 14, 7, 2)
        N, N_ = (RES * RES, RES_ * RES_)
        IN_DIM, OUT_DIM = (96, 128)
        H, KD, AR = (12, 32, 2)
        D = AR * KD
        DH = D * H
        NH_KD = KD * H
        KV_H = DH + NH_KD
        EPS = 1e-05

        def _bias_idxs():
            points = list(itertools.product(range(RES), range(RES)))
            points_ = list(itertools.product(range(RES_), range(RES_)))
            offsets, idxs = ({}, [])
            for p1 in points_:
                for p2 in points:
                    off = (abs(p1[0] * STRIDE - p2[0]), abs(p1[1] * STRIDE - p2[1]))
                    if off not in offsets:
                        offsets[off] = len(offsets)
                    idxs.append(offsets[off])
            return (np.array(idxs, dtype=np.int32).reshape(N_, N), len(offsets))

        def linear_bn(x, w, gamma, beta, mean, var):
            s = gamma / jnp.sqrt(var + EPS)
            return jnp.matmul(x, w.T) * s + (beta - mean * s)
        Bsz = x.shape[0]
        scale = KD ** (-0.5)
        kv = linear_bn(x, kv_w, kv_g, kv_b, kv_m, kv_v).reshape(Bsz, N, H, KD + D)
        k, v = (kv[..., :KD], kv[..., KD:])
        xs = x.reshape(Bsz, RES, RES, IN_DIM)[:, ::STRIDE, ::STRIDE].reshape(Bsz, N_, IN_DIM)
        q = linear_bn(xs, q_w, q_g, q_b, q_m, q_v).reshape(Bsz, N_, H, KD)
        bias = attention_biases[:, bias_idxs]
        attn = jnp.einsum('bqhd,bkhd->bhqk', q, k) * scale + bias
        attn = jax.nn.softmax(attn, axis=-1)
        out = jnp.einsum('bhqk,bkhd->bqhd', attn, v).reshape(Bsz, N_, DH)
        out = jax.nn.hard_swish(out)
        return linear_bn(out, proj_w, proj_g, proj_b, proj_m, proj_v)

    def _L0_attn_ref(x, Wqkv, bqkv, Wout, bout, ln_gamma, ln_beta, decay_logits):
        import jax, jax.numpy as jnp
        import numpy as np
        import math
        D_MODEL = 128
        NUM_HEADS = 8
        HEAD_DIM = D_MODEL // NUM_HEADS
        B, L = (2, 512)
        LN_EPS = 1e-05
        DEN_EPS = 1e-05
        Bv, Lv, D = x.shape
        H = decay_logits.shape[0]
        E = D // H
        qkv = x @ Wqkv + bqkv
        q, k, v = jnp.split(qkv, 3, axis=-1)
        q = q.reshape(Bv, Lv, H, E)
        k = k.reshape(Bv, Lv, H, E)
        v = v.reshape(Bv, Lv, H, E)
        q = (jax.nn.elu(q) + 1.0) / jnp.sqrt(jnp.asarray(E, x.dtype))
        k = jax.nn.elu(k) + 1.0
        lambdas = jax.nn.sigmoid(decay_logits).reshape(1, 1, H, 1)
        t = jnp.arange(Lv, dtype=x.dtype).reshape(1, Lv, 1, 1)
        decay_k = jnp.power(lambdas, -t)
        decay_q = jnp.power(lambdas, t)
        k_dec = k * decay_k
        kv = jnp.einsum('blhe,blhf->blhef', k_dec, v)
        memory = jnp.cumsum(kv, axis=1)
        k_sum = jnp.cumsum(k_dec, axis=1)
        q_dec = q * decay_q
        num = jnp.einsum('blhe,blhef->blhf', q_dec, memory)
        den = jnp.einsum('blhe,blhe->blh', q_dec, k_sum)[..., None] + DEN_EPS
        out = (num / den).reshape(Bv, Lv, D)
        out = out @ Wout + bout
        mu = jnp.mean(out, axis=-1, keepdims=True)
        var = jnp.var(out, axis=-1, keepdims=True)
        out = (out - mu) / jnp.sqrt(var + LN_EPS) * ln_gamma + ln_beta
        return out

    def _L0_ffn_ref(x, ln_g, ln_b, Wq, Wk, Wv, Wo, qn_g, kn_g, gate_W, gate_b, W1, b1, W2, b2):
        import jax, jax.numpy as jnp
        import numpy as np
        B, N, DIM = (1, 512, 128)
        DH, H = (64, 8)
        E, FF = (8, 512)

        def _layernorm(x, g, b, eps=1e-05):
            mu = jnp.mean(x, axis=-1, keepdims=True)
            var = jnp.mean(jnp.square(x - mu), axis=-1, keepdims=True)
            return (x - mu) * jax.lax.rsqrt(var + eps) * g + b

        def _l2norm(x, eps=1e-12):
            return x / jnp.sqrt(jnp.sum(jnp.square(x), axis=-1, keepdims=True) + eps)
        b, n, d = x.shape
        dh = qn_g.shape[0]
        h = d // dh
        hx = _layernorm(x, ln_g, ln_b)
        q = (hx @ Wq).reshape(b, n, h, dh).transpose(0, 2, 1, 3)
        k = (hx @ Wk).reshape(b, n, h, dh).transpose(0, 2, 1, 3)
        v = (hx @ Wv).reshape(b, n, h, dh).transpose(0, 2, 1, 3)
        scale = jnp.sqrt(jnp.float32(dh))
        q = _l2norm(q) * scale * qn_g
        k = _l2norm(k) * scale * kn_g
        scores = jnp.einsum('bhqd,bhkd->bhqk', q, k) * dh ** (-0.5)
        causal = jnp.tril(jnp.ones((n, n), bool))
        scores = jnp.where(causal, scores, jnp.finfo(scores.dtype).min)
        attn = jax.nn.softmax(scores, axis=-1)
        o = jnp.einsum('bhqk,bhkd->bhqd', attn, v)
        y = o.transpose(0, 2, 1, 3).reshape(b, n, d) @ Wo
        gate = jax.nn.softmax(y @ gate_W + gate_b, axis=-1)
        hid = jax.nn.gelu(jnp.einsum('bnd,edf->bnef', y, W1) + b1)
        eo = jnp.einsum('bnef,efd->bned', hid, W2) + b2
        out = jnp.einsum('bned,bne->bnd', eo, gate)
        return out
    h = _L0_tok_ref(x, L0_tok_kv_w, L0_tok_kv_g, L0_tok_kv_b, L0_tok_kv_m, L0_tok_kv_v, L0_tok_q_w, L0_tok_q_g, L0_tok_q_b, L0_tok_q_m, L0_tok_q_v, L0_tok_proj_w, L0_tok_proj_g, L0_tok_proj_b, L0_tok_proj_m, L0_tok_proj_v, L0_tok_attention_biases, L0_tok_bias_idxs)
    h = h + _L0_attn_ref(_layernorm(h, axis=-1), L0_attn_Wqkv, L0_attn_bqkv, L0_attn_Wout, L0_attn_bout, L0_attn_ln_gamma, L0_attn_ln_beta, L0_attn_decay_logits)
    h = h + _L0_ffn_ref(_layernorm(h, axis=-1), L0_ffn_ln_g, L0_ffn_ln_b, L0_ffn_Wq, L0_ffn_Wk, L0_ffn_Wv, L0_ffn_Wo, L0_ffn_qn_g, L0_ffn_kn_g, L0_ffn_gate_W, L0_ffn_gate_b, L0_ffn_W1, L0_ffn_b1, L0_ffn_W2, L0_ffn_b2)
    return h

_drawn_inputs = setup_inputs


def setup_inputs(seed=0):
    import zlib

    import numpy as np

    out = dict(_drawn_inputs(seed))
    spreads = {'L0_attn_bqkv': (0.0, 0.1),
     'L0_attn_bout': (0.0, 0.1),
     'L0_attn_ln_gamma': (1.0, 0.2),
     'L0_attn_ln_beta': (0.0, 0.1),
     'L0_attn_decay_logits': (5.0, 0.6),
     'L0_ffn_ln_g': (1.0, 0.6),
     'L0_ffn_ln_b': (0.0, 0.8),
     'L0_ffn_qn_g': (1.0, 0.6),
     'L0_ffn_kn_g': (1.0, 0.6),
     'L0_ffn_gate_b': (0.0, 0.8),
     'L0_ffn_b1': (0.0, 0.8),
     'L0_ffn_b2': (0.0, 0.8)}
    factors = {'L0_tok_attention_biases': 8.0,
     'L0_ffn_Wq': 8.0,
     'L0_ffn_Wk': 8.0,
     'L0_ffn_Wv': 8.0,
     'L0_ffn_Wo': 8.0,
     'L0_ffn_gate_W': 8.0,
     'L0_ffn_W1': 8.0,
     'L0_ffn_W2': 6.734}
    for name, (base, spread) in spreads.items():
        noise = np.random.default_rng([zlib.crc32(name.encode()), seed]).standard_normal(out[name].shape)
        drawn = base * np.exp(spread * noise) if base else spread * noise
        out[name] = jnp.asarray(drawn.astype(out[name].dtype))
    for name, factor in factors.items():
        out[name] = (out[name] * factor).astype(out[name].dtype)
    return out
```

```python
from contextlib import ExitStack

import concourse.bass as bass
import numpy as np
from concourse import mybir

F32 = mybir.dt.float32
I32 = mybir.dt.int32
ALU = mybir.AluOpType
ACT = mybir.ActivationFunctionType
AX = mybir.AxisListType

BATCH, RES, OUT_RES, CIN = 64, 14, 7, 96
KPOS, QPOS = RES * RES, OUT_RES * OUT_RES
HEADS, KD, VD = 12, 32, 64
D = 128
LHEADS, LHD = 8, 16
FHEADS, FHD = 2, 64
EXPERTS, FF = 8, 512
NOFF = 196
EPS = 1e-5

NB = 8
GROUPS = BATCH // NB
TOK = NB * QPOS
CA = CIN + 1
HALF = KPOS // 2
ROWS = HEADS * QPOS
TILES = 5
MT = 118
PAIR = 2 * QPOS
PAIRS = NB // 2
FCH = FF // 128
NEG = -3.0e38


def tile_rows(t):
    return min(MT, ROWS - MT * t)


C_ID, C_CENTER, C_MEAN, C_HEADSUM, C_CAUSAL, C_ADDMASK, C_HMASK, C_T, C_IOTA = (
    0, 128, 256, 384, 512, 610, 708, 716, 765)
C_EPS = 767
NCONST = 772

P_PROJ, P_BQ, P_BK, P_BOUT, P_GAMMA, P_BETA, P_FG, P_FB, P_QN, P_KN, P_DEC, P_B1, P_B2, P_BNQ, P_BNK, P_BNV = (
    0, 4, 5, 6, 7, 8, 9, 10, 11, 12, 13, 14, 46, 54, 102, 150)
NPAR = 198


class Steps:

    def __init__(self, sem, names):
        self.sem, self.names = sem, names
        self.index = {n: i for i, n in enumerate(names)}
        self.per_group = len(names)
        self.told = 0

    def at(self, g, name, back=0):
        return (g + 1 - back) * self.per_group + self.index[name] + 1

    def tell(self, name):
        assert self.names[self.told % self.per_group] == name, (name, self.names[self.told % self.per_group])
        self.told += 1
        return self.sem


def wide(ap, axis, n):
    shape = list(ap.shape)
    return ap.unsqueeze(axis).broadcast_to(tuple(shape[:axis] + [n] + shape[axis:]))


def steps_a():
    pe = [f"qk{h}" for h in range(HEADS)]
    act = [f"qk{h}" for h in range(0, HEADS, 2)]
    dve = [f"qk{h}" for h in range(1, HEADS, 2)]
    pool = []
    for b in range(NB):
        pe += [f"s{b}.{j}" for j in range(3)] + [f"tr{b}.{j}" for j in range(3)] + [f"t{b}.{n}" for n in range(2)]
        act += [f"exp{b}.{t}" for t in range(TILES)] + [f"pt{b}.0", f"pt{b}.2", f"tt{b}.0"]
        dve += [f"neg{b}.{t}" for t in range(TILES)] + [f"rec{b}", f"pt{b}.1", f"tt{b}.1"]
        pool += [f"norm{b}.{t}" for t in range(TILES)]
    pe += [f"wv{j}" for j in range(HEADS // 2)]
    act += [f"relu{j}" for j in range(HEADS // 2)]
    dve += [f"hs{j}" for j in range(HEADS // 2)]
    return pe, act, dve, pool


def steps_b():
    pe = ["proj", "c1", "v1", "q", "k", "v"]
    act = ["h1", "c1", "sq1", "ln1", "rs1", "eq", "pq", "ek", "pk"]
    dve = ["hn", "q", "k", "v"]
    pool = ["q", "k"]
    for p in range(PAIRS):
        pool += [f"qm{p}"]
        pe += [f"a{p}.0", f"a{p}.1"]
        dve += [f"a{p}.0", f"a{p}.1"]
        if p % 2:
            pe += [f"num{p // 2}"]
            dve += [f"den{p // 2}", f"rden{p // 2}", f"o{p // 2}"]
    pe += ["oT", "wout", "c2", "v2", "c3", "v3", "q2", "qss", "k2", "kss", "vx", "s0", "s1", "pT0", "pT1", "av", "wo",
           "g", "gT"]
    act += ["oT", "a2", "c2", "sq2", "ln2", "rs2", "c3", "sq3", "ln3", "rs3", "q2", "qsq", "qln", "qrs",
            "k2", "ksq", "kln", "krs", "vx", "e0", "e1", "pT0", "pT1", "o2T", "y", "gexp"]
    dve += ["ga", "h2", "gx", "hx", "q2n", "k2n", "sm0", "mx0", "sub0", "sm1", "mx1", "sub1",
            "sum0", "rc0", "pn0", "sum1", "rc1", "pn1", "g", "gmx", "gsub", "gsum", "grc", "gn", "gT"]
    return pe, act, dve, pool


def steps_c():
    ej = [(e, j) for e in range(EXPERTS) for j in range(FCH)]
    pe = []
    for n, (e, j) in enumerate(ej):
        pe += [f"u{e}.{j}"]
        if n:
            pe += ["d%d.%d" % ej[n - 1]]
    pe += ["d%d.%d" % ej[-1], "ot"]
    act = [f"g{e}.{j}" for e, j in ej] + ["ot"]
    dve = ["yc", "acc"]
    for e in range(EXPERTS):
        dve += [f"m{e}", f"acc{e}"]
    return pe, act, dve


def audio_tower_kernel(nc, xT, xn, consts, params, qw, kw, vw, pw, ab, idxs, wqkv, bqkv, wout, fwq, fwk, fwv, fwo,
                       gw, gb, w1, w2, bias_dram, gate_dram, out):
    with ExitStack() as ctx:
        def sb(name, shape, dt=F32):
            return ctx.enter_context(nc.sbuf_tensor(name, shape, dt))

        def sem(name):
            return ctx.enter_context(nc.semaphore(name))

        cst = sb("cst", [128, NCONST])
        par = sb("par", [128, NPAR])
        ident = cst[:, C_ID:C_ID + 128]
        center = cst[:, C_CENTER:C_CENTER + 128]
        mean = cst[:, C_MEAN:C_MEAN + 128]
        headsum = cst[:, C_HEADSUM:C_HEADSUM + 128]
        causal = cst[0:PAIR, C_CAUSAL:C_CAUSAL + PAIR]
        addmask = cst[0:PAIR, C_ADDMASK:C_ADDMASK + PAIR]
        hmask = cst[:, C_HMASK:C_HMASK + LHEADS]
        eps_col = cst[:, C_EPS:C_EPS + 1]
        eps2_col = cst[:, C_EPS + 1:C_EPS + 2]
        eps12_col = cst[:, C_EPS + 2:C_EPS + 3]
        one_col = cst[:, C_EPS + 3:C_EPS + 4]
        three_col = cst[:, C_EPS + 4:C_EPS + 5]
        abt = sb("abt", [HALF, 2, HEADS])
        wqkv_s = sb("wqkv_s", [D, 3 * D])
        wout_s = sb("wout_s", [D, D])
        fw = sb("fw", [D, 4, D])
        gws = sb("gws", [D, EXPERTS])
        gbs = sb("gbs", [PAIR, EXPERTS])
        bvs = sb("bvs", [PAIR, D])
        w1s = sb("w1s", [D, EXPERTS, FF])
        w2s = sb("w2s", [D, EXPERTS * FCH, D])
        mqk = sb("mqk", [CA, HEADS, CA])
        wvT = sb("wvT", [CA, HEADS, VD])
        pwT = sb("pwT", [D, HEADS // 2, D])
        bias = sb("bias", [MT, TILES, KPOS])
        bn = sb("bn", [128, 6, HEADS])
        proj_s = sb("proj_s", [128, 4])
        decq = sb("decq", [128, QPOS])
        deck = sb("deck", [128, QPOS])
        nl = sb("nl", [128, 3])
        fg2 = sb("fg2", [128, 2])

        xa = sb("xa", [CA, NB, KPOS])
        xp = sb("xp", [HALF, NB, 2, CA])
        qp_all = sb("qp", [128, NB, ROWS])
        qp = qp_all[0:CA, :, :]
        sneg = sb("sneg", [MT, TILES, KPOS])
        prob = sb("prob", [MT, TILES, KPOS])
        stat = sb("stat", [MT, 3, 8])
        pT = sb("pT", [HALF, 2, ROWS])
        tT_all = sb("tT", [128, HEADS, TOK])
        tT = tT_all[0:CA, :, :]
        relu = sb("relu", [128, 2, TOK])
        hs = sb("hs", [128, HEADS // 2, TOK])

        def feat(name):
            return sb(name, [128, TOK])
        h1T, cT, sq, lnb, r, hnT = feat("h1T"), feat("cT"), feat("sq"), feat("lnb"), feat("r"), feat("hnT")
        eq, pq, ek, pk, qd, kd, qT, kT = (feat(n) for n in ("eq", "pq", "ek", "pk", "qd", "kd", "qT", "kT"))
        ga, gx, q2T, k2T, q2n, k2n = eq, pq, ek, pk, qd, kd
        v1 = sb("v1", [PAIR, PAIRS, LHEADS, LHD + 1])
        qm = sb("qm", [128, 2, LHEADS, PAIR])
        aT = sb("aT", [PAIR, 2, LHEADS, PAIR])
        den = sb("den", [PAIR, 2, 16])
        lo = sb("lo", [PAIR, PAIRS, D])
        oT, a2T, h2T, hxT, r2 = (feat(n) for n in ("oT", "a2T", "h2T", "hxT", "r2"))
        v2 = sb("v2", [PAIR, PAIRS, D])
        s2, p2 = (aT[:, i, :, :].rearrange("p (h n) q -> p h n q", h=FHEADS) for i in range(2))
        st2 = sb("st2", [PAIR, 3, FHEADS, PAIRS])
        p2T = qm[0:PAIR, 0, :, :].rearrange("p (h n) q -> p h n q", h=FHEADS)
        o2T, yT = feat("o2T"), feat("yT")
        gl = sb("gl", [PAIR, 3, PAIRS, EXPERTS])
        gst = sb("gst", [PAIR, 3, PAIRS])
        gT = sb("gT", [EXPERTS, TOK])

        yc, acc = feat("yc"), feat("acc")
        gbc = sb("gbc", [128, EXPERTS, TOK])
        hid = sb("hid", [128, 2, TOK])
        tmp = feat("tmp")
        outs = sb("outs", [PAIR, PAIRS, D])

        early = hs[0:KD, :, :].rearrange("p a b -> p (a b)")
        qwa, kwa = (early[:, i * HEADS * CA:(i + 1) * HEADS * CA].rearrange("p (h c) -> p h c", h=HEADS) for i in range(2))
        late = gbc[:, :, :].rearrange("p a b -> p (a b)")
        vwa = late[0:VD, 0:HEADS * CA].rearrange("p (h c) -> p h c", h=HEADS)
        pws = late[:, HEADS * CA:HEADS * CA + HEADS * VD]
        idx_i = tT_all[0:HALF, 0:4, :].rearrange("p a b -> p (a b)")[:, 0:1372].bitcast(I32)
        idx_f = tT_all[0:HALF, 4:8, :].rearrange("p a b -> p (a b)")[:, 0:1372]
        onehot = [qp_all[0:HALF, 3 * c:3 * c + 3, :].rearrange("p a b -> p (a b)")[:, 0:1372] for c in range(2)]
        bias_rows = tT_all[0:HEADS, 8:12, :].rearrange("p a b -> p (a b)")[:, 0:1372]

        def bank(name):
            return ctx.enter_context(nc.psum_tensor(name, [128, 512], F32))
        ps_s = [bank(f"ps_s{j}") for j in range(3)]
        ps_t = [bank(f"ps_t{n}") for n in range(2)]
        ps_b, ps_h, ps_e = bank("ps_b"), bank("ps_h"), bank("ps_e")

        pe_a, act_a, dve_a, pool_a = (Steps(sem(n), s) for n, s in zip(("pe_a", "act_a", "dve_a", "pool_a"), steps_a()))
        pe_b, act_b, dve_b, pool_b = (Steps(sem(n), s) for n, s in zip(("pe_b", "act_b", "dve_b", "pool_b"), steps_b()))
        pe_c, act_c, dve_c = (Steps(sem(n), s) for n, s in zip(("pe_c", "act_c", "dve_c"), steps_c()))

        def start_at_one_group(eng, *stages):
            for s in stages:
                eng.sem_inc(s.sem, s.per_group)

        dve_waited, pool_waited = sem("dve_waited"), sem("pool_waited")
        xa_in = [sem(f"xa_in{b}") for b in range(NB)]
        xp_in = [sem(f"xp_in{b}") for b in range(NB)]
        gate_out, gate_in, out_done = sem("gate_out"), sem("gate_in"), sem("out_done")
        consts_in, attn_w_in, ffn_w_in, w1_in, w2_in = (
            sem(n) for n in ("consts_in", "attn_w_in", "ffn_w_in", "w1_in", "w2_in"))
        idx_in, bias_out, bias_in = sem("idx_in"), sem("bias_out"), sem("bias_in")
        dve_set, act_set, pe_set, ones_set = sem("dve_set"), sem("act_set"), sem("pe_set"), sem("ones_set")
        NCHUNK = 7
        CHUNK = QPOS * KPOS // NCHUNK
        NSUB = 4
        SUB = CHUNK // NSUB

        BN_STEPS = 6
        IDX_READ = 4 * BN_STEPS + 7
        ACT_BIAS = 9 + HEADS + HEADS // 2
        PE_BIAS = HEADS + HEADS // 2 + 3

        def pT_evac(j):
            if j == 2:
                m = tile_rows(TILES - 1)
                return (pT[:, :, 4 * MT:ROWS], ps_s[2][0:HALF, 0:2 * MT].rearrange("p (c q) -> p c q", c=2)[:, :, 0:m])
            return (pT[:, :, 2 * MT * j:2 * MT * (j + 1)].rearrange("p c (t q) -> p t c q", t=2),
                    ps_s[j][0:HALF, 0:4 * MT].rearrange("p (t c q) -> p t c q", t=2, c=2))

        def tT_evac(b, n):
            return (tT[:, 6 * n:6 * n + 6, b * QPOS:(b + 1) * QPOS],
                    ps_t[n][0:CA, 0:6 * QPOS].rearrange("p (h q) -> p h q", h=6))

        block = ctx.enter_context(nc.Block())

        @block.sync
        def _(sp):
            sp.sem_inc(gate_out, 16)
            sp.sem_inc(out_done, 16)
            sp.dma_start(cst[:, :], consts).then_inc(consts_in, 16)
            sp.dma_start(par[:, :], params).then_inc(consts_in, 16)
            sp.dma_start(qwa[:, :, 0:CIN], qw).then_inc(consts_in, 16)
            sp.dma_start(kwa[:, :, 0:CIN], kw).then_inc(consts_in, 16)
            sp.dma_start(vwa[:, :, 0:CIN], vw).then_inc(consts_in, 16)
            sp.dma_start(pws[:, :], pw).then_inc(consts_in, 16)
            sp.dma_start(abt[:, :, :], ab).then_inc(consts_in, 16)

            def load_x(g, b):
                sp.wait_ge(pe_a.sem, pe_a.at(g, f"s{b}.2", back=1))
                sp.dma_start(xa[0:CIN, b, :], xT[:, bass.ds((g * NB + b) * KPOS, KPOS)]).then_inc(xa_in[b], 16)
                sp.wait_ge(pe_a.sem, pe_a.at(g, f"t{b}.1", back=1))
                sp.dma_start(xp[:, b, :, 0:CIN], xn[:, bass.ds(g * NB + b, 1), :, :].rearrange("p b c f -> p (b c) f")
                             ).then_inc(xp_in[b], 16)

            def gates_and_out(g):
                sp.wait_ge(dve_b.sem, dve_b.at(g, "gT"))
                sp.dma_start(gate_dram[:, :], gT[:, :]).then_inc(gate_out, 16)
                sp.wait_ge(gate_out, (g + 2) * 16)
                sp.wait_ge(dve_c.sem, dve_c.at(g, f"m{EXPERTS - 1}", back=1))
                sp.dma_start(gbc[:, :, :], gate_dram[:, :].rearrange("(o e) t -> o e t", o=1).broadcast_to((128, EXPERTS, TOK))
                             ).then_inc(gate_in, 16)
                sp.wait_ge(act_c.sem, act_c.at(g, "ot"))
                sp.dma_start(out[bass.ds(g * TOK, TOK), :].rearrange("(p t) d -> t p d", t=PAIR), outs[:, :, :]
                             ).then_inc(out_done, 16)

            for c in range(NCHUNK):
                if c:
                    sp.wait_ge(dve_set, IDX_READ + 3 * (c - 1) + 1)
                sp.dma_start(idx_i, idxs[c].broadcast_to((HALF, CHUNK))).then_inc(idx_in, 16)
                if c == 0:
                    sp.dma_start(bvs[:, :], bqkv[:, 2 * D:3 * D].broadcast_to((PAIR, D))).then_inc(attn_w_in, 16)
                    sp.dma_start(wqkv_s[:, :], wqkv).then_inc(attn_w_in, 16)
                    sp.dma_start(wout_s[:, :], wout).then_inc(attn_w_in, 16)
                    for i, w in enumerate((fwq, fwk, fwv, fwo)):
                        sp.dma_start(fw[:, i, :], w).then_inc(ffn_w_in, 16)
                    sp.dma_start(gws[:, :], gw).then_inc(ffn_w_in, 16)
                    sp.dma_start(gbs[:, :], gb.broadcast_to((PAIR, EXPERTS))).then_inc(ffn_w_in, 16)
                sp.wait_ge(act_set, ACT_BIAS + NSUB * (c + 1))
                sp.dma_start(bias_dram[:, c, :], bias_rows).then_inc(bias_out, 16)
                sp.wait_ge(bias_out, 16 * (c + 1))
            rows = bias_dram.rearrange("h c (q k) -> (h c q) k", k=KPOS)
            sp.dma_start(bias[:, 0:TILES - 1, :], rows[0:MT * (TILES - 1), :].rearrange("(t p) k -> p t k", p=MT)
                         ).then_inc(bias_in, 16)
            sp.dma_start(bias[0:tile_rows(TILES - 1), TILES - 1, :], rows[MT * (TILES - 1):ROWS, :]).then_inc(bias_in, 16)
            sp.wait_ge(ones_set, 4)
            for b in range(NB):
                load_x(0, b)
            sp.dma_start(w1s[:, :, :], w1).then_inc(w1_in, 16)
            sp.dma_start(w2s[:, :, :], w2).then_inc(w2_in, 16)
            with sp.Fori(0, GROUPS - 1) as g:
                for b in range(NB):
                    load_x(g + 1, b)
                gates_and_out(g)
            gates_and_out(GROUPS - 1)
            sp.wait_ge(out_done, 16 * (GROUPS + 1))

        @block.gpsimd
        def _(pool):
            start_at_one_group(pool, pool_a, pool_b)
            nc.gpsimd.memset(xa[CIN:CA, :, :], 1.0).then_inc(ones_set, 1)
            pool.wait_ge(ones_set, 1)
            nc.gpsimd.memset(xp[:, :, :, CIN:CA], 1.0).then_inc(ones_set, 1)
            nc.gpsimd.memset(v1[:, :, :, LHD:LHD + 1], 1.0).then_inc(ones_set, 1)
            nc.gpsimd.memset(stat[:, :, :], 1.0).then_inc(ones_set, 1)

            def stage_a(g):
                for b in range(NB):
                    pool.wait_ge(dve_a.sem, dve_a.at(g, f"rec{b}"))
                    pool.sem_inc(pool_waited, 1)
                    for t in range(TILES):
                        m = tile_rows(t)
                        nc.gpsimd.tensor_scalar(prob[0:m, t, :], prob[0:m, t, :], stat[0:m, 2, t:t + 1], None, ALU.mult
                                                ).then_inc(pool_a.tell(f"norm{b}.{t}"), 1)

            def stage_b(g):
                for name, src, dst, dec in (("q", qd, qT, decq), ("k", kd, kT, deck)):
                    pool.wait_ge(dve_b.sem, dve_b.at(g, name))
                    nc.gpsimd.tensor_tensor(dst[:, :].rearrange("p (b t) -> p b t", b=NB),
                                            src[:, :].rearrange("p (b t) -> p b t", b=NB),
                                            wide(dec[:, :], 1, NB), ALU.mult
                                            ).then_inc(pool_b.tell(name), 1)
                for p in range(PAIRS):
                    pool.wait_ge(pool_b.sem, pool_b.at(g, "q"))
                    if p >= 2:
                        pool.wait_ge(pe_b.sem, pe_b.at(g, f"a{p - 2}.1"))
                    nc.gpsimd.tensor_tensor(qm[:, p % 2, :, :],
                                            wide(qT[:, p * PAIR:(p + 1) * PAIR], 1, LHEADS),
                                            wide(hmask, 2, PAIR), ALU.mult
                                            ).then_inc(pool_b.tell(f"qm{p}"), 1)

            with pool.Fori(0, GROUPS) as g:
                stage_a(g)
                stage_b(g)

        @block.scalar
        def _(act):
            start_at_one_group(act, act_a, act_b, act_c)
            act.wait_ge(consts_in, 7 * 16)
            for i, (n, col, w) in enumerate(((KD, P_BNQ, HEADS), (KD, P_BNK, HEADS), (VD, P_BNV, HEADS), (D, P_PROJ, 1))):
                dst = bn[0:n, i, 0:w] if i < 3 else proj_s[:, 0:1]
                nc.scalar.activation(dst, par[0:n, col + 3 * w:col + 4 * w], ACT.Sqrt, bias=eps_col[0:n, :]
                                     ).then_inc(act_set, 1)
            act.preload_act_table_set("natural_log_exp_and_others")
            nc.scalar.activation(nl[:, 0:1], par[:, P_DEC:P_DEC + 1], ACT.Exp, scale=-1.0).then_inc(act_set, 1)
            act.wait_ge(act_set, 5)
            nc.scalar.activation(nl[:, 1:2], nl[:, 0:1], ACT.Ln, bias=one_col).then_inc(act_set, 1)
            act.wait_ge(act_set, 6)
            nc.scalar.mul(nl[:, 2:3], nl[:, 1:2], -1.0).then_inc(act_set, 1)
            act.wait_ge(act_set, 7)
            tcol = cst[:, C_T:C_T + QPOS]
            nc.scalar.activation(deck[:, :], tcol, ACT.Exp, scale=nl[:, 1:2]).then_inc(act_set, 1)
            nc.scalar.activation(decq[:, :], tcol, ACT.Exp, scale=nl[:, 2:3]).then_inc(act_set, 1)
            for h in range(HEADS):
                act.wait_ge(pe_set, h + 1)
                nc.scalar.mul(mqk[:, h, :], ps_t[h % 2][0:CA, 0:CA], KD ** -0.5).then_inc(act_set, 1)
            for h2 in range(HEADS // 2):
                act.wait_ge(pe_set, HEADS + h2 + 1)
                nc.scalar.copy(wvT[:, 2 * h2:2 * h2 + 2, :],
                               ps_s[h2 % 2][0:CA, 0:2 * VD].rearrange("p (h d) -> p h d", h=2)).then_inc(act_set, 1)
            for c in range(NCHUNK):
                for s in range(NSUB):
                    act.wait_ge(pe_set, PE_BIAS + NSUB * c + s + 1)
                    if c and s == 0:
                        act.wait_ge(bias_out, 16 * c)
                    nc.scalar.copy(bias_rows[:, s * SUB:(s + 1) * SUB], ps_t[s % 2][0:HEADS, 0:SUB]).then_inc(act_set, 1)

            def stage_a(g):
                for h in range(0, HEADS, 2):
                    act.wait_ge(pe_a.sem, pe_a.at(g, f"qk{h}"))
                    nc.scalar.copy(qp[:, :, h * QPOS:(h + 1) * QPOS],
                                   ps_t[0][0:CA, 0:TOK].rearrange("p (b q) -> p b q", b=NB)
                                   ).then_inc(act_a.tell(f"qk{h}"), 1)
                for b in range(NB):
                    for t in range(TILES):
                        m = tile_rows(t)
                        act.wait_ge(dve_a.sem, dve_a.at(g, f"neg{b}.{t}"))
                        nc.scalar.activation(prob[0:m, t, :], sneg[0:m, t, :], ACT.Exp, bias=stat[0:m, 0, t:t + 1],
                                             scale=-1.0, accum_out=stat[0:m, 1, t:t + 1]
                                             ).then_inc(act_a.tell(f"exp{b}.{t}"), 1)
                    for j in (0, 2):
                        act.wait_ge(pe_a.sem, pe_a.at(g, f"tr{b}.{j}"))
                        nc.scalar.copy(*pT_evac(j)).then_inc(act_a.tell(f"pt{b}.{j}"), 1)
                    act.wait_ge(pe_a.sem, pe_a.at(g, f"t{b}.0"))
                    nc.scalar.copy(*tT_evac(b, 0)).then_inc(act_a.tell(f"tt{b}.0"), 1)
                for j in range(HEADS // 2):
                    act.wait_ge(pe_a.sem, pe_a.at(g, f"wv{j}"))
                    nc.scalar.activation(relu[:, j % 2, :], ps_t[j % 2][:, 0:TOK], ACT.Relu, bias=three_col
                                         ).then_inc(act_a.tell(f"relu{j}"), 1)

            def stage_b(g):
                tok = ps_b[:, 0:TOK]

                def centred(n):
                    act.wait_ge(pe_b.sem, pe_b.at(g, f"c{n}"))
                    nc.scalar.copy(cT[:, :], tok).then_inc(act_b.tell(f"c{n}"), 1)
                    nc.scalar.activation(sq[:, :], tok, ACT.Square).then_inc(act_b.tell(f"sq{n}"), 1)

                def inverse_root(pe_name, ln, rs, dst, bias_col, scale):
                    act.wait_ge(pe_b.sem, pe_b.at(g, pe_name))
                    nc.scalar.activation(lnb[:, :], tok, ACT.Ln, bias=bias_col, scale=scale).then_inc(act_b.tell(ln), 1)
                    act.wait_ge(act_b.sem, act_b.at(g, ln))
                    nc.scalar.activation(dst[:, :], lnb[:, :], ACT.Exp, scale=-0.5).then_inc(act_b.tell(rs), 1)

                act.wait_ge(pe_b.sem, pe_b.at(g, "proj"))
                nc.scalar.activation(h1T[:, :], tok, ACT.Identity, bias=proj_s[:, 2:3], scale=proj_s[:, 3:4]
                                     ).then_inc(act_b.tell("h1"), 1)
                centred(1)
                inverse_root("v1", "ln1", "rs1", r, eps_col, 1.0)
                for name, e, p, col in (("q", eq, pq, P_BQ), ("k", ek, pk, P_BK)):
                    act.wait_ge(pe_b.sem, pe_b.at(g, name))
                    nc.scalar.activation(e[:, :], tok, ACT.Exp, bias=par[:, col:col + 1]).then_inc(act_b.tell("e" + name), 1)
                    nc.scalar.activation(p[:, :], tok, ACT.Relu, bias=par[:, col:col + 1]).then_inc(act_b.tell("p" + name), 1)
                act.wait_ge(pe_b.sem, pe_b.at(g, "oT"))
                nc.scalar.copy(oT[:, :], tok).then_inc(act_b.tell("oT"), 1)
                act.wait_ge(pe_b.sem, pe_b.at(g, "wout"))
                nc.scalar.activation(a2T[:, :], tok, ACT.Identity, bias=par[:, P_BOUT:P_BOUT + 1]
                                     ).then_inc(act_b.tell("a2"), 1)
                centred(2)
                inverse_root("v2", "ln2", "rs2", r, eps_col, 1.0)
                centred(3)
                inverse_root("v3", "ln3", "rs3", r, eps2_col, 1.0 + EPS)
                for name, dst, rr in (("q", q2T, r), ("k", k2T, r2)):
                    act.wait_ge(pe_b.sem, pe_b.at(g, name + "2"))
                    nc.scalar.copy(dst[:, :], tok).then_inc(act_b.tell(name + "2"), 1)
                    nc.scalar.activation(sq[:, :], tok, ACT.Square).then_inc(act_b.tell(name + "sq"), 1)
                    inverse_root(name + "ss", name + "ln", name + "rs", rr, eps12_col, 1.0)
                act.wait_ge(pe_b.sem, pe_b.at(g, "vx"))
                nc.scalar.copy(v2[:, :, :], ps_b[0:PAIR, :].rearrange("p (n d) -> p n d", n=PAIRS)
                               ).then_inc(act_b.tell("vx"), 1)
                for h in range(FHEADS):
                    act.wait_ge(dve_b.sem, dve_b.at(g, f"sub{h}"))
                    nc.scalar.activation(p2[:, h, :, :], s2[:, h, :, :], ACT.Exp).then_inc(act_b.tell(f"e{h}"), 1)
                for h in range(FHEADS):
                    act.wait_ge(pe_b.sem, pe_b.at(g, f"pT{h}"))
                    nc.scalar.copy(p2T[:, h, :, :], ps_b[0:PAIR, 0:TOK].rearrange("p (n q) -> p n q", n=PAIRS)
                                   ).then_inc(act_b.tell(f"pT{h}"), 1)
                act.wait_ge(pe_b.sem, pe_b.at(g, "av"))
                nc.scalar.copy(o2T[:, :], tok).then_inc(act_b.tell("o2T"), 1)
                act.wait_ge(pe_b.sem, pe_b.at(g, "wo"))
                nc.scalar.copy(yT[:, :], tok).then_inc(act_b.tell("y"), 1)
                act.wait_ge(dve_b.sem, dve_b.at(g, "gsub"))
                nc.scalar.activation(gl[:, 1, :, :], gl[:, 0, :, :], ACT.Exp).then_inc(act_b.tell("gexp"), 1)

            def stage_c(g):
                for e in range(EXPERTS):
                    for j in range(FCH):
                        act.wait_ge(pe_c.sem, pe_c.at(g, f"u{e}.{j}"))
                        col = P_B1 + e * FCH + j
                        nc.scalar.activation(hid[:, j % 2, :], ps_h[:, 0:TOK], ACT.Gelu_apprx_tanh,
                                             bias=par[:, col:col + 1]).then_inc(act_c.tell(f"g{e}.{j}"), 1)
                act.wait_ge(pe_c.sem, pe_c.at(g, "ot"))
                act.wait_ge(out_done, (g + 1) * 16)
                nc.scalar.copy(outs[:, :, :], ps_e[0:PAIR, :].rearrange("p (n d) -> p n d", n=PAIRS)
                               ).then_inc(act_c.tell("ot"), 1)

            with act.Fori(0, GROUPS) as g:
                act.preload_act_table_set("natural_log_exp_and_others")
                stage_a(g)
                stage_b(g)
                stage_c(g)

        @block.vector
        def _(dve):
            start_at_one_group(dve, dve_a, dve_b, dve_c)
            told = [0]

            def then(ins):
                told[0] += 1
                ins.then_inc(dve_set, 1)
                dve.wait_ge(dve_set, told[0])

            dve.wait_ge(consts_in, 7 * 16)
            for i, (n, col, w, wa) in enumerate(((KD, P_BNQ, HEADS, qwa), (KD, P_BNK, HEADS, kwa), (VD, P_BNV, HEADS, vwa),
                                                 (D, P_PROJ, 1, None))):
                dve.wait_ge(act_set, i + 1)
                root = bn[0:n, i, 0:w] if i < 3 else proj_s[:, 0:1]
                scale = bn[0:n, 3, 0:w] if i < 3 else proj_s[:, 1:2]
                prod = bn[0:n, 4, 0:w] if i < 3 else proj_s[:, 0:1]
                shift = bn[0:n, 5, 0:w] if i < 3 else proj_s[:, 2:3]
                gamma, beta, mu = (par[0:n, col + k * w:col + (k + 1) * w] for k in range(3))
                then(nc.vector.reciprocal(root, root))
                then(nc.vector.tensor_tensor(scale, gamma, root, ALU.mult))
                then(nc.vector.tensor_tensor(prod, mu, scale, ALU.mult))
                then(nc.vector.tensor_tensor(shift, beta, prod, ALU.subtract))
                if wa is not None:
                    then(nc.vector.tensor_tensor(wa[:, :, 0:CIN], wa[:, :, 0:CIN],
                                                 wide(scale, 2, CIN), ALU.mult))
                    then(nc.vector.tensor_copy(wa[:, :, CIN:CA], shift.unsqueeze(2)))
                else:
                    then(nc.vector.tensor_scalar(proj_s[:, 3:4], scale, 1.0 / 6.0, None, ALU.mult))
                    then(nc.vector.memset(den[:, :, :], 1.0))
            dve.wait_ge(act_set, 9)
            then(nc.vector.tensor_scalar(decq[:, :], decq[:, :], LHD ** -0.5, None, ALU.mult))
            then(nc.vector.tensor_scalar(fg2[:, 0:1], par[:, P_FG:P_FG + 1], 1.0, None, ALU.mult))
            then(nc.vector.tensor_scalar(fg2[:, 1:2], par[:, P_KN:P_KN + 1], FHD ** 0.5, None, ALU.mult))
            for i in range(3):
                dve.wait_ge(pe_set, HEADS + HEADS // 2 + i + 1)
                then(nc.vector.tensor_copy(pwT[:, 2 * i:2 * i + 2, :],
                                           ps_s[2 if i % 2 == 0 else 1][:, 256:512].rearrange("p (n d) -> p n d", n=2)))
            then(nc.vector.memset(gl[:, 2, :, :], 0.0))
            assert told[0] == IDX_READ
            for c in range(NCHUNK):
                dve.wait_ge(idx_in, 16 * (c + 1))
                then(nc.vector.tensor_copy(idx_f, idx_i))
                if c:
                    dve.wait_ge(pe_set, PE_BIAS + NSUB * c)
                for k in range(2):
                    then(nc.vector.tensor_scalar(onehot[k], idx_f, cst[0:HALF, C_IOTA + k:C_IOTA + k + 1], None,
                                                 ALU.is_equal))
            dve.wait_ge(bias_in, 32)
            dve.wait_ge(ones_set, 4)

            def stage_a(g):
                for h in range(1, HEADS, 2):
                    dve.wait_ge(pe_a.sem, pe_a.at(g, f"qk{h}"))
                    nc.vector.tensor_copy(qp[:, :, h * QPOS:(h + 1) * QPOS],
                                          ps_t[1][0:CA, 0:TOK].rearrange("p (b q) -> p b q", b=NB)
                                          ).then_inc(dve_a.tell(f"qk{h}"), 1)
                for b in range(NB):
                    for t in range(TILES):
                        m = tile_rows(t)
                        if t % 2 == 0:
                            dve.wait_ge(pe_a.sem, pe_a.at(g, f"s{b}.{t // 2}"))
                            dve.sem_inc(dve_waited, 1)
                        nc.vector.tensor_tensor_reduce(
                            out=sneg[0:m, t, :], in0=ps_s[t // 2][0:m, (t % 2) * KPOS:(t % 2 + 1) * KPOS],
                            in1=bias[0:m, t, :], scale=-1.0, scalar=3.0e38, op0=ALU.add, op1=ALU.min,
                            accum_out=stat[0:m, 0, t:t + 1]).then_inc(dve_a.tell(f"neg{b}.{t}"), 1)
                    dve.wait_ge(act_a.sem, act_a.at(g, f"exp{b}.{TILES - 1}"))
                    nc.vector.reciprocal(stat[:, 2, 0:TILES], stat[:, 1, 0:TILES]).then_inc(dve_a.tell(f"rec{b}"), 1)
                    dve.wait_ge(pe_a.sem, pe_a.at(g, f"tr{b}.1"))
                    nc.vector.tensor_copy(*pT_evac(1)).then_inc(dve_a.tell(f"pt{b}.1"), 1)
                    dve.wait_ge(pe_a.sem, pe_a.at(g, f"t{b}.1"))
                    nc.vector.tensor_copy(*tT_evac(b, 1)).then_inc(dve_a.tell(f"tt{b}.1"), 1)
                for j in range(HEADS // 2):
                    dve.wait_ge(act_a.sem, act_a.at(g, f"relu{j}"))
                    nc.vector.scalar_tensor_tensor(out=hs[:, j, :], in0=relu[:, j % 2, :], scalar=6.0,
                                                   in1=ps_t[j % 2][:, 0:TOK], op0=ALU.min, op1=ALU.mult
                                                   ).then_inc(dve_a.tell(f"hs{j}"), 1)

            def stage_b(g):
                tok = ps_b[:, 0:TOK]
                stt = nc.vector.scalar_tensor_tensor
                tt = nc.vector.tensor_tensor

                dve.wait_ge(act_b.sem, act_b.at(g, "rs1"))
                tt(hnT[:, :], cT[:, :], r[:, :], ALU.mult).then_inc(dve_b.tell("hn"), 1)
                for name, e, p, dst in (("q", eq, pq, qd), ("k", ek, pk, kd)):
                    dve.wait_ge(act_b.sem, act_b.at(g, "p" + name))
                    stt(out=dst[:, :], in0=e[:, :], scalar=1.0, in1=p[:, :], op0=ALU.min, op1=ALU.add
                        ).then_inc(dve_b.tell(name), 1)
                dve.wait_ge(pe_b.sem, pe_b.at(g, "v"))
                tt(v1[:, :, :, 0:LHD], ps_b[0:PAIR, :].rearrange("p (n h f) -> p n h f", n=PAIRS, h=LHEADS),
                   wide(bvs[:, :].rearrange("p (h f) -> p h f", h=LHEADS), 1, PAIRS), ALU.add
                   ).then_inc(dve_b.tell("v"), 1)
                for p in range(PAIRS):
                    for i in range(2):
                        dve.wait_ge(pe_b.sem, pe_b.at(g, f"a{p}.{i}"))
                        tt(aT[:, p % 2, 4 * i:4 * i + 4, :], ps_b[0:PAIR, 0:4 * PAIR].rearrange("p (h q) -> p h q", h=4),
                           wide(causal, 1, 4), ALU.mult).then_inc(dve_b.tell(f"a{p}.{i}"), 1)
                    if p % 2:
                        n = p // 2
                        num = ps_b[0:PAIR, 0:16 * (LHD + 1)].rearrange("p (h f) -> p h f", h=16)
                        dve.wait_ge(pe_b.sem, pe_b.at(g, f"num{n}"))
                        nc.vector.tensor_scalar(den[:, 0, :].unsqueeze(2), num[:, :, LHD:LHD + 1], EPS, None, ALU.add
                                                ).then_inc(dve_b.tell(f"den{n}"), 1)
                        dve.wait_ge(dve_b.sem, dve_b.at(g, f"den{n}"))
                        nc.vector.reciprocal(den[:, 1, :], den[:, 0, :]).then_inc(dve_b.tell(f"rden{n}"), 1)
                        dve.wait_ge(dve_b.sem, dve_b.at(g, f"rden{n}"))
                        tt(lo[:, 2 * n:2 * n + 2, :].rearrange("p n (h f) -> p (n h) f", f=LHD), num[:, :, 0:LHD],
                           wide(den[:, 1, :], 2, LHD), ALU.mult).then_inc(dve_b.tell(f"o{n}"), 1)
                dve.wait_ge(act_b.sem, act_b.at(g, "rs2"))
                stt(out=ga[:, :], in0=cT[:, :], scalar=par[:, P_GAMMA:P_GAMMA + 1], in1=r[:, :], op0=ALU.mult,
                    op1=ALU.mult).then_inc(dve_b.tell("ga"), 1)
                dve.wait_ge(dve_b.sem, dve_b.at(g, "ga"))
                stt(out=h2T[:, :], in0=ga[:, :], scalar=par[:, P_BETA:P_BETA + 1], in1=h1T[:, :], op0=ALU.add,
                    op1=ALU.add).then_inc(dve_b.tell("h2"), 1)
                dve.wait_ge(act_b.sem, act_b.at(g, "rs3"))
                stt(out=gx[:, :], in0=cT[:, :], scalar=fg2[:, 0:1], in1=r[:, :], op0=ALU.mult, op1=ALU.mult
                    ).then_inc(dve_b.tell("gx"), 1)
                dve.wait_ge(dve_b.sem, dve_b.at(g, "gx"))
                nc.vector.tensor_scalar(hxT[:, :], gx[:, :], par[:, P_FB:P_FB + 1], None, ALU.add
                                        ).then_inc(dve_b.tell("hx"), 1)
                for name, src, rr, dst, col in (("q", q2T, r, q2n, par[:, P_QN:P_QN + 1]), ("k", k2T, r2, k2n, fg2[:, 1:2])):
                    dve.wait_ge(act_b.sem, act_b.at(g, name + "rs"))
                    stt(out=dst[:, :], in0=src[:, :], scalar=col, in1=rr[:, :], op0=ALU.mult, op1=ALU.mult
                        ).then_inc(dve_b.tell(name + "2n"), 1)
                for h in range(FHEADS):
                    dve.wait_ge(pe_b.sem, pe_b.at(g, f"s{h}"))
                    tt(s2[:, h, :, :], ps_b[0:PAIR, 0:TOK].rearrange("p (n k) -> p n k", n=PAIRS),
                       wide(addmask, 1, PAIRS), ALU.add).then_inc(dve_b.tell(f"sm{h}"), 1)
                    dve.wait_ge(dve_b.sem, dve_b.at(g, f"sm{h}"))
                    nc.vector.tensor_reduce(st2[:, 0, h, :], s2[:, h, :, :], AX.X, ALU.max).then_inc(dve_b.tell(f"mx{h}"), 1)
                    dve.wait_ge(dve_b.sem, dve_b.at(g, f"mx{h}"))
                    tt(s2[:, h, :, :], s2[:, h, :, :], wide(st2[:, 0, h, :], 2, PAIR), ALU.subtract
                       ).then_inc(dve_b.tell(f"sub{h}"), 1)
                for h in range(FHEADS):
                    dve.wait_ge(act_b.sem, act_b.at(g, f"e{h}"))
                    nc.vector.tensor_reduce(st2[:, 1, h, :], p2[:, h, :, :], AX.X, ALU.add).then_inc(dve_b.tell(f"sum{h}"), 1)
                    dve.wait_ge(dve_b.sem, dve_b.at(g, f"sum{h}"))
                    nc.vector.reciprocal(st2[:, 2, h, :], st2[:, 1, h, :]).then_inc(dve_b.tell(f"rc{h}"), 1)
                    dve.wait_ge(dve_b.sem, dve_b.at(g, f"rc{h}"))
                    tt(p2[:, h, :, :], p2[:, h, :, :], wide(st2[:, 2, h, :], 2, PAIR), ALU.mult
                       ).then_inc(dve_b.tell(f"pn{h}"), 1)
                dve.wait_ge(pe_b.sem, pe_b.at(g, "g"))
                tt(gl[:, 0, :, :], ps_b[0:PAIR, 0:PAIRS * EXPERTS].rearrange("p (n e) -> p n e", n=PAIRS),
                   wide(gbs[:, :], 1, PAIRS), ALU.add).then_inc(dve_b.tell("g"), 1)
                dve.wait_ge(dve_b.sem, dve_b.at(g, "g"))
                nc.vector.tensor_reduce(gst[:, 0, :], gl[:, 0, :, :], AX.X, ALU.max).then_inc(dve_b.tell("gmx"), 1)
                dve.wait_ge(dve_b.sem, dve_b.at(g, "gmx"))
                tt(gl[:, 0, :, :], gl[:, 0, :, :], wide(gst[:, 0, :], 2, EXPERTS), ALU.subtract
                   ).then_inc(dve_b.tell("gsub"), 1)
                dve.wait_ge(act_b.sem, act_b.at(g, "gexp"))
                nc.vector.tensor_reduce(gst[:, 1, :], gl[:, 1, :, :], AX.X, ALU.add).then_inc(dve_b.tell("gsum"), 1)
                dve.wait_ge(dve_b.sem, dve_b.at(g, "gsum"))
                nc.vector.reciprocal(gst[:, 2, :], gst[:, 1, :]).then_inc(dve_b.tell("grc"), 1)
                dve.wait_ge(dve_b.sem, dve_b.at(g, "grc"))
                tt(gl[:, 2, :, :], gl[:, 1, :, :], wide(gst[:, 2, :], 2, EXPERTS), ALU.mult
                   ).then_inc(dve_b.tell("gn"), 1)
                dve.wait_ge(pe_b.sem, pe_b.at(g, "gT"))
                dve.wait_ge(gate_out, (g + 1) * 16)
                nc.vector.tensor_copy(gT[:, :], ps_b[0:EXPERTS, 0:TOK]).then_inc(dve_b.tell("gT"), 1)

            def stage_c(g):
                dve.wait_ge(act_b.sem, act_b.at(g, "y"))
                nc.vector.tensor_copy(yc[:, :], yT[:, :]).then_inc(dve_c.tell("yc"), 1)
                nc.vector.tensor_copy(acc[:, :], h2T[:, :]).then_inc(dve_c.tell("acc"), 1)
                dve.wait_ge(gate_in, (g + 1) * 16)
                for e in range(EXPERTS):
                    dve.wait_ge(pe_c.sem, pe_c.at(g, f"d{e}.{FCH - 1}"))
                    dve.wait_ge(dve_c.sem, dve_c.at(g, f"acc{e - 1}" if e else "acc"))
                    nc.vector.scalar_tensor_tensor(out=tmp[:, :], in0=ps_e[:, 0:TOK], scalar=par[:, P_B2 + e:P_B2 + e + 1],
                                                   in1=gbc[:, e, :], op0=ALU.add, op1=ALU.mult
                                                   ).then_inc(dve_c.tell(f"m{e}"), 1)
                    dve.wait_ge(dve_c.sem, dve_c.at(g, f"m{e}"))
                    nc.vector.tensor_tensor(acc[:, :], acc[:, :], tmp[:, :], ALU.add).then_inc(dve_c.tell(f"acc{e}"), 1)

            with dve.Fori(0, GROUPS) as g:
                stage_a(g)
                stage_b(g)
                stage_c(g)

        @block.tensor
        def _(pe):
            start_at_one_group(pe, pe_a, pe_b, pe_c)
            mm = nc.tensor.matmul
            pe.wait_ge(dve_set, 2 * BN_STEPS)
            for h in range(HEADS):
                if h >= 2:
                    pe.wait_ge(act_set, 9 + h - 1)
                mm(ps_t[h % 2][0:CA, 0:CA], qwa[:, h, :], kwa[:, h, :], start=True, stop=True).then_inc(pe_set, 1)
            pe.wait_ge(dve_set, 3 * BN_STEPS)
            for h2 in range(HEADS // 2):
                if h2 >= 2:
                    pe.wait_ge(act_set, 9 + HEADS + h2 - 1)
                for i in range(2):
                    last = nc.tensor.transpose(ps_s[h2 % 2][0:CA, i * VD:(i + 1) * VD], vwa[:, 2 * h2 + i, :],
                                               ident[0:VD, 0:VD])
                last.then_inc(pe_set, 1)
            pe.wait_ge(act_set, 9 + HEADS + HEADS // 2)
            for i in range(3):
                if i == 2:
                    pe.wait_ge(dve_set, IDX_READ - 3)
                for k in range(2):
                    last = nc.tensor.transpose(ps_s[2 if i % 2 == 0 else 1][:, 256 + 128 * k:384 + 128 * k],
                                               pws[:, (2 * i + k) * 128:(2 * i + k + 1) * 128], ident)
                last.then_inc(pe_set, 1)
            for c in range(NCHUNK):
                pe.wait_ge(dve_set, IDX_READ + 3 * (c + 1))
                for s in range(NSUB):
                    if s >= 2 or c:
                        pe.wait_ge(act_set, ACT_BIAS + NSUB * c + s - 1)
                    for k in range(2):
                        last = mm(ps_t[s % 2][0:HEADS, 0:SUB], abt[:, k, :], onehot[k][:, s * SUB:(s + 1) * SUB],
                                  start=(k == 0), stop=(k == 1))
                    last.then_inc(pe_set, 1)
            pe.wait_ge(act_set, ACT_BIAS + NSUB * NCHUNK)
            pe.wait_ge(ones_set, 4)

            def stage_a(g):
                for b in range(NB):
                    pe.wait_ge(xa_in[b], (g + 1) * 16)
                for h in range(HEADS):
                    if h >= 2:
                        s = (act_a, dve_a)[h % 2]
                        pe.wait_ge(s.sem, s.at(g, f"qk{h - 2}"))
                    elif h == 0:
                        pe.wait_ge(dve_a.sem, dve_a.at(g, f"hs{HEADS // 2 - 1}", back=1))
                    xs = xa[:, :, :].rearrange("p b (i u j v) -> p b i u j v", i=OUT_RES, u=2, v=2)[:, :, :, 0, :, 0]
                    mm(ps_t[h % 2][0:CA, 0:TOK], mqk[:, h, :], xs, start=True, stop=True
                       ).then_inc(pe_a.tell(f"qk{h}"), 1)
                pe.wait_ge(act_a.sem, act_a.at(g, f"qk{HEADS - 2}"))
                pe.wait_ge(dve_a.sem, dve_a.at(g, f"qk{HEADS - 1}"))
                for b in range(NB):
                    for j in range(3):
                        s = (act_a, dve_a, act_a)[j]
                        pe.wait_ge(s.sem, s.at(g, f"pt{b - 1}.{j}") if b else s.at(g, f"pt{NB - 1}.{j}", back=1))
                        for t in range(2 * j, min(2 * j + 2, TILES)):
                            m = tile_rows(t)
                            last = mm(ps_s[j][0:m, (t % 2) * KPOS:(t % 2 + 1) * KPOS], qp[:, b, MT * t:MT * t + m],
                                      xa[:, b, :], start=True, stop=True)
                        last.then_inc(pe_a.tell(f"s{b}.{j}"), 1)
                    for j in range(3):
                        for t in range(2 * j, min(2 * j + 2, TILES)):
                            m = tile_rows(t)
                            pe.wait_ge(pool_a.sem, pool_a.at(g, f"norm{b}.{t}"))
                            for c in range(2):
                                col = (t % 2) * 2 * MT + c * MT
                                last = nc.tensor.transpose(ps_s[j][0:HALF, col:col + m],
                                                           prob[0:m, t, c * HALF:(c + 1) * HALF], ident[0:m, 0:m])
                        last.then_inc(pe_a.tell(f"tr{b}.{j}"), 1)
                    pe.wait_ge(xp_in[b], (g + 1) * 16)
                    pe.wait_ge(act_a.sem, act_a.at(g, f"pt{b}.2"))
                    pe.wait_ge(dve_a.sem, dve_a.at(g, f"pt{b}.1"))
                    for n in range(2):
                        s = (act_a, dve_a)[n]
                        if b:
                            pe.wait_ge(s.sem, s.at(g, f"tt{b - 1}.{n}"))
                        for c in range(2):
                            last = mm(ps_t[n][0:CA, 0:6 * QPOS], xp[:, b, c, :],
                                      pT[:, c, 6 * QPOS * n:6 * QPOS * (n + 1)], start=(c == 0), stop=(c == 1))
                        last.then_inc(pe_a.tell(f"t{b}.{n}"), 1)
                pe.wait_ge(act_a.sem, act_a.at(g, f"tt{NB - 1}.0"))
                pe.wait_ge(dve_a.sem, dve_a.at(g, f"tt{NB - 1}.1"))
                for j in range(HEADS // 2):
                    if j >= 2:
                        pe.wait_ge(dve_a.sem, dve_a.at(g, f"hs{j - 2}"))
                    for i in range(2):
                        last = mm(ps_t[j % 2][VD * i:VD * (i + 1), 0:TOK], wvT[:, 2 * j + i, :], tT[:, 2 * j + i, :],
                                  start=True, stop=True)
                    last.then_inc(pe_a.tell(f"wv{j}"), 1)

            def stage_b(g):
                tok = ps_b[:, 0:TOK]

                def product(name, w, x):
                    mm(tok, w, x, start=True, stop=True).then_inc(pe_b.tell(name), 1)

                def token_rows(name, x, w, n):
                    for p in range(PAIRS):
                        last = mm(ps_b[0:PAIR, n * p:n * (p + 1)], x[:, p * PAIR:(p + 1) * PAIR], w, start=True, stop=True)
                    last.then_inc(pe_b.tell(name), 1)

                pe.wait_ge(dve_b.sem, dve_b.at(g, "gT", back=1))
                pe.wait_ge(dve_a.sem, dve_a.at(g, f"hs{HEADS // 2 - 1}"))
                for j in range(HEADS // 2):
                    last = mm(tok, pwT[:, j, :], hs[:, j, :], start=(j == 0), stop=(j == HEADS // 2 - 1))
                last.then_inc(pe_b.tell("proj"), 1)
                pe.wait_ge(act_b.sem, act_b.at(g, "h1"))
                product("c1", center, h1T[:, :])
                pe.wait_ge(act_b.sem, act_b.at(g, "sq1"))
                product("v1", mean, sq[:, :])
                pe.wait_ge(dve_b.sem, dve_b.at(g, "hn"))
                product("q", wqkv_s[:, 0:D], hnT[:, :])
                pe.wait_ge(act_b.sem, act_b.at(g, "pq"))
                product("k", wqkv_s[:, D:2 * D], hnT[:, :])
                pe.wait_ge(act_b.sem, act_b.at(g, "pk"))
                token_rows("v", hnT, wqkv_s[:, 2 * D:3 * D], D)
                pe.wait_ge(dve_b.sem, dve_b.at(g, "v"))
                pe.wait_ge(pool_b.sem, pool_b.at(g, "k"))
                for p in range(PAIRS):
                    pe.wait_ge(pool_b.sem, pool_b.at(g, f"qm{p}"))
                    for i in range(2):
                        if i:
                            pe.wait_ge(dve_b.sem, dve_b.at(g, f"a{p}.0"))
                        elif p == 2:
                            pe.wait_ge(dve_b.sem, dve_b.at(g, "o0"))
                        elif p:
                            pe.wait_ge(dve_b.sem, dve_b.at(g, f"a{p - 1}.1"))
                        mm(ps_b[0:PAIR, 0:4 * PAIR], kT[:, p * PAIR:(p + 1) * PAIR], qm[:, p % 2, 4 * i:4 * i + 4, :],
                           start=True, stop=True).then_inc(pe_b.tell(f"a{p}.{i}"), 1)
                    if p % 2:
                        pe.wait_ge(dve_b.sem, dve_b.at(g, f"a{p}.1"))
                        for k in range(2):
                            for h in range(LHEADS):
                                col = (k * LHEADS + h) * (LHD + 1)
                                last = mm(ps_b[0:PAIR, col:col + LHD + 1], aT[:, k, h, :], v1[:, p - 1 + k, h, :],
                                          start=True, stop=True)
                        last.then_inc(pe_b.tell(f"num{p // 2}"), 1)
                pe.wait_ge(dve_b.sem, dve_b.at(g, "o1"))
                for p in range(PAIRS):
                    last = nc.tensor.transpose(ps_b[:, p * PAIR:(p + 1) * PAIR], lo[:, p, :], ident[0:PAIR, 0:PAIR])
                last.then_inc(pe_b.tell("oT"), 1)
                pe.wait_ge(act_b.sem, act_b.at(g, "oT"))
                product("wout", wout_s[:, :], oT[:, :])
                pe.wait_ge(act_b.sem, act_b.at(g, "a2"))
                product("c2", center, a2T[:, :])
                pe.wait_ge(act_b.sem, act_b.at(g, "sq2"))
                product("v2", mean, sq[:, :])
                pe.wait_ge(dve_b.sem, dve_b.at(g, "h2"))
                product("c3", center, h2T[:, :])
                pe.wait_ge(act_b.sem, act_b.at(g, "sq3"))
                product("v3", mean, sq[:, :])
                pe.wait_ge(dve_b.sem, dve_b.at(g, "hx"))
                product("q2", fw[:, 0, :], hxT[:, :])
                pe.wait_ge(act_b.sem, act_b.at(g, "qsq"))
                product("qss", headsum, sq[:, :])
                pe.wait_ge(act_b.sem, act_b.at(g, "qln"))
                product("k2", fw[:, 1, :], hxT[:, :])
                pe.wait_ge(act_b.sem, act_b.at(g, "ksq"))
                product("kss", headsum, sq[:, :])
                pe.wait_ge(act_b.sem, act_b.at(g, "kln"))
                token_rows("vx", hxT, fw[:, 2, :], D)
                pe.wait_ge(act_b.sem, act_b.at(g, "vx"))
                pe.wait_ge(dve_b.sem, dve_b.at(g, "k2n"))
                for h in range(FHEADS):
                    if h:
                        pe.wait_ge(dve_b.sem, dve_b.at(g, "sm0"))
                    f = slice(FHD * h, FHD * (h + 1))
                    for p in range(PAIRS):
                        t = slice(p * PAIR, (p + 1) * PAIR)
                        last = mm(ps_b[0:PAIR, t], q2n[f, t], k2n[f, t], start=True, stop=True)
                    last.then_inc(pe_b.tell(f"s{h}"), 1)
                for h in range(FHEADS):
                    if h:
                        pe.wait_ge(act_b.sem, act_b.at(g, "pT0"))
                    pe.wait_ge(dve_b.sem, dve_b.at(g, f"pn{h}"))
                    for p in range(PAIRS):
                        last = nc.tensor.transpose(ps_b[0:PAIR, p * PAIR:(p + 1) * PAIR], p2[:, h, p, :],
                                                   ident[0:PAIR, 0:PAIR])
                    last.then_inc(pe_b.tell(f"pT{h}"), 1)
                pe.wait_ge(act_b.sem, act_b.at(g, "pT1"))
                for h in range(FHEADS):
                    for p in range(PAIRS):
                        last = mm(ps_b[FHD * h:FHD * (h + 1), p * PAIR:(p + 1) * PAIR], v2[:, p, FHD * h:FHD * (h + 1)],
                                  p2T[:, h, p, :], start=True, stop=True)
                last.then_inc(pe_b.tell("av"), 1)
                pe.wait_ge(act_b.sem, act_b.at(g, "o2T"))
                product("wo", fw[:, 3, :], o2T[:, :])
                pe.wait_ge(act_b.sem, act_b.at(g, "y"))
                token_rows("g", yT, gws[:, :], EXPERTS)
                pe.wait_ge(dve_b.sem, dve_b.at(g, "gn"))
                for p in range(PAIRS):
                    last = nc.tensor.transpose(ps_b[0:EXPERTS, p * PAIR:(p + 1) * PAIR], gl[:, 2, p, :],
                                               ident[0:PAIR, 0:PAIR])
                last.then_inc(pe_b.tell("gT"), 1)

            def stage_c(g):
                def up(e, j):
                    if e or j:
                        pe.wait_ge(act_c.sem, act_c.at(g, f"g{e}.{j - 1}" if j else f"g{e - 1}.{FCH - 1}"))
                    mm(ps_h[:, 0:TOK], w1s[:, e, 128 * j:128 * (j + 1)], yc[:, :], start=True, stop=True
                       ).then_inc(pe_c.tell(f"u{e}.{j}"), 1)

                def down(e, j):
                    pe.wait_ge(act_c.sem, act_c.at(g, f"g{e}.{j}"))
                    if j == 0:
                        if e:
                            pe.wait_ge(dve_c.sem, dve_c.at(g, f"m{e - 1}"))
                        else:
                            pe.wait_ge(act_c.sem, act_c.at(g, "ot", back=1))
                    mm(ps_e[:, 0:TOK], w2s[:, e * FCH + j, :], hid[:, j % 2, :], start=(j == 0), stop=(j == FCH - 1)
                       ).then_inc(pe_c.tell(f"d{e}.{j}"), 1)

                pe.wait_ge(dve_c.sem, dve_c.at(g, "yc"))
                before = None
                for e in range(EXPERTS):
                    for j in range(FCH):
                        up(e, j)
                        if before:
                            down(*before)
                        before = (e, j)
                down(*before)
                pe.wait_ge(dve_c.sem, dve_c.at(g, f"acc{EXPERTS - 1}"))
                for p in range(PAIRS):
                    last = nc.tensor.transpose(ps_e[0:PAIR, p * D:(p + 1) * D], acc[:, p * PAIR:(p + 1) * PAIR], ident)
                last.then_inc(pe_c.tell("ot"), 1)

            pe.wait_ge(attn_w_in, 3 * 16)
            pe.wait_ge(ffn_w_in, 6 * 16)
            pe.wait_ge(w1_in, 16)
            pe.wait_ge(w2_in, 16)
            with pe.Fori(0, GROUPS) as g:
                stage_a(g)
                stage_b(g)
                stage_c(g)


def shape_constants():
    c = np.zeros((128, NCONST), np.float32)
    i = np.arange(128)
    c[:, C_ID:C_ID + 128] = np.eye(128)
    c[:, C_CENTER:C_CENTER + 128] = np.eye(128) - 1.0 / D
    c[:, C_MEAN:C_MEAN + 128] = 1.0 / D
    c[:, C_HEADSUM:C_HEADSUM + 128] = i[:, None] // FHD == i[None, :] // FHD
    t = np.arange(PAIR)
    same = t[:, None] // QPOS == t[None, :] // QPOS
    c[:PAIR, C_CAUSAL:C_CAUSAL + PAIR] = same & (t[:, None] <= t[None, :])
    c[:PAIR, C_ADDMASK:C_ADDMASK + PAIR] = np.where(same & (t[None, :] <= t[:, None]), 0.0, NEG)
    c[:, C_HMASK:C_HMASK + LHEADS] = i[:, None] // LHD == np.arange(LHEADS)[None, :]
    c[:, C_T:C_T + QPOS] = np.arange(QPOS)
    c[:, C_IOTA] = i
    c[:, C_IOTA + 1] = i + HALF
    c[:, C_EPS:C_EPS + 5] = (EPS, EPS * EPS, 1e-12, 1.0, 3.0)
    return c


def kernel(**inputs):
    import concourse.bacc as _bacc
    from concourse.bass_utils import run_bass_kernel_spmd as _run

    a = {k.replace("L0_", ""): np.asarray(v) for k, v in inputs.items()}
    assert a["tok_attention_biases"].shape[1] == NOFF == 2 * HALF
    x = a["x"]
    kv = a["tok_kv_w"].reshape(HEADS, KD + VD, CIN)

    par = np.zeros((128, NPAR), np.float32)
    for k, s in enumerate("gbmv"):
        par[:, P_PROJ + k] = a["tok_proj_" + s]
        par[:KD, P_BNQ + HEADS * k:P_BNQ + HEADS * (k + 1)] = a["tok_q_" + s].reshape(HEADS, KD).T
        kvp = a["tok_kv_" + s].reshape(HEADS, KD + VD)
        par[:KD, P_BNK + HEADS * k:P_BNK + HEADS * (k + 1)] = kvp[:, :KD].T
        par[:VD, P_BNV + HEADS * k:P_BNV + HEADS * (k + 1)] = kvp[:, KD:].T
    par[:, P_BQ] = a["attn_bqkv"][0:D]
    par[:, P_BK] = a["attn_bqkv"][D:2 * D]
    for col, name in ((P_BOUT, "attn_bout"), (P_GAMMA, "attn_ln_gamma"), (P_BETA, "attn_ln_beta"), (P_FG, "ffn_ln_g"),
                      (P_FB, "ffn_ln_b")):
        par[:, col] = a[name]
    par[:, P_QN] = np.tile(a["ffn_qn_g"], FHEADS)
    par[:, P_KN] = np.tile(a["ffn_kn_g"], FHEADS)
    par[:, P_DEC] = np.repeat(a["attn_decay_logits"], LHD)
    par[:, P_B1:P_B1 + EXPERTS * FCH] = a["ffn_b1"].reshape(EXPERTS * FCH, 128).T
    par[:, P_B2:P_B2 + EXPERTS] = a["ffn_b2"].T

    arrays = {
        "xT": x.transpose(2, 0, 1).reshape(CIN, BATCH * KPOS),
        "xn": x.reshape(BATCH, 2, HALF, CIN).transpose(2, 0, 1, 3),
        "consts": shape_constants(),
        "params": par,
        "qw": a["tok_q_w"].reshape(HEADS, KD, CIN).transpose(1, 0, 2),
        "kw": kv[:, :KD].transpose(1, 0, 2),
        "vw": kv[:, KD:].transpose(1, 0, 2),
        "pw": a["tok_proj_w"],
        "ab": a["tok_attention_biases"].T.reshape(2, HALF, HEADS).transpose(1, 0, 2),
        "idxs": a["tok_bias_idxs"].reshape(7, 1, QPOS * KPOS // 7),
        "wqkv": a["attn_Wqkv"],
        "bqkv": a["attn_bqkv"].reshape(1, 3 * D),
        "wout": a["attn_Wout"],
        "fwq": a["ffn_Wq"], "fwk": a["ffn_Wk"], "fwv": a["ffn_Wv"], "fwo": a["ffn_Wo"],
        "gw": a["ffn_gate_W"],
        "gb": a["ffn_gate_b"].reshape(1, EXPERTS),
        "w1": a["ffn_W1"].transpose(1, 0, 2),
        "w2": a["ffn_W2"].reshape(EXPERTS * FCH, 128, D).transpose(1, 0, 2),
    }
    nc = _bacc.Bacc("TRN2", target_bir_lowering=False, num_devices=1)
    given, args = {}, []
    for name, v in arrays.items():
        v = np.ascontiguousarray(v)
        given[f"in_{name}"] = v
        args.append(nc.dram_tensor(f"in_{name}", v.shape, mybir.dt.from_np(v.dtype), kind="ExternalInput").ap())
    bias_dram = nc.dram_tensor("bias_rows_dram", (HEADS, 7, QPOS * KPOS // 7), F32, kind="Internal").ap()
    gate_dram = nc.dram_tensor("gate_rows_dram", (EXPERTS, TOK), F32, kind="Internal").ap()
    out = nc.dram_tensor("out_dram", (BATCH * QPOS, D), F32, kind="ExternalOutput").ap()
    audio_tower_kernel(nc, *args, bias_dram, gate_dram, out)
    r = _run(nc, [given], core_ids=[0])
    return r.results[0]["out_dram"].reshape(BATCH, QPOS, D)
```

```python
from contextlib import ExitStack

import concourse.bass as bass
import numpy as np
from concourse import mybir

F32 = mybir.dt.float32
I32 = mybir.dt.int32
ALU = mybir.AluOpType
ACT = mybir.ActivationFunctionType
AX = mybir.AxisListType

BATCH, RES, OUT_RES, CIN = 64, 14, 7, 96
KPOS, QPOS = RES * RES, OUT_RES * OUT_RES
HEADS, KD, VD = 12, 32, 64
D = 128
LHEADS, LHD = 8, 16
FHEADS, FHD = 2, 64
EXPERTS, FF = 8, 512
NOFF = 196
EPS = 1e-5

NB = 8
GROUPS = BATCH // NB
TOK = NB * QPOS
CA = CIN + 1
HALF = KPOS // 2
ROWS = HEADS * QPOS
TILES = 5
MT = 118
PAIR = 2 * QPOS
PAIRS = NB // 2
FCH = FF // 128
NEG = -3.0e38


def tile_rows(t):
    return min(MT, ROWS - MT * t)


C_ID, C_CENTER, C_MEAN, C_HEADSUM, C_CAUSAL, C_ADDMASK, C_HMASK, C_T, C_IOTA = (
    0, 128, 256, 384, 512, 610, 708, 716, 765)
C_EPS = 767
NCONST = 772

P_PROJ, P_BQ, P_BK, P_BOUT, P_GAMMA, P_BETA, P_FG, P_FB, P_QN, P_KN, P_DEC, P_B1, P_B2, P_BNQ, P_BNK, P_BNV = (
    0, 4, 5, 6, 7, 8, 9, 10, 11, 12, 13, 14, 46, 54, 102, 150)
NPAR = 198


class Steps:

    def __init__(self, sem, names):
        self.sem, self.names = sem, names
        self.index = {n: i for i, n in enumerate(names)}
        self.per_group = len(names)
        self.told = 0

    def at(self, g, name, back=0):
        return (g + 1 - back) * self.per_group + self.index[name] + 1

    def tell(self, name):
        assert self.names[self.told % self.per_group] == name, (name, self.names[self.told % self.per_group])
        self.told += 1
        return self.sem


def wide(ap, axis, n):
    shape = list(ap.shape)
    return ap.unsqueeze(axis).broadcast_to(tuple(shape[:axis] + [n] + shape[axis:]))


def steps_a():
    pe = [f"qk{h}" for h in range(HEADS)]
    act = [f"qk{h}" for h in range(0, HEADS, 2)]
    dve = [f"qk{h}" for h in range(1, HEADS, 2)]
    pool = []
    for b in range(-1, NB):
        if b >= 0:
            pe += [f"tr{b}.{j}" for j in range(3)]
            act += [f"pt{b}.0", f"pt{b}.2"]
            dve += [f"rec{b}", f"pt{b}.1"]
            pool += [f"norm{b}.{t}" for t in range(TILES)]
        if b + 1 < NB:
            pe += [f"s{b + 1}.{j}" for j in range(3)]
            act += [f"exp{b + 1}.{t}" for t in range(TILES)]
            dve += [f"neg{b + 1}.{t}" for t in range(TILES)]
        if b >= 0:
            pe += [f"t{b}.{n}" for n in range(2)]
            act += [f"tt{b}.0"]
            dve += [f"tt{b}.1"]
    pe += [f"wv{j}" for j in range(HEADS // 2)]
    act += [f"relu{j}" for j in range(HEADS // 2)]
    dve += [f"hs{j}" for j in range(HEADS // 2)]
    return pe, act, dve, pool


def steps_b():
    pe = ["proj", "c1", "v1", "q", "k", "v"]
    act = ["h1", "c1", "sq1", "ln1", "rs1", "eq", "pq", "ek", "pk"]
    dve = ["hn", "q", "k", "v"]
    pool = ["q", "k"]
    for p in range(PAIRS):
        pool += [f"qm{p}"]
        pe += [f"a{p}.0", f"a{p}.1"]
        dve += [f"a{p}.0", f"a{p}.1"]
        if p % 2:
            pe += [f"num{p // 2}"]
            dve += [f"den{p // 2}", f"rden{p // 2}", f"o{p // 2}"]
    pe += ["oT", "wout", "c2", "v2", "c3", "v3", "q2", "qss", "k2", "kss", "vx", "s0", "s1", "pT0", "pT1", "av", "wo",
           "g", "gT"]
    act += ["oT", "a2", "c2", "sq2", "ln2", "rs2", "c3", "sq3", "ln3", "rs3", "q2", "qsq", "qln", "qrs",
            "k2", "ksq", "kln", "krs", "vx", "e0", "e1", "pT0", "pT1", "o2T", "y", "gexp"]
    dve += ["ga", "h2", "gx", "hx", "q2n", "k2n", "sm0", "mx0", "sub0", "sm1", "mx1", "sub1",
            "sum0", "rc0", "pn0", "sum1", "rc1", "pn1", "g", "gmx", "gsub", "gsum", "grc", "gn", "gT"]
    return pe, act, dve, pool


def steps_c():
    ej = [(e, j) for e in range(EXPERTS) for j in range(FCH)]
    pe = []
    for n, (e, j) in enumerate(ej):
        pe += [f"u{e}.{j}"]
        if n:
            pe += ["d%d.%d" % ej[n - 1]]
    pe += ["d%d.%d" % ej[-1], "ot"]
    act = [f"g{e}.{j}" for e, j in ej] + ["ot"]
    dve = ["yc", "acc"]
    for e in range(EXPERTS):
        dve += [f"m{e}", f"acc{e}"]
    return pe, act, dve


B_UNITS = steps_b()[0]
B_CURVED = {"v1", "q", "k", "v2", "v3", "qss", "kss", "s0", "s1", "g"}
UNITS_A = HEADS // 2 + 1 + 5 * NB - 1 + HEADS // 2


def schedule():
    plan = ["c", "b*", "a", "a", "c", "b*", "a", "c", "b*", "a", "c", "x", "b", "a", "a", "b", "a", "b"]
    for b in range(NB):
        with_c = b + 1 < EXPERTS
        if with_c:
            plan += ["c", "b*", "c", "b*"]
        plan += ["a"]
        if with_c:
            plan += ["c", "b*", "c"]
        plan += ["b*", "a"] + (["x"] if with_c else []) + ["b"]
        if b + 1 < NB:
            plan += ["a", "b"]
        plan += ["a", "b", "a", "b"]
    plan += ["c"] + ["a", "b"] * (HEADS // 2) + ["c"]
    points = sum(u[0] == "b" for u in plan)
    seen = done = 0
    order = []
    for u in plan:
        if u[0] != "b":
            order.append(u)
            continue
        seen += 1
        if done < len(B_UNITS) and done * points <= seen * len(B_UNITS) and not (
                u == "b*" and B_UNITS[done] in B_CURVED):
            order.append("b")
            done += 1
    order += ["b"] * (len(B_UNITS) - done)
    assert order.count("a") == UNITS_A and order.count("c") == EXPERTS * FCH + 2
    return order


def nothing(units):
    for _ in range(units):
        yield


def take_units(stages, on_x=None):
    for u in schedule():
        if u == "x":
            if on_x is not None and stages["c"] is not None:
                on_x()
        elif stages[u] is not None:
            next(stages[u])
    for stage in stages.values():
        assert stage is None or next(stage, "ended") == "ended"


def audio_tower_kernel(nc, xT, xn, consts, params, qw, kw, vw, pw, ab, idxs, wqkv, bqkv, wout, fwq, fwk, fwv, fwo,
                       gw, gb, w1, w2, bias_dram, gate_dram, out):
    with ExitStack() as ctx:
        def sb(name, shape, dt=F32):
            return ctx.enter_context(nc.sbuf_tensor(name, shape, dt))

        def sem(name):
            return ctx.enter_context(nc.semaphore(name))

        cst = sb("cst", [128, NCONST])
        par = sb("par", [128, NPAR])
        ident = cst[:, C_ID:C_ID + 128]
        center = cst[:, C_CENTER:C_CENTER + 128]
        mean = cst[:, C_MEAN:C_MEAN + 128]
        headsum = cst[:, C_HEADSUM:C_HEADSUM + 128]
        causal = cst[0:PAIR, C_CAUSAL:C_CAUSAL + PAIR]
        addmask = cst[0:PAIR, C_ADDMASK:C_ADDMASK + PAIR]
        hmask = cst[:, C_HMASK:C_HMASK + LHEADS]
        eps_col = cst[:, C_EPS:C_EPS + 1]
        eps2_col = cst[:, C_EPS + 1:C_EPS + 2]
        eps12_col = cst[:, C_EPS + 2:C_EPS + 3]
        one_col = cst[:, C_EPS + 3:C_EPS + 4]
        three_col = cst[:, C_EPS + 4:C_EPS + 5]
        abt = sb("abt", [HALF, 2, HEADS])
        wqkv_s = sb("wqkv_s", [D, 3 * D])
        wout_s = sb("wout_s", [D, D])
        fw = sb("fw", [D, 4, D])
        gws = sb("gws", [D, EXPERTS])
        gbs = sb("gbs", [PAIR, EXPERTS])
        bvs = sb("bvs", [PAIR, D])
        w1s = sb("w1s", [D, EXPERTS, FF])
        w2s = sb("w2s", [D, EXPERTS * FCH, D])
        mqk = sb("mqk", [CA, HEADS, CA])
        wvT = sb("wvT", [CA, HEADS, VD])
        pwT = sb("pwT", [D, HEADS // 2, D])
        bias = sb("bias", [MT, TILES, KPOS])
        bn = sb("bn", [128, 6, HEADS])
        proj_s = sb("proj_s", [128, 4])
        decq = sb("decq", [128, QPOS])
        deck = sb("deck", [128, QPOS])
        nl = sb("nl", [128, 3])
        fg2 = sb("fg2", [128, 2])

        xa = sb("xa", [CA, NB, KPOS])
        xp = sb("xp", [HALF, NB, 2, CA])
        qp_all = sb("qp", [128, NB, ROWS])
        qp = qp_all[0:CA, :, :]
        sneg = sb("sneg", [MT, TILES, KPOS])
        prob = sb("prob", [MT, TILES, KPOS])
        stat = sb("stat", [MT, 3, 8])
        pT = sb("pT", [HALF, 2, ROWS])
        tT_all = sb("tT", [128, HEADS, TOK])
        tT = tT_all[0:CA, :, :]
        relu = sb("relu", [128, 2, TOK])
        hs = sb("hs", [128, HEADS // 2, TOK])

        def feat(name):
            return sb(name, [128, TOK])
        h1T, cT, sq, lnb, r, hnT = feat("h1T"), feat("cT"), feat("sq"), feat("lnb"), feat("r"), feat("hnT")
        eq, pq, ek, pk, qd, kd, qT, kT = (feat(n) for n in ("eq", "pq", "ek", "pk", "qd", "kd", "qT", "kT"))
        ga, gx, q2T, k2T, q2n, k2n = eq, pq, ek, pk, qd, kd
        v1 = sb("v1", [PAIR, PAIRS, LHEADS, LHD + 1])
        qm = sb("qm", [128, 2, LHEADS, PAIR])
        aT = sb("aT", [PAIR, 2, LHEADS, PAIR])
        den = sb("den", [PAIR, 2, 16])
        lo = sb("lo", [PAIR, PAIRS, D])
        oT, a2T, h2T, hxT, r2 = (feat(n) for n in ("oT", "a2T", "h2T", "hxT", "r2"))
        v2 = sb("v2", [PAIR, PAIRS, D])
        s2, p2 = (aT[:, i, :, :].rearrange("p (h n) q -> p h n q", h=FHEADS) for i in range(2))
        st2 = sb("st2", [PAIR, 3, FHEADS, PAIRS])
        p2T = qm[0:PAIR, 0, :, :].rearrange("p (h n) q -> p h n q", h=FHEADS)
        o2T, yT = feat("o2T"), feat("yT")
        gl = sb("gl", [PAIR, 3, PAIRS, EXPERTS])
        gst = sb("gst", [PAIR, 3, PAIRS])
        gT = sb("gT", [EXPERTS, TOK])

        yc, acc = feat("yc"), feat("acc")
        gbc = sb("gbc", [128, EXPERTS, TOK])
        hid = sb("hid", [128, 2, TOK])
        tmp = feat("tmp")
        outs = sb("outs", [PAIR, PAIRS, D])

        early = hs[0:KD, :, :].rearrange("p a b -> p (a b)")
        qwa, kwa = (early[:, i * HEADS * CA:(i + 1) * HEADS * CA].rearrange("p (h c) -> p h c", h=HEADS) for i in range(2))
        late = gbc[:, :, :].rearrange("p a b -> p (a b)")
        vwa = late[0:VD, 0:HEADS * CA].rearrange("p (h c) -> p h c", h=HEADS)
        pws = late[:, HEADS * CA:HEADS * CA + HEADS * VD]
        idx_i = tT_all[0:HALF, 0:4, :].rearrange("p a b -> p (a b)")[:, 0:1372].bitcast(I32)
        idx_f = tT_all[0:HALF, 4:8, :].rearrange("p a b -> p (a b)")[:, 0:1372]
        onehot = [qp_all[0:HALF, 3 * c:3 * c + 3, :].rearrange("p a b -> p (a b)")[:, 0:1372] for c in range(2)]
        bias_rows = tT_all[0:HEADS, 8:12, :].rearrange("p a b -> p (a b)")[:, 0:1372]

        def bank(name):
            return ctx.enter_context(nc.psum_tensor(name, [128, 512], F32))
        ps_s = [bank(f"ps_s{j}") for j in range(3)]
        ps_t = [bank(f"ps_t{n}") for n in range(2)]
        ps_b, ps_h, ps_e = bank("ps_b"), bank("ps_h"), bank("ps_e")

        pe_a, act_a, dve_a, pool_a = (Steps(sem(n), s) for n, s in zip(("pe_a", "act_a", "dve_a", "pool_a"), steps_a()))
        pe_b, act_b, dve_b, pool_b = (Steps(sem(n), s) for n, s in zip(("pe_b", "act_b", "dve_b", "pool_b"), steps_b()))
        pe_c, act_c, dve_c = (Steps(sem(n), s) for n, s in zip(("pe_c", "act_c", "dve_c"), steps_c()))

        def start_at_one_group(eng, *stages):
            for s in stages:
                eng.sem_inc(s.sem, s.per_group)

        dve_waited, pool_waited = sem("dve_waited"), sem("pool_waited")
        xa_in = [sem(f"xa_in{b}") for b in range(NB)]
        xp_in = [sem(f"xp_in{b}") for b in range(NB)]
        gate_out, gate_in, out_done = sem("gate_out"), sem("gate_in"), sem("out_done")
        consts_in, attn_w_in, ffn_w_in, w1_in, w2_in = (
            sem(n) for n in ("consts_in", "attn_w_in", "ffn_w_in", "w1_in", "w2_in"))
        idx_in, bias_out, bias_in = sem("idx_in"), sem("bias_out"), sem("bias_in")
        dve_set, act_set, pe_set, ones_set = sem("dve_set"), sem("act_set"), sem("pe_set"), sem("ones_set")
        NCHUNK = 7
        CHUNK = QPOS * KPOS // NCHUNK
        NSUB = 4
        SUB = CHUNK // NSUB

        BN_STEPS = 6
        IDX_READ = 4 * BN_STEPS + 7
        ACT_BIAS = 9 + HEADS + HEADS // 2
        PE_BIAS = HEADS + HEADS // 2 + 3

        def pT_evac(j):
            if j == 2:
                m = tile_rows(TILES - 1)
                return (pT[:, :, 4 * MT:ROWS], ps_s[2][0:HALF, 0:2 * MT].rearrange("p (c q) -> p c q", c=2)[:, :, 0:m])
            return (pT[:, :, 2 * MT * j:2 * MT * (j + 1)].rearrange("p c (t q) -> p t c q", t=2),
                    ps_s[j][0:HALF, 0:4 * MT].rearrange("p (t c q) -> p t c q", t=2, c=2))

        def tT_evac(b, n):
            return (tT[:, 6 * n:6 * n + 6, b * QPOS:(b + 1) * QPOS],
                    ps_t[n][0:CA, 0:6 * QPOS].rearrange("p (h q) -> p h q", h=6))

        block = ctx.enter_context(nc.Block())

        @block.sync
        def _(sp):
            sp.sem_inc(gate_out, 16)
            sp.sem_inc(out_done, 16)
            sp.dma_start(cst[:, :], consts).then_inc(consts_in, 16)
            sp.dma_start(par[:, :], params).then_inc(consts_in, 16)
            sp.dma_start(qwa[:, :, 0:CIN], qw).then_inc(consts_in, 16)
            sp.dma_start(kwa[:, :, 0:CIN], kw).then_inc(consts_in, 16)
            sp.dma_start(vwa[:, :, 0:CIN], vw).then_inc(consts_in, 16)
            sp.dma_start(pws[:, :], pw).then_inc(consts_in, 16)
            sp.dma_start(abt[:, :, :], ab).then_inc(consts_in, 16)

            def load_x(g, b):
                sp.wait_ge(pe_a.sem, pe_a.at(g, f"s{b}.2", back=1))
                sp.dma_start(xa[0:CIN, b, :], xT[:, bass.ds((g * NB + b) * KPOS, KPOS)]).then_inc(xa_in[b], 16)
                sp.wait_ge(pe_a.sem, pe_a.at(g, f"t{b}.1", back=1))
                sp.dma_start(xp[:, b, :, 0:CIN], xn[:, bass.ds(g * NB + b, 1), :, :].rearrange("p b c f -> p (b c) f")
                             ).then_inc(xp_in[b], 16)

            def gates(g):
                sp.wait_ge(dve_b.sem, dve_b.at(g, "gT"))
                sp.dma_start(gate_dram[:, :], gT[:, :]).then_inc(gate_out, 16)
                sp.wait_ge(gate_out, (g + 2) * 16)
                sp.wait_ge(dve_c.sem, dve_c.at(g, f"m{EXPERTS - 1}", back=1))
                sp.dma_start(gbc[:, :, :], gate_dram[:, :].rearrange("(o e) t -> o e t", o=1).broadcast_to((128, EXPERTS, TOK))
                             ).then_inc(gate_in, 16)

            def results_out(g):
                sp.wait_ge(act_c.sem, act_c.at(g, "ot"))
                sp.dma_start(out[bass.ds(g * TOK, TOK), :].rearrange("(p t) d -> t p d", t=PAIR), outs[:, :, :]
                             ).then_inc(out_done, 16)

            for c in range(NCHUNK):
                if c:
                    sp.wait_ge(dve_set, IDX_READ + 3 * (c - 1) + 1)
                sp.dma_start(idx_i, idxs[c].broadcast_to((HALF, CHUNK))).then_inc(idx_in, 16)
                if c == 0:
                    sp.dma_start(bvs[:, :], bqkv[:, 2 * D:3 * D].broadcast_to((PAIR, D))).then_inc(attn_w_in, 16)
                    sp.dma_start(wqkv_s[:, :], wqkv).then_inc(attn_w_in, 16)
                    sp.dma_start(wout_s[:, :], wout).then_inc(attn_w_in, 16)
                    for i, w in enumerate((fwq, fwk, fwv, fwo)):
                        sp.dma_start(fw[:, i, :], w).then_inc(ffn_w_in, 16)
                    sp.dma_start(gws[:, :], gw).then_inc(ffn_w_in, 16)
                    sp.dma_start(gbs[:, :], gb.broadcast_to((PAIR, EXPERTS))).then_inc(ffn_w_in, 16)
                sp.wait_ge(act_set, ACT_BIAS + NSUB * (c + 1))
                sp.dma_start(bias_dram[:, c, :], bias_rows).then_inc(bias_out, 16)
                sp.wait_ge(bias_out, 16 * (c + 1))
            rows = bias_dram.rearrange("h c (q k) -> (h c q) k", k=KPOS)
            sp.dma_start(bias[:, 0:TILES - 1, :], rows[0:MT * (TILES - 1), :].rearrange("(t p) k -> p t k", p=MT)
                         ).then_inc(bias_in, 16)
            sp.dma_start(bias[0:tile_rows(TILES - 1), TILES - 1, :], rows[MT * (TILES - 1):ROWS, :]).then_inc(bias_in, 16)
            sp.wait_ge(ones_set, 4)
            for b in range(NB):
                load_x(0, b)
            sp.dma_start(w1s[:, :, :], w1).then_inc(w1_in, 16)
            sp.dma_start(w2s[:, :, :], w2).then_inc(w2_in, 16)
            def iteration(a, b, c):
                if a is not None:
                    for n in range(NB):
                        load_x(a, n)
                if b is not None:
                    gates(b)
                if c is not None:
                    results_out(c)

            iteration(1, None, None)
            iteration(2, 0, None)
            with sp.Fori(2, GROUPS - 1) as i:
                iteration(i + 1, i - 1, i - 2)
            iteration(None, GROUPS - 2, GROUPS - 3)
            iteration(None, GROUPS - 1, GROUPS - 2)
            iteration(None, None, GROUPS - 1)
            sp.wait_ge(out_done, 16 * (GROUPS + 1))

        @block.gpsimd
        def _(pool):
            start_at_one_group(pool, pool_a, pool_b)
            nc.gpsimd.memset(xa[CIN:CA, :, :], 1.0).then_inc(ones_set, 1)
            pool.wait_ge(ones_set, 1)
            nc.gpsimd.memset(xp[:, :, :, CIN:CA], 1.0).then_inc(ones_set, 1)
            nc.gpsimd.memset(v1[:, :, :, LHD:LHD + 1], 1.0).then_inc(ones_set, 1)
            nc.gpsimd.memset(stat[:, :, :], 1.0).then_inc(ones_set, 1)

            def stage_a(g):
                yield from nothing(HEADS // 2 + 1)
                for b in range(NB):
                    pool.wait_ge(dve_a.sem, dve_a.at(g, f"rec{b}"))
                    pool.sem_inc(pool_waited, 1)
                    for t in range(TILES):
                        m = tile_rows(t)
                        nc.gpsimd.tensor_scalar(prob[0:m, t, :], prob[0:m, t, :], stat[0:m, 2, t:t + 1], None, ALU.mult
                                                ).then_inc(pool_a.tell(f"norm{b}.{t}"), 1)
                    yield
                    yield from nothing(4 if b + 1 < NB else 3)
                yield from nothing(HEADS // 2)

            def stage_b(g):
                def decayed(name, src, dst, dec):
                    pool.wait_ge(dve_b.sem, dve_b.at(g, name))
                    nc.gpsimd.tensor_tensor(dst[:, :].rearrange("p (b t) -> p b t", b=NB),
                                            src[:, :].rearrange("p (b t) -> p b t", b=NB),
                                            wide(dec[:, :], 1, NB), ALU.mult).then_inc(pool_b.tell(name), 1)

                def by_head(p):
                    pool.wait_ge(pool_b.sem, pool_b.at(g, "q"))
                    if p >= 2:
                        pool.wait_ge(pe_b.sem, pe_b.at(g, f"a{p - 2}.1"))
                    nc.gpsimd.tensor_tensor(qm[:, p % 2, :, :], wide(qT[:, p * PAIR:(p + 1) * PAIR], 1, LHEADS),
                                            wide(hmask, 2, PAIR), ALU.mult).then_inc(pool_b.tell(f"qm{p}"), 1)

                for name in B_UNITS:
                    if name == "q":
                        decayed("q", qd, qT, decq)
                    if name == "k":
                        decayed("k", kd, kT, deck)
                    if name == "v":
                        by_head(0)
                        by_head(1)
                    if name in ("a0.1", "a1.1"):
                        by_head(int(name[1]) + 2)
                    yield

            def iteration(a, b, c):
                take_units({"a": stage_a(a) if a is not None else None, "b": stage_b(b) if b is not None else None,
                            "c": None})

            iteration(0, None, None)
            iteration(1, 0, None)
            with pool.Fori(2, GROUPS) as i:
                iteration(i, i - 1, i - 2)
            iteration(None, GROUPS - 1, GROUPS - 2)
            iteration(None, None, GROUPS - 1)

        @block.scalar
        def _(act):
            start_at_one_group(act, act_a, act_b, act_c)
            act.wait_ge(consts_in, 7 * 16)
            for i, (n, col, w) in enumerate(((KD, P_BNQ, HEADS), (KD, P_BNK, HEADS), (VD, P_BNV, HEADS), (D, P_PROJ, 1))):
                dst = bn[0:n, i, 0:w] if i < 3 else proj_s[:, 0:1]
                nc.scalar.activation(dst, par[0:n, col + 3 * w:col + 4 * w], ACT.Sqrt, bias=eps_col[0:n, :]
                                     ).then_inc(act_set, 1)
            act.preload_act_table_set("natural_log_exp_and_others")
            nc.scalar.activation(nl[:, 0:1], par[:, P_DEC:P_DEC + 1], ACT.Exp, scale=-1.0).then_inc(act_set, 1)
            act.wait_ge(act_set, 5)
            nc.scalar.activation(nl[:, 1:2], nl[:, 0:1], ACT.Ln, bias=one_col).then_inc(act_set, 1)
            act.wait_ge(act_set, 6)
            nc.scalar.mul(nl[:, 2:3], nl[:, 1:2], -1.0).then_inc(act_set, 1)
            act.wait_ge(act_set, 7)
            tcol = cst[:, C_T:C_T + QPOS]
            nc.scalar.activation(deck[:, :], tcol, ACT.Exp, scale=nl[:, 1:2]).then_inc(act_set, 1)
            nc.scalar.activation(decq[:, :], tcol, ACT.Exp, scale=nl[:, 2:3]).then_inc(act_set, 1)
            for h in range(HEADS):
                act.wait_ge(pe_set, h + 1)
                nc.scalar.mul(mqk[:, h, :], ps_t[h % 2][0:CA, 0:CA], KD ** -0.5).then_inc(act_set, 1)
            for h2 in range(HEADS // 2):
                act.wait_ge(pe_set, HEADS + h2 + 1)
                nc.scalar.copy(wvT[:, 2 * h2:2 * h2 + 2, :],
                               ps_s[h2 % 2][0:CA, 0:2 * VD].rearrange("p (h d) -> p h d", h=2)).then_inc(act_set, 1)
            for c in range(NCHUNK):
                for s in range(NSUB):
                    act.wait_ge(pe_set, PE_BIAS + NSUB * c + s + 1)
                    if c and s == 0:
                        act.wait_ge(bias_out, 16 * c)
                    nc.scalar.copy(bias_rows[:, s * SUB:(s + 1) * SUB], ps_t[s % 2][0:HEADS, 0:SUB]).then_inc(act_set, 1)

            def stage_a(g):
                def exponentials(b):
                    for t in range(TILES):
                        m = tile_rows(t)
                        act.wait_ge(dve_a.sem, dve_a.at(g, f"neg{b}.{t}"))
                        nc.scalar.activation(prob[0:m, t, :], sneg[0:m, t, :], ACT.Exp, bias=stat[0:m, 0, t:t + 1],
                                             scale=-1.0, accum_out=stat[0:m, 1, t:t + 1]
                                             ).then_inc(act_a.tell(f"exp{b}.{t}"), 1)

                for h in range(0, HEADS, 2):
                    act.wait_ge(pe_a.sem, pe_a.at(g, f"qk{h}"))
                    nc.scalar.copy(qp[:, :, h * QPOS:(h + 1) * QPOS],
                                   ps_t[0][0:CA, 0:TOK].rearrange("p (b q) -> p b q", b=NB)
                                   ).then_inc(act_a.tell(f"qk{h}"), 1)
                    yield
                exponentials(0)
                yield
                for b in range(NB):
                    yield
                    for j in (0, 2):
                        act.wait_ge(pe_a.sem, pe_a.at(g, f"tr{b}.{j}"))
                        nc.scalar.copy(*pT_evac(j)).then_inc(act_a.tell(f"pt{b}.{j}"), 1)
                    yield
                    if b + 1 < NB:
                        exponentials(b + 1)
                        yield
                    act.wait_ge(pe_a.sem, pe_a.at(g, f"t{b}.0"))
                    nc.scalar.copy(*tT_evac(b, 0)).then_inc(act_a.tell(f"tt{b}.0"), 1)
                    yield
                    yield
                for j in range(HEADS // 2):
                    act.wait_ge(pe_a.sem, pe_a.at(g, f"wv{j}"))
                    nc.scalar.activation(relu[:, j % 2, :], ps_t[j % 2][:, 0:TOK], ACT.Relu, bias=three_col
                                         ).then_inc(act_a.tell(f"relu{j}"), 1)
                    yield

            def stage_b(g):
                tok = ps_b[:, 0:TOK]

                def centred(n):
                    act.wait_ge(pe_b.sem, pe_b.at(g, f"c{n}"))
                    nc.scalar.copy(cT[:, :], tok).then_inc(act_b.tell(f"c{n}"), 1)
                    nc.scalar.activation(sq[:, :], tok, ACT.Square).then_inc(act_b.tell(f"sq{n}"), 1)

                def inverse_root(pe_name, ln, rs, dst, bias_col, scale):
                    act.wait_ge(pe_b.sem, pe_b.at(g, pe_name))
                    nc.scalar.activation(lnb[:, :], tok, ACT.Ln, bias=bias_col, scale=scale).then_inc(act_b.tell(ln), 1)
                    act.wait_ge(act_b.sem, act_b.at(g, ln))
                    nc.scalar.activation(dst[:, :], lnb[:, :], ACT.Exp, scale=-0.5).then_inc(act_b.tell(rs), 1)

                act.wait_ge(pe_b.sem, pe_b.at(g, "proj"))
                nc.scalar.activation(h1T[:, :], tok, ACT.Identity, bias=proj_s[:, 2:3], scale=proj_s[:, 3:4]
                                     ).then_inc(act_b.tell("h1"), 1)
                yield
                centred(1)
                yield
                inverse_root("v1", "ln1", "rs1", r, eps_col, 1.0)
                yield
                for name, e, p, col in (("q", eq, pq, P_BQ), ("k", ek, pk, P_BK)):
                    act.wait_ge(pe_b.sem, pe_b.at(g, name))
                    nc.scalar.activation(e[:, :], tok, ACT.Exp, bias=par[:, col:col + 1]).then_inc(act_b.tell("e" + name), 1)
                    nc.scalar.activation(p[:, :], tok, ACT.Relu, bias=par[:, col:col + 1]).then_inc(act_b.tell("p" + name), 1)
                    yield
                yield from nothing(1 + 2 * PAIRS + PAIRS // 2)
                act.wait_ge(pe_b.sem, pe_b.at(g, "oT"))
                nc.scalar.copy(oT[:, :], tok).then_inc(act_b.tell("oT"), 1)
                yield
                act.wait_ge(pe_b.sem, pe_b.at(g, "wout"))
                nc.scalar.activation(a2T[:, :], tok, ACT.Identity, bias=par[:, P_BOUT:P_BOUT + 1]
                                     ).then_inc(act_b.tell("a2"), 1)
                yield
                centred(2)
                yield
                inverse_root("v2", "ln2", "rs2", r, eps_col, 1.0)
                yield
                centred(3)
                yield
                inverse_root("v3", "ln3", "rs3", r, eps2_col, 1.0 + EPS)
                yield
                for name, dst, rr in (("q", q2T, r), ("k", k2T, r2)):
                    act.wait_ge(pe_b.sem, pe_b.at(g, name + "2"))
                    nc.scalar.copy(dst[:, :], tok).then_inc(act_b.tell(name + "2"), 1)
                    nc.scalar.activation(sq[:, :], tok, ACT.Square).then_inc(act_b.tell(name + "sq"), 1)
                    yield
                    inverse_root(name + "ss", name + "ln", name + "rs", rr, eps12_col, 1.0)
                    yield
                act.wait_ge(pe_b.sem, pe_b.at(g, "vx"))
                nc.scalar.copy(v2[:, :, :], ps_b[0:PAIR, :].rearrange("p (n d) -> p n d", n=PAIRS)
                               ).then_inc(act_b.tell("vx"), 1)
                yield
                for h in range(FHEADS):
                    act.wait_ge(dve_b.sem, dve_b.at(g, f"sub{h}"))
                    nc.scalar.activation(p2[:, h, :, :], s2[:, h, :, :], ACT.Exp).then_inc(act_b.tell(f"e{h}"), 1)
                    yield
                for h in range(FHEADS):
                    act.wait_ge(pe_b.sem, pe_b.at(g, f"pT{h}"))
                    nc.scalar.copy(p2T[:, h, :, :], ps_b[0:PAIR, 0:TOK].rearrange("p (n q) -> p n q", n=PAIRS)
                                   ).then_inc(act_b.tell(f"pT{h}"), 1)
                    yield
                act.wait_ge(pe_b.sem, pe_b.at(g, "av"))
                nc.scalar.copy(o2T[:, :], tok).then_inc(act_b.tell("o2T"), 1)
                yield
                act.wait_ge(pe_b.sem, pe_b.at(g, "wo"))
                nc.scalar.copy(yT[:, :], tok).then_inc(act_b.tell("y"), 1)
                yield
                act.wait_ge(dve_b.sem, dve_b.at(g, "gsub"))
                nc.scalar.activation(gl[:, 1, :, :], gl[:, 0, :, :], ACT.Exp).then_inc(act_b.tell("gexp"), 1)
                yield
                yield

            def stage_c(g):
                for e in range(EXPERTS):
                    for j in range(FCH):
                        act.wait_ge(pe_c.sem, pe_c.at(g, f"u{e}.{j}"))
                        col = P_B1 + e * FCH + j
                        nc.scalar.activation(hid[:, j % 2, :], ps_h[:, 0:TOK], ACT.Gelu_apprx_tanh,
                                             bias=par[:, col:col + 1]).then_inc(act_c.tell(f"g{e}.{j}"), 1)
                        yield
                yield
                act.wait_ge(pe_c.sem, pe_c.at(g, "ot"))
                act.wait_ge(out_done, (g + 1) * 16)
                nc.scalar.copy(outs[:, :, :], ps_e[0:PAIR, :].rearrange("p (n d) -> p n d", n=PAIRS)
                               ).then_inc(act_c.tell("ot"), 1)
                yield

            def iteration(a, b, c):
                take_units({"a": stage_a(a) if a is not None else None, "b": stage_b(b) if b is not None else None,
                            "c": stage_c(c) if c is not None else None},
                           on_x=lambda: act.preload_act_table_set("natural_log_exp_and_others"))

            iteration(0, None, None)
            iteration(1, 0, None)
            with act.Fori(2, GROUPS) as i:
                iteration(i, i - 1, i - 2)
            iteration(None, GROUPS - 1, GROUPS - 2)
            iteration(None, None, GROUPS - 1)

        @block.vector
        def _(dve):
            start_at_one_group(dve, dve_a, dve_b, dve_c)
            told = [0]

            def then(ins):
                told[0] += 1
                ins.then_inc(dve_set, 1)
                dve.wait_ge(dve_set, told[0])

            dve.wait_ge(consts_in, 7 * 16)
            for i, (n, col, w, wa) in enumerate(((KD, P_BNQ, HEADS, qwa), (KD, P_BNK, HEADS, kwa), (VD, P_BNV, HEADS, vwa),
                                                 (D, P_PROJ, 1, None))):
                dve.wait_ge(act_set, i + 1)
                root = bn[0:n, i, 0:w] if i < 3 else proj_s[:, 0:1]
                scale = bn[0:n, 3, 0:w] if i < 3 else proj_s[:, 1:2]
                prod = bn[0:n, 4, 0:w] if i < 3 else proj_s[:, 0:1]
                shift = bn[0:n, 5, 0:w] if i < 3 else proj_s[:, 2:3]
                gamma, beta, mu = (par[0:n, col + k * w:col + (k + 1) * w] for k in range(3))
                then(nc.vector.reciprocal(root, root))
                then(nc.vector.tensor_tensor(scale, gamma, root, ALU.mult))
                then(nc.vector.tensor_tensor(prod, mu, scale, ALU.mult))
                then(nc.vector.tensor_tensor(shift, beta, prod, ALU.subtract))
                if wa is not None:
                    then(nc.vector.tensor_tensor(wa[:, :, 0:CIN], wa[:, :, 0:CIN],
                                                 wide(scale, 2, CIN), ALU.mult))
                    then(nc.vector.tensor_copy(wa[:, :, CIN:CA], shift.unsqueeze(2)))
                else:
                    then(nc.vector.tensor_scalar(proj_s[:, 3:4], scale, 1.0 / 6.0, None, ALU.mult))
                    then(nc.vector.memset(den[:, :, :], 1.0))
            dve.wait_ge(act_set, 9)
            then(nc.vector.tensor_scalar(decq[:, :], decq[:, :], LHD ** -0.5, None, ALU.mult))
            then(nc.vector.tensor_scalar(fg2[:, 0:1], par[:, P_FG:P_FG + 1], 1.0, None, ALU.mult))
            then(nc.vector.tensor_scalar(fg2[:, 1:2], par[:, P_KN:P_KN + 1], FHD ** 0.5, None, ALU.mult))
            for i in range(3):
                dve.wait_ge(pe_set, HEADS + HEADS // 2 + i + 1)
                then(nc.vector.tensor_copy(pwT[:, 2 * i:2 * i + 2, :],
                                           ps_s[2 if i % 2 == 0 else 1][:, 256:512].rearrange("p (n d) -> p n d", n=2)))
            then(nc.vector.memset(gl[:, 2, :, :], 0.0))
            assert told[0] == IDX_READ
            for c in range(NCHUNK):
                dve.wait_ge(idx_in, 16 * (c + 1))
                then(nc.vector.tensor_copy(idx_f, idx_i))
                if c:
                    dve.wait_ge(pe_set, PE_BIAS + NSUB * c)
                for k in range(2):
                    then(nc.vector.tensor_scalar(onehot[k], idx_f, cst[0:HALF, C_IOTA + k:C_IOTA + k + 1], None,
                                                 ALU.is_equal))
            dve.wait_ge(bias_in, 32)
            dve.wait_ge(ones_set, 4)

            def stage_a(g):
                def negated_scores(b):
                    for t in range(TILES):
                        m = tile_rows(t)
                        if t % 2 == 0:
                            dve.wait_ge(pe_a.sem, pe_a.at(g, f"s{b}.{t // 2}"))
                            dve.sem_inc(dve_waited, 1)
                        nc.vector.tensor_tensor_reduce(
                            out=sneg[0:m, t, :], in0=ps_s[t // 2][0:m, (t % 2) * KPOS:(t % 2 + 1) * KPOS],
                            in1=bias[0:m, t, :], scale=-1.0, scalar=3.0e38, op0=ALU.add, op1=ALU.min,
                            accum_out=stat[0:m, 0, t:t + 1]).then_inc(dve_a.tell(f"neg{b}.{t}"), 1)

                for h in range(1, HEADS, 2):
                    dve.wait_ge(pe_a.sem, pe_a.at(g, f"qk{h}"))
                    nc.vector.tensor_copy(qp[:, :, h * QPOS:(h + 1) * QPOS],
                                          ps_t[1][0:CA, 0:TOK].rearrange("p (b q) -> p b q", b=NB)
                                          ).then_inc(dve_a.tell(f"qk{h}"), 1)
                    yield
                negated_scores(0)
                yield
                for b in range(NB):
                    dve.wait_ge(act_a.sem, act_a.at(g, f"exp{b}.{TILES - 1}"))
                    nc.vector.reciprocal(stat[:, 2, 0:TILES], stat[:, 1, 0:TILES]).then_inc(dve_a.tell(f"rec{b}"), 1)
                    yield
                    dve.wait_ge(pe_a.sem, pe_a.at(g, f"tr{b}.1"))
                    nc.vector.tensor_copy(*pT_evac(1)).then_inc(dve_a.tell(f"pt{b}.1"), 1)
                    yield
                    if b + 1 < NB:
                        negated_scores(b + 1)
                        yield
                    yield
                    dve.wait_ge(pe_a.sem, pe_a.at(g, f"t{b}.1"))
                    nc.vector.tensor_copy(*tT_evac(b, 1)).then_inc(dve_a.tell(f"tt{b}.1"), 1)
                    yield
                for j in range(HEADS // 2):
                    dve.wait_ge(act_a.sem, act_a.at(g, f"relu{j}"))
                    nc.vector.scalar_tensor_tensor(out=hs[:, j, :], in0=relu[:, j % 2, :], scalar=6.0,
                                                   in1=ps_t[j % 2][:, 0:TOK], op0=ALU.min, op1=ALU.mult
                                                   ).then_inc(dve_a.tell(f"hs{j}"), 1)
                    yield

            def stage_b(g):
                tok = ps_b[:, 0:TOK]
                stt = nc.vector.scalar_tensor_tensor
                tt = nc.vector.tensor_tensor

                yield from nothing(2)
                dve.wait_ge(act_b.sem, act_b.at(g, "rs1"))
                tt(hnT[:, :], cT[:, :], r[:, :], ALU.mult).then_inc(dve_b.tell("hn"), 1)
                yield
                for name, e, p, dst in (("q", eq, pq, qd), ("k", ek, pk, kd)):
                    dve.wait_ge(act_b.sem, act_b.at(g, "p" + name))
                    stt(out=dst[:, :], in0=e[:, :], scalar=1.0, in1=p[:, :], op0=ALU.min, op1=ALU.add
                        ).then_inc(dve_b.tell(name), 1)
                    yield
                dve.wait_ge(pe_b.sem, pe_b.at(g, "v"))
                tt(v1[:, :, :, 0:LHD], ps_b[0:PAIR, :].rearrange("p (n h f) -> p n h f", n=PAIRS, h=LHEADS),
                   wide(bvs[:, :].rearrange("p (h f) -> p h f", h=LHEADS), 1, PAIRS), ALU.add
                   ).then_inc(dve_b.tell("v"), 1)
                yield
                for p in range(PAIRS):
                    for i in range(2):
                        dve.wait_ge(pe_b.sem, pe_b.at(g, f"a{p}.{i}"))
                        tt(aT[:, p % 2, 4 * i:4 * i + 4, :], ps_b[0:PAIR, 0:4 * PAIR].rearrange("p (h q) -> p h q", h=4),
                           wide(causal, 1, 4), ALU.mult).then_inc(dve_b.tell(f"a{p}.{i}"), 1)
                        yield
                    if p % 2:
                        n = p // 2
                        num = ps_b[0:PAIR, 0:16 * (LHD + 1)].rearrange("p (h f) -> p h f", h=16)
                        dve.wait_ge(pe_b.sem, pe_b.at(g, f"num{n}"))
                        nc.vector.tensor_scalar(den[:, 0, :].unsqueeze(2), num[:, :, LHD:LHD + 1], EPS, None, ALU.add
                                                ).then_inc(dve_b.tell(f"den{n}"), 1)
                        dve.wait_ge(dve_b.sem, dve_b.at(g, f"den{n}"))
                        nc.vector.reciprocal(den[:, 1, :], den[:, 0, :]).then_inc(dve_b.tell(f"rden{n}"), 1)
                        dve.wait_ge(dve_b.sem, dve_b.at(g, f"rden{n}"))
                        tt(lo[:, 2 * n:2 * n + 2, :].rearrange("p n (h f) -> p (n h) f", f=LHD), num[:, :, 0:LHD],
                           wide(den[:, 1, :], 2, LHD), ALU.mult).then_inc(dve_b.tell(f"o{n}"), 1)
                        yield
                yield from nothing(3)
                dve.wait_ge(act_b.sem, act_b.at(g, "rs2"))
                stt(out=ga[:, :], in0=cT[:, :], scalar=par[:, P_GAMMA:P_GAMMA + 1], in1=r[:, :], op0=ALU.mult,
                    op1=ALU.mult).then_inc(dve_b.tell("ga"), 1)
                dve.wait_ge(dve_b.sem, dve_b.at(g, "ga"))
                stt(out=h2T[:, :], in0=ga[:, :], scalar=par[:, P_BETA:P_BETA + 1], in1=h1T[:, :], op0=ALU.add,
                    op1=ALU.add).then_inc(dve_b.tell("h2"), 1)
                yield
                yield
                dve.wait_ge(act_b.sem, act_b.at(g, "rs3"))
                stt(out=gx[:, :], in0=cT[:, :], scalar=fg2[:, 0:1], in1=r[:, :], op0=ALU.mult, op1=ALU.mult
                    ).then_inc(dve_b.tell("gx"), 1)
                dve.wait_ge(dve_b.sem, dve_b.at(g, "gx"))
                nc.vector.tensor_scalar(hxT[:, :], gx[:, :], par[:, P_FB:P_FB + 1], None, ALU.add
                                        ).then_inc(dve_b.tell("hx"), 1)
                yield
                for name, src, rr, dst, col in (("q", q2T, r, q2n, par[:, P_QN:P_QN + 1]), ("k", k2T, r2, k2n, fg2[:, 1:2])):
                    yield
                    dve.wait_ge(act_b.sem, act_b.at(g, name + "rs"))
                    stt(out=dst[:, :], in0=src[:, :], scalar=col, in1=rr[:, :], op0=ALU.mult, op1=ALU.mult
                        ).then_inc(dve_b.tell(name + "2n"), 1)
                    yield
                yield
                for h in range(FHEADS):
                    if h:
                        yield
                    dve.wait_ge(pe_b.sem, pe_b.at(g, f"s{h}"))
                    tt(s2[:, h, :, :], ps_b[0:PAIR, 0:TOK].rearrange("p (n k) -> p n k", n=PAIRS),
                       wide(addmask, 1, PAIRS), ALU.add).then_inc(dve_b.tell(f"sm{h}"), 1)
                    dve.wait_ge(dve_b.sem, dve_b.at(g, f"sm{h}"))
                    nc.vector.tensor_reduce(st2[:, 0, h, :], s2[:, h, :, :], AX.X, ALU.max).then_inc(dve_b.tell(f"mx{h}"), 1)
                    dve.wait_ge(dve_b.sem, dve_b.at(g, f"mx{h}"))
                    tt(s2[:, h, :, :], s2[:, h, :, :], wide(st2[:, 0, h, :], 2, PAIR), ALU.subtract
                       ).then_inc(dve_b.tell(f"sub{h}"), 1)
                for h in range(FHEADS):
                    dve.wait_ge(act_b.sem, act_b.at(g, f"e{h}"))
                    nc.vector.tensor_reduce(st2[:, 1, h, :], p2[:, h, :, :], AX.X, ALU.add).then_inc(dve_b.tell(f"sum{h}"), 1)
                    dve.wait_ge(dve_b.sem, dve_b.at(g, f"sum{h}"))
                    nc.vector.reciprocal(st2[:, 2, h, :], st2[:, 1, h, :]).then_inc(dve_b.tell(f"rc{h}"), 1)
                    dve.wait_ge(dve_b.sem, dve_b.at(g, f"rc{h}"))
                    tt(p2[:, h, :, :], p2[:, h, :, :], wide(st2[:, 2, h, :], 2, PAIR), ALU.mult
                       ).then_inc(dve_b.tell(f"pn{h}"), 1)
                yield
                yield from nothing(4)
                dve.wait_ge(pe_b.sem, pe_b.at(g, "g"))
                tt(gl[:, 0, :, :], ps_b[0:PAIR, 0:PAIRS * EXPERTS].rearrange("p (n e) -> p n e", n=PAIRS),
                   wide(gbs[:, :], 1, PAIRS), ALU.add).then_inc(dve_b.tell("g"), 1)
                dve.wait_ge(dve_b.sem, dve_b.at(g, "g"))
                nc.vector.tensor_reduce(gst[:, 0, :], gl[:, 0, :, :], AX.X, ALU.max).then_inc(dve_b.tell("gmx"), 1)
                dve.wait_ge(dve_b.sem, dve_b.at(g, "gmx"))
                tt(gl[:, 0, :, :], gl[:, 0, :, :], wide(gst[:, 0, :], 2, EXPERTS), ALU.subtract
                   ).then_inc(dve_b.tell("gsub"), 1)
                dve.wait_ge(act_b.sem, act_b.at(g, "gexp"))
                nc.vector.tensor_reduce(gst[:, 1, :], gl[:, 1, :, :], AX.X, ALU.add).then_inc(dve_b.tell("gsum"), 1)
                dve.wait_ge(dve_b.sem, dve_b.at(g, "gsum"))
                nc.vector.reciprocal(gst[:, 2, :], gst[:, 1, :]).then_inc(dve_b.tell("grc"), 1)
                dve.wait_ge(dve_b.sem, dve_b.at(g, "grc"))
                tt(gl[:, 2, :, :], gl[:, 1, :, :], wide(gst[:, 2, :], 2, EXPERTS), ALU.mult
                   ).then_inc(dve_b.tell("gn"), 1)
                yield
                dve.wait_ge(pe_b.sem, pe_b.at(g, "gT"))
                dve.wait_ge(gate_out, (g + 1) * 16)
                nc.vector.tensor_copy(gT[:, :], ps_b[0:EXPERTS, 0:TOK]).then_inc(dve_b.tell("gT"), 1)
                yield

            def stage_c(g):
                def gated(e):
                    dve.wait_ge(pe_c.sem, pe_c.at(g, f"d{e}.{FCH - 1}"))
                    dve.wait_ge(dve_c.sem, dve_c.at(g, f"acc{e - 1}" if e else "acc"))
                    nc.vector.scalar_tensor_tensor(out=tmp[:, :], in0=ps_e[:, 0:TOK], scalar=par[:, P_B2 + e:P_B2 + e + 1],
                                                   in1=gbc[:, e, :], op0=ALU.add, op1=ALU.mult
                                                   ).then_inc(dve_c.tell(f"m{e}"), 1)
                    dve.wait_ge(dve_c.sem, dve_c.at(g, f"m{e}"))
                    nc.vector.tensor_tensor(acc[:, :], acc[:, :], tmp[:, :], ALU.add).then_inc(dve_c.tell(f"acc{e}"), 1)

                dve.wait_ge(act_b.sem, act_b.at(g, "y"))
                nc.vector.tensor_copy(yc[:, :], yT[:, :]).then_inc(dve_c.tell("yc"), 1)
                dve.wait_ge(pe_c.sem, pe_c.at(g, "ot", back=1))
                nc.vector.tensor_copy(acc[:, :], h2T[:, :]).then_inc(dve_c.tell("acc"), 1)
                for e in range(EXPERTS):
                    if e == 1:
                        dve.wait_ge(gate_in, (g + 1) * 16)
                    if e:
                        gated(e - 1)
                    yield from nothing(FCH)
                gated(EXPERTS - 1)
                yield
                yield

            def iteration(a, b, c):
                take_units({"a": stage_a(a) if a is not None else None, "b": stage_b(b) if b is not None else None,
                            "c": stage_c(c) if c is not None else None})

            iteration(0, None, None)
            iteration(1, 0, None)
            with dve.Fori(2, GROUPS) as i:
                iteration(i, i - 1, i - 2)
            iteration(None, GROUPS - 1, GROUPS - 2)
            iteration(None, None, GROUPS - 1)

        @block.tensor
        def _(pe):
            start_at_one_group(pe, pe_a, pe_b, pe_c)
            mm = nc.tensor.matmul
            pe.wait_ge(dve_set, 2 * BN_STEPS)
            for h in range(HEADS):
                if h >= 2:
                    pe.wait_ge(act_set, 9 + h - 1)
                mm(ps_t[h % 2][0:CA, 0:CA], qwa[:, h, :], kwa[:, h, :], start=True, stop=True).then_inc(pe_set, 1)
            pe.wait_ge(dve_set, 3 * BN_STEPS)
            for h2 in range(HEADS // 2):
                if h2 >= 2:
                    pe.wait_ge(act_set, 9 + HEADS + h2 - 1)
                for i in range(2):
                    last = nc.tensor.transpose(ps_s[h2 % 2][0:CA, i * VD:(i + 1) * VD], vwa[:, 2 * h2 + i, :],
                                               ident[0:VD, 0:VD])
                last.then_inc(pe_set, 1)
            pe.wait_ge(act_set, 9 + HEADS + HEADS // 2)
            for i in range(3):
                if i == 2:
                    pe.wait_ge(dve_set, IDX_READ - 3)
                for k in range(2):
                    last = nc.tensor.transpose(ps_s[2 if i % 2 == 0 else 1][:, 256 + 128 * k:384 + 128 * k],
                                               pws[:, (2 * i + k) * 128:(2 * i + k + 1) * 128], ident)
                last.then_inc(pe_set, 1)
            for c in range(NCHUNK):
                pe.wait_ge(dve_set, IDX_READ + 3 * (c + 1))
                for s in range(NSUB):
                    if s >= 2 or c:
                        pe.wait_ge(act_set, ACT_BIAS + NSUB * c + s - 1)
                    for k in range(2):
                        last = mm(ps_t[s % 2][0:HEADS, 0:SUB], abt[:, k, :], onehot[k][:, s * SUB:(s + 1) * SUB],
                                  start=(k == 0), stop=(k == 1))
                    last.then_inc(pe_set, 1)
            pe.wait_ge(act_set, ACT_BIAS + NSUB * NCHUNK)
            pe.wait_ge(ones_set, 4)

            def stage_a(g):
                def scores(b):
                    for j in range(3):
                        s = (act_a, dve_a, act_a)[j]
                        pe.wait_ge(s.sem, s.at(g, f"pt{b - 1}.{j}") if b else s.at(g, f"pt{NB - 1}.{j}", back=1))
                        for t in range(2 * j, min(2 * j + 2, TILES)):
                            m = tile_rows(t)
                            last = mm(ps_s[j][0:m, (t % 2) * KPOS:(t % 2 + 1) * KPOS], qp[:, b, MT * t:MT * t + m],
                                      xa[:, b, :], start=True, stop=True)
                        last.then_inc(pe_a.tell(f"s{b}.{j}"), 1)

                for b in range(NB):
                    pe.wait_ge(xa_in[b], (g + 1) * 16)
                for h in range(HEADS):
                    if h >= 2:
                        s = (act_a, dve_a)[h % 2]
                        pe.wait_ge(s.sem, s.at(g, f"qk{h - 2}"))
                    elif h == 0:
                        pe.wait_ge(dve_a.sem, dve_a.at(g, f"hs{HEADS // 2 - 1}", back=1))
                    xs = xa[:, :, :].rearrange("p b (i u j v) -> p b i u j v", i=OUT_RES, u=2, v=2)[:, :, :, 0, :, 0]
                    mm(ps_t[h % 2][0:CA, 0:TOK], mqk[:, h, :], xs, start=True, stop=True
                       ).then_inc(pe_a.tell(f"qk{h}"), 1)
                    if h % 2:
                        yield
                pe.wait_ge(act_a.sem, act_a.at(g, f"qk{HEADS - 2}"))
                pe.wait_ge(dve_a.sem, dve_a.at(g, f"qk{HEADS - 1}"))
                scores(0)
                yield
                for b in range(NB):
                    yield
                    for j in range(3):
                        for t in range(2 * j, min(2 * j + 2, TILES)):
                            m = tile_rows(t)
                            pe.wait_ge(pool_a.sem, pool_a.at(g, f"norm{b}.{t}"))
                            for c in range(2):
                                col = (t % 2) * 2 * MT + c * MT
                                last = nc.tensor.transpose(ps_s[j][0:HALF, col:col + m],
                                                           prob[0:m, t, c * HALF:(c + 1) * HALF], ident[0:m, 0:m])
                        last.then_inc(pe_a.tell(f"tr{b}.{j}"), 1)
                    yield
                    if b + 1 < NB:
                        scores(b + 1)
                        yield
                    pe.wait_ge(xp_in[b], (g + 1) * 16)
                    pe.wait_ge(act_a.sem, act_a.at(g, f"pt{b}.2"))
                    pe.wait_ge(dve_a.sem, dve_a.at(g, f"pt{b}.1"))
                    for n in range(2):
                        s = (act_a, dve_a)[n]
                        if b:
                            pe.wait_ge(s.sem, s.at(g, f"tt{b - 1}.{n}"))
                        for c in range(2):
                            last = mm(ps_t[n][0:CA, 0:6 * QPOS], xp[:, b, c, :],
                                      pT[:, c, 6 * QPOS * n:6 * QPOS * (n + 1)], start=(c == 0), stop=(c == 1))
                        last.then_inc(pe_a.tell(f"t{b}.{n}"), 1)
                        yield
                pe.wait_ge(act_a.sem, act_a.at(g, f"tt{NB - 1}.0"))
                pe.wait_ge(dve_a.sem, dve_a.at(g, f"tt{NB - 1}.1"))
                for j in range(HEADS // 2):
                    if j >= 2:
                        pe.wait_ge(dve_a.sem, dve_a.at(g, f"hs{j - 2}"))
                    for i in range(2):
                        last = mm(ps_t[j % 2][VD * i:VD * (i + 1), 0:TOK], wvT[:, 2 * j + i, :], tT[:, 2 * j + i, :],
                                  start=True, stop=True)
                    last.then_inc(pe_a.tell(f"wv{j}"), 1)
                    yield

            def stage_b(g):
                tok = ps_b[:, 0:TOK]

                def product(name, w, x):
                    mm(tok, w, x, start=True, stop=True).then_inc(pe_b.tell(name), 1)

                def token_rows(name, x, w, n):
                    for p in range(PAIRS):
                        last = mm(ps_b[0:PAIR, n * p:n * (p + 1)], x[:, p * PAIR:(p + 1) * PAIR], w, start=True, stop=True)
                    last.then_inc(pe_b.tell(name), 1)

                pe.wait_ge(dve_b.sem, dve_b.at(g, "gT", back=1))
                pe.wait_ge(dve_a.sem, dve_a.at(g, f"hs{HEADS // 2 - 1}"))
                for j in range(HEADS // 2):
                    last = mm(tok, pwT[:, j, :], hs[:, j, :], start=(j == 0), stop=(j == HEADS // 2 - 1))
                last.then_inc(pe_b.tell("proj"), 1)
                yield
                pe.wait_ge(act_b.sem, act_b.at(g, "h1"))
                product("c1", center, h1T[:, :])
                yield
                pe.wait_ge(act_b.sem, act_b.at(g, "sq1"))
                product("v1", mean, sq[:, :])
                yield
                pe.wait_ge(dve_b.sem, dve_b.at(g, "hn"))
                product("q", wqkv_s[:, 0:D], hnT[:, :])
                yield
                pe.wait_ge(act_b.sem, act_b.at(g, "pq"))
                product("k", wqkv_s[:, D:2 * D], hnT[:, :])
                yield
                pe.wait_ge(act_b.sem, act_b.at(g, "pk"))
                token_rows("v", hnT, wqkv_s[:, 2 * D:3 * D], D)
                yield
                pe.wait_ge(dve_b.sem, dve_b.at(g, "v"))
                pe.wait_ge(pool_b.sem, pool_b.at(g, "k"))
                for p in range(PAIRS):
                    pe.wait_ge(pool_b.sem, pool_b.at(g, f"qm{p}"))
                    for i in range(2):
                        if i:
                            pe.wait_ge(dve_b.sem, dve_b.at(g, f"a{p}.0"))
                        elif p == 2:
                            pe.wait_ge(dve_b.sem, dve_b.at(g, "o0"))
                        elif p:
                            pe.wait_ge(dve_b.sem, dve_b.at(g, f"a{p - 1}.1"))
                        mm(ps_b[0:PAIR, 0:4 * PAIR], kT[:, p * PAIR:(p + 1) * PAIR], qm[:, p % 2, 4 * i:4 * i + 4, :],
                           start=True, stop=True).then_inc(pe_b.tell(f"a{p}.{i}"), 1)
                        yield
                    if p % 2:
                        pe.wait_ge(dve_b.sem, dve_b.at(g, f"a{p}.1"))
                        for k in range(2):
                            for h in range(LHEADS):
                                col = (k * LHEADS + h) * (LHD + 1)
                                last = mm(ps_b[0:PAIR, col:col + LHD + 1], aT[:, k, h, :], v1[:, p - 1 + k, h, :],
                                          start=True, stop=True)
                        last.then_inc(pe_b.tell(f"num{p // 2}"), 1)
                        yield
                pe.wait_ge(dve_b.sem, dve_b.at(g, "o1"))
                for p in range(PAIRS):
                    last = nc.tensor.transpose(ps_b[:, p * PAIR:(p + 1) * PAIR], lo[:, p, :], ident[0:PAIR, 0:PAIR])
                last.then_inc(pe_b.tell("oT"), 1)
                yield
                pe.wait_ge(act_b.sem, act_b.at(g, "oT"))
                product("wout", wout_s[:, :], oT[:, :])
                yield
                pe.wait_ge(act_b.sem, act_b.at(g, "a2"))
                product("c2", center, a2T[:, :])
                yield
                pe.wait_ge(act_b.sem, act_b.at(g, "sq2"))
                product("v2", mean, sq[:, :])
                yield
                pe.wait_ge(dve_b.sem, dve_b.at(g, "h2"))
                product("c3", center, h2T[:, :])
                yield
                pe.wait_ge(act_b.sem, act_b.at(g, "sq3"))
                product("v3", mean, sq[:, :])
                yield
                pe.wait_ge(dve_b.sem, dve_b.at(g, "hx"))
                product("q2", fw[:, 0, :], hxT[:, :])
                yield
                pe.wait_ge(act_b.sem, act_b.at(g, "qsq"))
                product("qss", headsum, sq[:, :])
                yield
                pe.wait_ge(act_b.sem, act_b.at(g, "qln"))
                product("k2", fw[:, 1, :], hxT[:, :])
                yield
                pe.wait_ge(act_b.sem, act_b.at(g, "ksq"))
                product("kss", headsum, sq[:, :])
                yield
                pe.wait_ge(act_b.sem, act_b.at(g, "kln"))
                token_rows("vx", hxT, fw[:, 2, :], D)
                yield
                pe.wait_ge(act_b.sem, act_b.at(g, "vx"))
                pe.wait_ge(dve_b.sem, dve_b.at(g, "k2n"))
                for h in range(FHEADS):
                    if h:
                        pe.wait_ge(dve_b.sem, dve_b.at(g, "sm0"))
                    f = slice(FHD * h, FHD * (h + 1))
                    for p in range(PAIRS):
                        t = slice(p * PAIR, (p + 1) * PAIR)
                        last = mm(ps_b[0:PAIR, t], q2n[f, t], k2n[f, t], start=True, stop=True)
                    last.then_inc(pe_b.tell(f"s{h}"), 1)
                    yield
                for h in range(FHEADS):
                    if h:
                        pe.wait_ge(act_b.sem, act_b.at(g, "pT0"))
                    pe.wait_ge(dve_b.sem, dve_b.at(g, f"pn{h}"))
                    for p in range(PAIRS):
                        last = nc.tensor.transpose(ps_b[0:PAIR, p * PAIR:(p + 1) * PAIR], p2[:, h, p, :],
                                                   ident[0:PAIR, 0:PAIR])
                    last.then_inc(pe_b.tell(f"pT{h}"), 1)
                    yield
                pe.wait_ge(act_b.sem, act_b.at(g, "pT1"))
                for h in range(FHEADS):
                    for p in range(PAIRS):
                        last = mm(ps_b[FHD * h:FHD * (h + 1), p * PAIR:(p + 1) * PAIR], v2[:, p, FHD * h:FHD * (h + 1)],
                                  p2T[:, h, p, :], start=True, stop=True)
                last.then_inc(pe_b.tell("av"), 1)
                yield
                pe.wait_ge(act_b.sem, act_b.at(g, "o2T"))
                product("wo", fw[:, 3, :], o2T[:, :])
                yield
                pe.wait_ge(act_b.sem, act_b.at(g, "y"))
                token_rows("g", yT, gws[:, :], EXPERTS)
                yield
                pe.wait_ge(dve_b.sem, dve_b.at(g, "gn"))
                for p in range(PAIRS):
                    last = nc.tensor.transpose(ps_b[0:EXPERTS, p * PAIR:(p + 1) * PAIR], gl[:, 2, p, :],
                                               ident[0:PAIR, 0:PAIR])
                last.then_inc(pe_b.tell("gT"), 1)
                yield

            def stage_c(g):
                def up(e, j):
                    if e or j:
                        pe.wait_ge(act_c.sem, act_c.at(g, f"g{e}.{j - 1}" if j else f"g{e - 1}.{FCH - 1}"))
                    mm(ps_h[:, 0:TOK], w1s[:, e, 128 * j:128 * (j + 1)], yc[:, :], start=True, stop=True
                       ).then_inc(pe_c.tell(f"u{e}.{j}"), 1)

                def down(e, j):
                    pe.wait_ge(act_c.sem, act_c.at(g, f"g{e}.{j}"))
                    if j == 0:
                        if e:
                            pe.wait_ge(dve_c.sem, dve_c.at(g, f"m{e - 1}"))
                        else:
                            pe.wait_ge(act_c.sem, act_c.at(g, "ot", back=1))
                    mm(ps_e[:, 0:TOK], w2s[:, e * FCH + j, :], hid[:, j % 2, :], start=(j == 0), stop=(j == FCH - 1)
                       ).then_inc(pe_c.tell(f"d{e}.{j}"), 1)

                pe.wait_ge(dve_c.sem, dve_c.at(g, "acc"))
                before = None
                for e in range(EXPERTS):
                    for j in range(FCH):
                        up(e, j)
                        if before:
                            down(*before)
                        before = (e, j)
                        yield
                down(*before)
                yield
                pe.wait_ge(dve_c.sem, dve_c.at(g, f"acc{EXPERTS - 1}"))
                for p in range(PAIRS):
                    last = nc.tensor.transpose(ps_e[0:PAIR, p * D:(p + 1) * D], acc[:, p * PAIR:(p + 1) * PAIR], ident)
                last.then_inc(pe_c.tell("ot"), 1)
                yield

            pe.wait_ge(attn_w_in, 3 * 16)
            pe.wait_ge(ffn_w_in, 6 * 16)
            pe.wait_ge(w1_in, 16)
            pe.wait_ge(w2_in, 16)
            def iteration(a, b, c):
                take_units({"a": stage_a(a) if a is not None else None, "b": stage_b(b) if b is not None else None,
                            "c": stage_c(c) if c is not None else None})

            iteration(0, None, None)
            iteration(1, 0, None)
            with pe.Fori(2, GROUPS) as i:
                iteration(i, i - 1, i - 2)
            iteration(None, GROUPS - 1, GROUPS - 2)
            iteration(None, None, GROUPS - 1)


def shape_constants():
    c = np.zeros((128, NCONST), np.float32)
    i = np.arange(128)
    c[:, C_ID:C_ID + 128] = np.eye(128)
    c[:, C_CENTER:C_CENTER + 128] = np.eye(128) - 1.0 / D
    c[:, C_MEAN:C_MEAN + 128] = 1.0 / D
    c[:, C_HEADSUM:C_HEADSUM + 128] = i[:, None] // FHD == i[None, :] // FHD
    t = np.arange(PAIR)
    same = t[:, None] // QPOS == t[None, :] // QPOS
    c[:PAIR, C_CAUSAL:C_CAUSAL + PAIR] = same & (t[:, None] <= t[None, :])
    c[:PAIR, C_ADDMASK:C_ADDMASK + PAIR] = np.where(same & (t[None, :] <= t[:, None]), 0.0, NEG)
    c[:, C_HMASK:C_HMASK + LHEADS] = i[:, None] // LHD == np.arange(LHEADS)[None, :]
    c[:, C_T:C_T + QPOS] = np.arange(QPOS)
    c[:, C_IOTA] = i
    c[:, C_IOTA + 1] = i + HALF
    c[:, C_EPS:C_EPS + 5] = (EPS, EPS * EPS, 1e-12, 1.0, 3.0)
    return c


def kernel(**inputs):
    import concourse.bacc as _bacc
    from concourse.bass_utils import run_bass_kernel_spmd as _run

    a = {k.replace("L0_", ""): np.asarray(v) for k, v in inputs.items()}
    assert a["tok_attention_biases"].shape[1] == NOFF == 2 * HALF
    x = a["x"]
    kv = a["tok_kv_w"].reshape(HEADS, KD + VD, CIN)

    par = np.zeros((128, NPAR), np.float32)
    for k, s in enumerate("gbmv"):
        par[:, P_PROJ + k] = a["tok_proj_" + s]
        par[:KD, P_BNQ + HEADS * k:P_BNQ + HEADS * (k + 1)] = a["tok_q_" + s].reshape(HEADS, KD).T
        kvp = a["tok_kv_" + s].reshape(HEADS, KD + VD)
        par[:KD, P_BNK + HEADS * k:P_BNK + HEADS * (k + 1)] = kvp[:, :KD].T
        par[:VD, P_BNV + HEADS * k:P_BNV + HEADS * (k + 1)] = kvp[:, KD:].T
    par[:, P_BQ] = a["attn_bqkv"][0:D]
    par[:, P_BK] = a["attn_bqkv"][D:2 * D]
    for col, name in ((P_BOUT, "attn_bout"), (P_GAMMA, "attn_ln_gamma"), (P_BETA, "attn_ln_beta"), (P_FG, "ffn_ln_g"),
                      (P_FB, "ffn_ln_b")):
        par[:, col] = a[name]
    par[:, P_QN] = np.tile(a["ffn_qn_g"], FHEADS)
    par[:, P_KN] = np.tile(a["ffn_kn_g"], FHEADS)
    par[:, P_DEC] = np.repeat(a["attn_decay_logits"], LHD)
    par[:, P_B1:P_B1 + EXPERTS * FCH] = a["ffn_b1"].reshape(EXPERTS * FCH, 128).T
    par[:, P_B2:P_B2 + EXPERTS] = a["ffn_b2"].T

    arrays = {
        "xT": x.transpose(2, 0, 1).reshape(CIN, BATCH * KPOS),
        "xn": x.reshape(BATCH, 2, HALF, CIN).transpose(2, 0, 1, 3),
        "consts": shape_constants(),
        "params": par,
        "qw": a["tok_q_w"].reshape(HEADS, KD, CIN).transpose(1, 0, 2),
        "kw": kv[:, :KD].transpose(1, 0, 2),
        "vw": kv[:, KD:].transpose(1, 0, 2),
        "pw": a["tok_proj_w"],
        "ab": a["tok_attention_biases"].T.reshape(2, HALF, HEADS).transpose(1, 0, 2),
        "idxs": a["tok_bias_idxs"].reshape(7, 1, QPOS * KPOS // 7),
        "wqkv": a["attn_Wqkv"],
        "bqkv": a["attn_bqkv"].reshape(1, 3 * D),
        "wout": a["attn_Wout"],
        "fwq": a["ffn_Wq"], "fwk": a["ffn_Wk"], "fwv": a["ffn_Wv"], "fwo": a["ffn_Wo"],
        "gw": a["ffn_gate_W"],
        "gb": a["ffn_gate_b"].reshape(1, EXPERTS),
        "w1": a["ffn_W1"].transpose(1, 0, 2),
        "w2": a["ffn_W2"].reshape(EXPERTS * FCH, 128, D).transpose(1, 0, 2),
    }
    nc = _bacc.Bacc("TRN2", target_bir_lowering=False, num_devices=1)
    given, args = {}, []
    for name, v in arrays.items():
        v = np.ascontiguousarray(v)
        given[f"in_{name}"] = v
        args.append(nc.dram_tensor(f"in_{name}", v.shape, mybir.dt.from_np(v.dtype), kind="ExternalInput").ap())
    bias_dram = nc.dram_tensor("bias_rows_dram", (HEADS, 7, QPOS * KPOS // 7), F32, kind="Internal").ap()
    gate_dram = nc.dram_tensor("gate_rows_dram", (EXPERTS, TOK), F32, kind="Internal").ap()
    out = nc.dram_tensor("out_dram", (BATCH * QPOS, D), F32, kind="ExternalOutput").ap()
    audio_tower_kernel(nc, *args, bias_dram, gate_dram, out)
    r = _run(nc, [given], core_ids=[0])
    return r.results[0]["out_dram"].reshape(BATCH, QPOS, D)
```

```python
from contextlib import ExitStack

import concourse.bass as bass
import numpy as np
from concourse import mybir

F32 = mybir.dt.float32
I32 = mybir.dt.int32
BF16 = mybir.dt.bfloat16
ALU = mybir.AluOpType
ACT = mybir.ActivationFunctionType
AX = mybir.AxisListType

BATCH, RES, OUT_RES, CIN = 64, 14, 7, 96
KPOS, QPOS = RES * RES, OUT_RES * OUT_RES
HEADS, KD, VD = 12, 32, 64
D = 128
LHEADS, LHD = 8, 16
FHEADS, FHD = 2, 64
EXPERTS, FF = 8, 512
NOFF = 196
EPS = 1e-5

NB = 8
GROUPS = BATCH // NB
TOK = NB * QPOS
CA = CIN + 1
HALF = KPOS // 2
ROWS = HEADS * QPOS
TILES = 5
MT = 118
PAIR = 2 * QPOS
PAIRS = NB // 2
FCH = FF // 128
NCHUNK = 7
CHUNK = QPOS * KPOS // NCHUNK
NSUB = 4
PARTS = 3
SUB = CHUNK // NSUB
NEG = -3.0e38


def tile_rows(t):
    return min(MT, ROWS - MT * t)


C_ID, C_CENTER, C_MEAN, C_HEADSUM, C_CAUSAL, C_ADDMASK, C_HMASK, C_T, C_IOTA = (
    0, 128, 256, 384, 512, 610, 708, 716, 765)
C_EPS = 767
NCONST = 772

P_PROJ, P_BQ, P_BK, P_BOUT, P_GAMMA, P_BETA, P_FG, P_FB, P_QN, P_KN, P_DEC, P_B1, P_B2, P_BNQ, P_BNK, P_BNV = (
    0, 4, 5, 6, 7, 8, 9, 10, 11, 12, 13, 14, 46, 54, 102, 150)
NPAR = 198


class Steps:

    def __init__(self, sem, names):
        self.sem, self.names = sem, names
        self.index = {n: i for i, n in enumerate(names)}
        self.per_group = len(names)
        self.told = 0

    def at(self, g, name, back=0):
        return (g + 1 - back) * self.per_group + self.index[name] + 1

    def tell(self, name):
        assert self.names[self.told % self.per_group] == name, (name, self.names[self.told % self.per_group])
        self.told += 1
        return self.sem


NORM_PARTS = ((0, 1, 2), (3, 4))


def wide(ap, axis, n):
    shape = list(ap.shape)
    return ap.unsqueeze(axis).broadcast_to(tuple(shape[:axis] + [n] + shape[axis:]))


def steps_a():
    pe = [f"qk{h}" for h in range(HEADS)]
    act = [f"qk{h}" for h in range(0, HEADS, 2)]
    dve = [f"qk{h}" for h in range(1, HEADS, 2)]
    for b in range(-1, NB):
        if b >= 0:
            pe += [f"tr{b}.{j}" for j in range(3)]
            act += [f"pt{b}.0", f"pt{b}.2"]
            dve += [f"pt{b}.1"]
        if b + 1 < NB:
            pe += [f"s{b + 1}.{j}" for j in range(3)]
            act += [f"exp{b + 1}.{t}" for t in range(TILES)]
            dve += [f"neg{b + 1}.{t}" for t in range(TILES)] 
            for part, tiles in enumerate(NORM_PARTS):
                dve += [f"rec{b + 1}.{part}"] + [f"norm{b + 1}.{t}" for t in tiles]
        if b >= 0:
            pe += [f"t{b}.{n}" for n in range(2)]
            act += [f"tt{b}.0"]
            dve += [f"tt{b}.1"]
    pe += [f"wv{j}" for j in range(HEADS // 2)]
    act += [f"relu{j}" for j in range(HEADS // 2)]
    dve += [f"hs{j}" for j in range(HEADS // 2)]
    return pe, act, dve


def steps_b():
    pe = ["proj", "c1", "v1", "q", "k", "v"]
    act = ["h1", "c1", "sq1", "ln1", "rs1", "eq", "pq", "ek", "pk"]
    dve = ["hn", "q", "k", "v"]
    pool = ["q", "k"]
    for p in range(PAIRS):
        pool += [f"qm{p}"]
        pe += [f"a{p}.0", f"a{p}.1"]
        dve += [f"a{p}.0", f"a{p}.1"]
        if p % 2:
            pe += [f"num{p // 2}"]
            dve += [f"den{p // 2}", f"rden{p // 2}", f"o{p // 2}"]
    pe += ["oT", "wout", "v2", "c3", "v3", "q2", "k2", "qss", "kss", "vx", "s0", "s1", "pT0", "pT1", "av", "wo",
           "g", "gT"]
    act += ["oT", "c2", "sq2", "ln2", "rs2", "c3", "sq3", "ln3", "rs3", "q2", "qsq", "k2", "ksq", "qln", "qrs",
            "kln", "krs", "vx", "e0", "e1", "pT0", "pT1", "o2T", "y", "gexp"]
    dve += ["ga", "h2", "gx", "hx", "q2n", "k2n", "sm0", "mx0", "sub0", "sm1", "mx1", "sub1",
            "sum0", "rc0", "pn0", "sum1", "rc1", "pn1", "g", "gmx", "gsub", "gsum", "grc", "gn", "gT"]
    return pe, act, dve, pool


def steps_c():
    ej = [(e, j) for e in range(EXPERTS) for j in range(FCH)]
    pe = []
    for n, (e, j) in enumerate(ej):
        pe += [f"u{e}.{j}"]
        if n:
            pe += ["d%d.%d" % ej[n - 1]]
    pe += ["d%d.%d" % ej[-1], "ot"]
    act = [f"g{e}.{j}" for e, j in ej] + ["ot"]
    dve = []
    for e in range(EXPERTS):
        dve += [f"m{e}", f"acc{e}"]
    return pe, act, dve


UNITS_A = HEADS // 2 + 5 * NB + HEADS // 2
B_UNITS = """proj c1 v1 hn q k v a0.0 a0.1 a1.0 a1.1 num0 a2.0 a2.1 a3.0 a3.1 num1 oT wout v2 h2 c3 v3 hx q2 k2 qss kss
             q2n vx s0 s1 exp pn0 pn1 pT0 pT1 av wo g gexp gT""".split()


def schedule(group_a, group_b, group_c):
    if group_c is None:
        plan = """
            a proj a c1 a v1 hn a a a q a k a
            v     a        a0.0     a0.1 a         a    a a a1.0
            a1.1  a        num0     a2.0 a         a    a a a2.1
            a3.0  a        a3.1     num1 a         a    a a
            oT    a        wout     v2   a h2      a    a a
            c3    a        v3            a hx      a    a a
            q2    a        k2 qss        a kss q2n a    a a vx
            s0    a        s1 exp        a         a pn0 pn1 a a
            pT0 a pT1 a av a a wo a a g a gexp a a gT
            """
    elif group_a is None:
        plan = """
            c c proj c c1 c x v1 hn q k y c v c a0.0 c a0.1 c a1.0 c a1.1 c num0 c a2.0 c a2.1 c a3.0 c a3.1 c num1
            c oT c wout x v2 h2 y c c3 x v3 hx y c q2 c k2 x qss kss q2n y c vx c s0 c s1 c x exp pn0 pn1 y
            c c pT0 c pT1 c av c c c c wo g gexp c gT c
            """
    else:
        plan = """
            c proj c a c c x a c1 a v1 hn a a a q a k a
            c v a c a0.0 c a0.1 c x a a a a a1.0
            c a1.1 a c num0 c a2.0 c x a a a a a2.1
            c a3.0 a c a3.1 c num1 c x a a a a
            c oT a c wout c c x v2 a h2 a a a
            c c3 a c c c x v3 a hx a a a
            c q2 a c k2 c c x qss a kss q2n a a a vx
            c s0 a c s1 c c x exp a a pn0 pn1 a a
            c pT0 a pT1 a av a a wo a a g a a gexp a c gT
            """
    order = plan.split()
    assert [u for u in order if u not in ("a", "c", "x", "y")] == B_UNITS
    assert group_a is None or order.count("a") == UNITS_A
    assert group_c is None or order.count("c") == EXPERTS * FCH + 2
    return order


def nothing(units):
    for _ in range(units):
        yield


def take_units(groups, stages, tables=None):
    in_turn = dict(zip("abc", groups))
    running = {s: stages[s](g) for s, g in in_turn.items() if g is not None and stages.get(s) is not None}
    for u in schedule(*groups):
        if u in ("x", "y"):
            if tables is not None and in_turn["b"] is not None and in_turn["c"] is not None:
                tables(u)
        else:
            next(running.get(u if u in ("a", "c") else "b", iter(())), None)
    for stage in running.values():
        assert next(stage, "ended") == "ended"


def audio_tower_kernel(nc, xT, xn, consts, params, qw, kw, vw, pw, ab, idxs, wqkv, bqkv, wout, fwq, fwk, fwv, fwo,
                       gw, gb, w1, w2, bias_dram, gate_dram, out):
    with ExitStack() as ctx:
        def sb(name, shape, dt=F32):
            return ctx.enter_context(nc.sbuf_tensor(name, shape, dt))

        def sem(name):
            return ctx.enter_context(nc.semaphore(name))

        cst = sb("cst", [128, NCONST])
        par = sb("par", [128, NPAR])
        ident = cst[:, C_ID:C_ID + 128]
        center = cst[:, C_CENTER:C_CENTER + 128]
        mean = cst[:, C_MEAN:C_MEAN + 128]
        headsum = cst[:, C_HEADSUM:C_HEADSUM + 128]
        causal = cst[0:PAIR, C_CAUSAL:C_CAUSAL + PAIR]
        addmask = cst[0:PAIR, C_ADDMASK:C_ADDMASK + PAIR]
        hmask = cst[:, C_HMASK:C_HMASK + LHEADS]
        eps_col = cst[:, C_EPS:C_EPS + 1]
        eps2_col = cst[:, C_EPS + 1:C_EPS + 2]
        eps12_col = cst[:, C_EPS + 2:C_EPS + 3]
        one_col = cst[:, C_EPS + 3:C_EPS + 4]
        three_col = cst[:, C_EPS + 4:C_EPS + 5]
        abt = sb("abt", [HALF, 2, HEADS])
        ab_parts = sb("ab_parts", [HALF, 2, PARTS, HEADS], BF16)
        ab_rest = sb("ab_rest", [HALF, PARTS - 1, 2, HEADS])
        wqkv_s = sb("wqkv_s", [D, 3 * D])
        wout_s = sb("wout_s", [D, D])
        fw = sb("fw", [D, 4, D])
        gws = sb("gws", [D, EXPERTS])
        gbs = sb("gbs", [PAIR, EXPERTS])
        bvs = sb("bvs", [PAIR, D])
        w1s = sb("w1s", [D, EXPERTS, FF])
        w2s = sb("w2s", [D, EXPERTS * FCH, D])
        mqk = sb("mqk", [CA, HEADS, CA])
        wvT = sb("wvT", [CA, HEADS, VD])
        pwT = sb("pwT", [D, HEADS // 2, D])
        bias = sb("bias", [MT, TILES, KPOS])
        bn = sb("bn", [128, 6, HEADS])
        proj_s = sb("proj_s", [128, 4])
        decq = sb("decq", [128, QPOS])
        deck = sb("deck", [128, QPOS])
        nl = sb("nl", [128, 3])
        kn_scale = sb("kn_scale", [128, 1])
        bout_c, row_mean = sb("bout_c", [128, 1]), sb("row_mean", [128, 2])

        xa = sb("xa", [CA, NB, KPOS])
        xp = sb("xp", [HALF, NB, 2, CA])
        qp_all = sb("qp", [128, NB, ROWS])
        qp = qp_all[0:CA, :, :]
        sneg = sb("sneg", [MT, TILES, KPOS])
        prob = sb("prob", [MT, TILES, KPOS])
        stat = sb("stat", [MT, 3, 8])
        pT = sb("pT", [HALF, 2, ROWS])
        tT_all = sb("tT", [128, HEADS, TOK])
        tT = tT_all[0:CA, :, :]
        relu = sb("relu", [128, 2, TOK])
        hs = sb("hs", [128, HEADS // 2, TOK])

        def feat(name):
            return sb(name, [128, TOK])
        h1T, cT, sq, lnb, r, hnT = feat("h1T"), feat("cT"), feat("sq"), feat("lnb"), feat("r"), feat("hnT")
        eq, pq, ek, pk, qd, kd, qT, kT = (feat(n) for n in ("eq", "pq", "ek", "pk", "qd", "kd", "qT", "kT"))
        ksq = hnT
        ga, gx, q2T, k2T, q2n, k2n = eq, pq, ek, pk, qd, kd
        v1 = sb("v1", [PAIR, PAIRS, LHEADS, LHD + 1])
        qm = sb("qm", [128, 2, LHEADS, PAIR])
        aT = sb("aT", [PAIR, 2, LHEADS, PAIR])
        den = sb("den", [PAIR, 2, 16])
        lo = sb("lo", [PAIR, PAIRS, D])
        oT, h2T, hxT, r2 = (feat(n) for n in ("oT", "h2T", "hxT", "r2"))
        v2 = sb("v2", [PAIR, PAIRS, D])
        s2, p2 = (aT[:, i, :, :].rearrange("p (h n) q -> p h n q", h=FHEADS) for i in range(2))
        st2 = sb("st2", [PAIR, 3, FHEADS, PAIRS])
        p2T = qm[0:PAIR, 0, :, :].rearrange("p (h n) q -> p h n q", h=FHEADS)
        o2T, yT = feat("o2T"), feat("yT")
        gl = sb("gl", [PAIR, 3, PAIRS, EXPERTS])
        gst = sb("gst", [PAIR, 3, PAIRS])
        gT = sb("gT", [EXPERTS, TOK])

        acc = feat("acc")
        gbc = sb("gbc", [128, EXPERTS, TOK])
        hid = sb("hid", [128, 2, TOK])
        tmp = feat("tmp")
        outs = sb("outs", [PAIR, PAIRS, D])

        early = hs[0:KD, :, :].rearrange("p a b -> p (a b)")
        qwa, kwa = (early[:, i * HEADS * CA:(i + 1) * HEADS * CA].rearrange("p (h c) -> p h c", h=HEADS) for i in range(2))
        late = gbc[:, :, :].rearrange("p a b -> p (a b)")
        vwa = late[0:VD, 0:HEADS * CA].rearrange("p (h c) -> p h c", h=HEADS)
        pws = late[:, HEADS * CA:HEADS * CA + HEADS * VD]
        idx_room = tT_all[0:HALF, :, :].rearrange("p a b -> p (a b)")
        idx_i = [idx_room[:, i * CHUNK:(i + 1) * CHUNK].bitcast(I32) for i in range(2)]
        idx_b = idx_room[:, 2 * CHUNK:2 * CHUNK + CHUNK // 2].bitcast(BF16)
        onehot = [room[0:HALF, :, :].rearrange("p a b -> p (a b)")[:, 0:CHUNK].bitcast(BF16)
                  .rearrange("p (k n) -> p k n", k=2) for room in (qp_all, w1s)]
        table_rows = w2s[0:PARTS * HEADS, :, :].rearrange("p a b -> p (a b)")[:, 0:2 * CHUNK].rearrange(
            "p (i n) -> p i n", i=2)

        def bank(name):
            return ctx.enter_context(nc.psum_tensor(name, [128, 512], F32))
        ps_s = [bank(f"ps_s{j}") for j in range(3)]
        ps_t = [bank(f"ps_t{n}") for n in range(2)]
        ps_b, ps_h, ps_e = bank("ps_b"), bank("ps_h"), bank("ps_e")
        value_banks = ps_t + ps_s[0:2]

        pe_a, act_a, dve_a = (Steps(sem(n), s) for n, s in zip(("pe_a", "act_a", "dve_a"), steps_a()))
        pe_b, act_b, dve_b, pool_b = (Steps(sem(n), s) for n, s in zip(("pe_b", "act_b", "dve_b", "pool_b"), steps_b()))
        pe_c, act_c, dve_c = (Steps(sem(n), s) for n, s in zip(("pe_c", "act_c", "dve_c"), steps_c()))

        def start_at_one_group(eng, *stages):
            for s in stages:
                eng.sem_inc(s.sem, s.per_group)

        dve_waited = sem("dve_waited")
        xa_in = [sem(f"xa_in{b}") for b in range(NB)]
        xp_in = [sem(f"xp_in{b}") for b in range(NB)]
        gate_out, gate_in, out_done = sem("gate_out"), sem("gate_in"), sem("out_done")
        consts_in, attn_w_in, ffn_w_in, w1_in, w2_in = (
            sem(n) for n in ("consts_in", "attn_w_in", "ffn_w_in", "w1_in", "w2_in"))
        idx_in, bias_out = ([sem(f"{n}{i}") for i in range(2)] for n in ("idx_in", "bias_out"))
        table_in, bias_in = sem("table_in"), sem("bias_in")
        dve_set, act_set, pe_set, ones_set = sem("dve_set"), sem("act_set"), sem("pe_set"), sem("ones_set")
        dve_table, act_table, pe_table = (sem(n) for n in ("dve_table", "act_table", "pe_table"))
        BN_STEPS = 6
        SPLIT_STEPS = 2 * PARTS - 1
        PWT_READ = SPLIT_STEPS + 4 * BN_STEPS + 3
        SETUP_STEPS = SPLIT_STEPS + 4 * BN_STEPS + 2 + 3 + 2 + 3

        key_banks = ((ps_t[0], range(0, 5)), (ps_t[1], range(5, 10)), (ps_s[2], range(10, HEADS)))
        value_weight_banks = ((ps_s[0], range(0, 8)), (ps_s[1], range(8, HEADS)))
        WEIGHT_BANKS = len(key_banks) + len(value_weight_banks)

        def hidden_banks(g):
            return (ps_h, ps_s[0]) if isinstance(g, int) and g == GROUPS - 1 else (ps_h,)

        def pT_evac(j):
            if j == 2:
                m = tile_rows(TILES - 1)
                return (pT[:, :, 4 * MT:ROWS], ps_s[2][0:HALF, 0:2 * MT].rearrange("p (c q) -> p c q", c=2)[:, :, 0:m])
            return (pT[:, :, 2 * MT * j:2 * MT * (j + 1)].rearrange("p c (t q) -> p t c q", t=2),
                    ps_s[j][0:HALF, 0:4 * MT].rearrange("p (t c q) -> p t c q", t=2, c=2))

        def tT_evac(b, n):
            return (tT[:, 6 * n:6 * n + 6, b * QPOS:(b + 1) * QPOS],
                    ps_t[n][0:CA, 0:6 * QPOS].rearrange("p (h q) -> p h q", h=6))

        block = ctx.enter_context(nc.Block())

        @block.sync
        def _(sp):
            sp.sem_inc(gate_out, 16)
            sp.sem_inc(out_done, 16)

            def load_idx(c):
                if c >= 2:
                    sp.wait_ge(dve_table, 3 * (c - 2) + 1)
                sp.dma_start(idx_i[c % 2], idxs[c].broadcast_to((HALF, CHUNK))).then_inc(idx_in[c % 2], 16)

            sp.dma_start(cst[:, :], consts).then_inc(table_in, 16)
            load_idx(0)
            sp.dma_start(abt[:, :, :], ab).then_inc(table_in, 16)
            load_idx(1)

            def load_x(g, b):
                sp.wait_ge(pe_a.sem, pe_a.at(g, f"s{b}.2", back=1))
                sp.dma_start(xa[0:CIN, b, :], xT[:, bass.ds((g * NB + b) * KPOS, KPOS)]).then_inc(xa_in[b], 16)
                sp.wait_ge(pe_a.sem, pe_a.at(g, f"t{b}.1", back=1))
                sp.dma_start(xp[:, b, :, 0:CIN], xn[:, bass.ds(g * NB + b, 1), :, :].rearrange("p b c f -> p (b c) f")
                             ).then_inc(xp_in[b], 16)

            def gates(g):
                sp.wait_ge(dve_b.sem, dve_b.at(g, "gT"))
                sp.dma_start(gate_dram[:, :], gT[:, :]).then_inc(gate_out, 16)
                sp.wait_ge(gate_out, (g + 2) * 16)
                sp.wait_ge(dve_c.sem, dve_c.at(g, f"m{EXPERTS - 1}", back=1))
                sp.dma_start(gbc[:, :, :], gate_dram[:, :].rearrange("(o e) t -> o e t", o=1).broadcast_to((128, EXPERTS, TOK))
                             ).then_inc(gate_in, 16)

            def results_out(g):
                sp.wait_ge(act_c.sem, act_c.at(g, "ot"))
                sp.dma_start(out[bass.ds(g * TOK, TOK), :].rearrange("(p t) d -> t p d", t=PAIR), outs[:, :, :]
                             ).then_inc(out_done, 16)

            sp.wait_ge(ones_set, 4)
            for c in range(2, NCHUNK):
                load_idx(c)
                if c < 4:
                    for b in range(NB // 2 * (c - 2), NB // 2 * (c - 1)):
                        load_x(0, b)
            sp.dma_start(wout_s[:, :], wout).then_inc(attn_w_in, 16)
            sp.dma_start(bvs[:, :], bqkv[:, 2 * D:3 * D].broadcast_to((PAIR, D))).then_inc(attn_w_in, 16)
            sp.dma_start(wqkv_s[:, :], wqkv).then_inc(attn_w_in, 16)
            for i in range(2):
                sp.wait_ge(bias_out[i], 16 * ((NCHUNK + 1 - i) // 2))
            for part, dst in enumerate((bias, sneg, prob)):
                rows = bias_dram[part * HEADS:(part + 1) * HEADS, :, :].rearrange("h c (q k) -> (h c q) k", k=KPOS)
                sp.dma_start(dst[:, 0:TILES - 1, :], rows[0:MT * (TILES - 1), :].rearrange("(t p) k -> p t k", p=MT)
                             ).then_inc(bias_in, 16)
                sp.dma_start(dst[0:tile_rows(TILES - 1), TILES - 1, :], rows[MT * (TILES - 1):ROWS, :]
                             ).then_inc(bias_in, 16)
            for i, w in enumerate((fwq, fwk, fwv, fwo)):
                sp.dma_start(fw[:, i, :], w).then_inc(ffn_w_in, 16)
            sp.dma_start(gws[:, :], gw).then_inc(ffn_w_in, 16)
            sp.dma_start(gbs[:, :], gb.broadcast_to((PAIR, EXPERTS))).then_inc(ffn_w_in, 16)
            sp.dma_start(w1s[:, :, :], w1).then_inc(w1_in, 16)
            sp.dma_start(w2s[:, :, :], w2).then_inc(w2_in, 16)

            def iteration(a, b, c):
                if a is not None:
                    for n in range(NB):
                        load_x(a, n)
                if b is not None:
                    gates(b)
                if c is not None:
                    results_out(c)

            iteration(1, None, None)
            iteration(2, 0, None)
            with sp.Fori(2, GROUPS - 1) as i:
                iteration(i + 1, i - 1, i - 2)
            iteration(None, GROUPS - 2, GROUPS - 3)
            iteration(None, GROUPS - 1, GROUPS - 2)
            iteration(None, None, GROUPS - 1)
            sp.wait_ge(out_done, 16 * (GROUPS + 1))

        @block.gpsimd
        def _(pool):
            start_at_one_group(pool, pool_b)
            nc.gpsimd.memset(xa[CIN:CA, :, :], 1.0).then_inc(ones_set, 1)
            pool.wait_ge(ones_set, 1)
            nc.gpsimd.memset(xp[:, :, :, CIN:CA], 1.0).then_inc(ones_set, 1)
            nc.gpsimd.memset(v1[:, :, :, LHD:LHD + 1], 1.0).then_inc(ones_set, 1)
            nc.gpsimd.memset(stat[:, :, :], 1.0).then_inc(ones_set, 1)

            def stage_b(g):
                def decayed(name, src, dst, dec):
                    pool.wait_ge(dve_b.sem, dve_b.at(g, name))
                    nc.gpsimd.tensor_tensor(dst[:, :].rearrange("p (b t) -> p b t", b=NB),
                                            src[:, :].rearrange("p (b t) -> p b t", b=NB),
                                            wide(dec[:, :], 1, NB), ALU.mult).then_inc(pool_b.tell(name), 1)

                def by_head(p):
                    pool.wait_ge(pool_b.sem, pool_b.at(g, "q"))
                    if p >= 2:
                        pool.wait_ge(pe_b.sem, pe_b.at(g, f"a{p - 2}.1"))
                    nc.gpsimd.tensor_tensor(qm[:, p % 2, :, :], wide(qT[:, p * PAIR:(p + 1) * PAIR], 1, LHEADS),
                                            wide(hmask, 2, PAIR), ALU.mult).then_inc(pool_b.tell(f"qm{p}"), 1)

                for name in B_UNITS:
                    if name == "q":
                        decayed("q", qd, qT, decq)
                    if name == "k":
                        decayed("k", kd, kT, deck)
                    if name == "v":
                        by_head(0)
                        by_head(1)
                    if name in ("a0.1", "a1.1"):
                        by_head(int(name[1]) + 2)
                    yield

            def iteration(a, b, c):
                take_units((a, b, c), {"b": stage_b})

            iteration(0, None, None)
            iteration(1, 0, None)
            with pool.Fori(2, GROUPS) as i:
                iteration(i, i - 1, i - 2)
            iteration(None, GROUPS - 1, GROUPS - 2)
            iteration(None, None, GROUPS - 1)

        @block.scalar
        def _(act):
            start_at_one_group(act, act_a, act_b, act_c)
            act.dma_start(par[:, :], params).then_inc(consts_in, 16)
            act.dma_start(qwa[:, :, 0:CIN], qw).then_inc(consts_in, 16)
            act.dma_start(kwa[:, :, 0:CIN], kw).then_inc(consts_in, 16)
            act.dma_start(vwa[:, :, 0:CIN], vw).then_inc(consts_in, 16)
            act.dma_start(pws[:, :], pw).then_inc(consts_in, 16)
            act.wait_ge(table_in, 2 * 16)
            act.wait_ge(consts_in, 5 * 16)
            for i, (n, col, w) in enumerate(((KD, P_BNQ, HEADS), (KD, P_BNK, HEADS), (VD, P_BNV, HEADS), (D, P_PROJ, 1))):
                dst = bn[0:n, i, 0:w] if i < 3 else proj_s[:, 0:1]
                nc.scalar.activation(dst, par[0:n, col + 3 * w:col + 4 * w], ACT.Sqrt, bias=eps_col[0:n, :]
                                     ).then_inc(act_set, 1)
            act.preload_act_table_set("natural_log_exp_and_others")
            nc.scalar.activation(nl[:, 0:1], par[:, P_DEC:P_DEC + 1], ACT.Exp, scale=-1.0).then_inc(act_set, 1)
            act.wait_ge(act_set, 5)
            nc.scalar.activation(nl[:, 1:2], nl[:, 0:1], ACT.Ln, bias=one_col).then_inc(act_set, 1)
            act.wait_ge(act_set, 6)
            nc.scalar.mul(nl[:, 2:3], nl[:, 1:2], -1.0).then_inc(act_set, 1)
            act.wait_ge(act_set, 7)
            tcol = cst[:, C_T:C_T + QPOS]
            nc.scalar.activation(deck[:, :], tcol, ACT.Exp, scale=nl[:, 1:2]).then_inc(act_set, 1)
            nc.scalar.activation(decq[:, :], tcol, ACT.Exp, scale=nl[:, 2:3]).then_inc(act_set, 1)
            def table_chunk(c):
                for s in range(NSUB):
                    act.wait_ge(pe_table, NSUB * c + s + 1)
                    if c >= 2 and s == 0:
                        act.wait_ge(bias_out[c % 2], 16 * (c // 2))
                    nc.scalar.copy(table_rows[:, c % 2, s * SUB:(s + 1) * SUB],
                                   (ps_b, ps_h)[s % 2][0:PARTS * HEADS, 0:SUB]
                                   ).then_inc(act_table, 1)
                act.wait_ge(act_table, NSUB * (c + 1))
                act.dma_start(bias_dram[:, c, :], table_rows[:, c % 2, :]).then_inc(bias_out[c % 2], 16)

            for c in range(NCHUNK):
                table_chunk(c)
            for n, (ps, heads) in enumerate(key_banks):
                act.wait_ge(pe_set, n + 1)
                nc.scalar.mul(mqk[:, heads[0]:heads[-1] + 1, :],
                              ps[0:CA, 0:len(heads) * CA].rearrange("p (h c) -> p h c", c=CA), KD ** -0.5
                              ).then_inc(act_set, 1)
            for n, (ps, heads) in enumerate(value_weight_banks):
                act.wait_ge(pe_set, len(key_banks) + n + 1)
                nc.scalar.copy(wvT[:, heads[0]:heads[-1] + 1, :],
                               ps[0:CA, 0:len(heads) * VD].rearrange("p (h d) -> p h d", d=VD)).then_inc(act_set, 1)

            def stage_a(g):
                def exponentials(b):
                    for t in range(TILES):
                        m = tile_rows(t)
                        act.wait_ge(dve_a.sem, dve_a.at(g, f"neg{b}.{t}"))
                        nc.scalar.activation(prob[0:m, t, :], sneg[0:m, t, :], ACT.Exp, bias=stat[0:m, 0, t:t + 1],
                                             scale=-1.0, accum_out=stat[0:m, 1, t:t + 1]
                                             ).then_inc(act_a.tell(f"exp{b}.{t}"), 1)

                for h in range(0, HEADS, 2):
                    act.wait_ge(pe_a.sem, pe_a.at(g, f"qk{h}"))
                    nc.scalar.copy(qp[:, :, h * QPOS:(h + 1) * QPOS],
                                   ps_t[0][0:CA, 0:TOK].rearrange("p (b q) -> p b q", b=NB)
                                   ).then_inc(act_a.tell(f"qk{h}"), 1)
                    yield
                yield
                exponentials(0)
                yield
                for b in range(NB):
                    for j in (0, 2):
                        act.wait_ge(pe_a.sem, pe_a.at(g, f"tr{b}.{j}"))
                        nc.scalar.copy(*pT_evac(j)).then_inc(act_a.tell(f"pt{b}.{j}"), 1)
                    yield
                    if b + 1 < NB:
                        yield
                        exponentials(b + 1)
                        yield
                    act.wait_ge(pe_a.sem, pe_a.at(g, f"t{b}.0"))
                    nc.scalar.copy(*tT_evac(b, 0)).then_inc(act_a.tell(f"tt{b}.0"), 1)
                    yield
                    yield
                for j in range(HEADS // 2):
                    if j >= 2:
                        act.wait_ge(dve_a.sem, dve_a.at(g, f"hs{j - 2}"))
                    act.wait_ge(pe_a.sem, pe_a.at(g, f"wv{j}"))
                    nc.scalar.activation(relu[:, j % 2, :], value_banks[j % len(value_banks)][:, 0:TOK], ACT.Relu, bias=three_col
                                         ).then_inc(act_a.tell(f"relu{j}"), 1)
                    yield

            def stage_b(g):
                tok = ps_b[:, 0:TOK]

                def centred(n):
                    act.wait_ge(pe_b.sem, pe_b.at(g, f"c{n}"))
                    nc.scalar.copy(cT[:, :], tok).then_inc(act_b.tell(f"c{n}"), 1)
                    nc.scalar.activation(sq[:, :], tok, ACT.Square).then_inc(act_b.tell(f"sq{n}"), 1)

                def inverse_root(pe_name, ln, rs, dst, bias_col, scale):
                    act.wait_ge(pe_b.sem, pe_b.at(g, pe_name))
                    nc.scalar.activation(lnb[:, :], tok, ACT.Ln, bias=bias_col, scale=scale).then_inc(act_b.tell(ln), 1)
                    act.wait_ge(act_b.sem, act_b.at(g, ln))
                    nc.scalar.activation(dst[:, :], lnb[:, :], ACT.Exp, scale=-0.5).then_inc(act_b.tell(rs), 1)

                act.wait_ge(pe_b.sem, pe_b.at(g, "proj"))
                nc.scalar.activation(h1T[:, :], tok, ACT.Identity, bias=proj_s[:, 2:3], scale=proj_s[:, 3:4]
                                     ).then_inc(act_b.tell("h1"), 1)
                yield
                centred(1)
                yield
                inverse_root("v1", "ln1", "rs1", r, eps_col, 1.0)
                yield
                yield
                for name, e, p, col in (("q", eq, pq, P_BQ), ("k", ek, pk, P_BK)):
                    act.wait_ge(pe_b.sem, pe_b.at(g, name))
                    nc.scalar.activation(e[:, :], tok, ACT.Exp, bias=par[:, col:col + 1]).then_inc(act_b.tell("e" + name), 1)
                    nc.scalar.activation(p[:, :], tok, ACT.Relu, bias=par[:, col:col + 1]).then_inc(act_b.tell("p" + name), 1)
                    yield
                yield from nothing(1 + 2 * PAIRS + PAIRS // 2)
                act.wait_ge(pe_b.sem, pe_b.at(g, "oT"))
                nc.scalar.copy(oT[:, :], tok).then_inc(act_b.tell("oT"), 1)
                yield
                act.wait_ge(pe_b.sem, pe_b.at(g, "wout"))
                nc.scalar.activation(cT[:, :], tok, ACT.Identity, bias=bout_c[:, :]).then_inc(act_b.tell("c2"), 1)
                nc.scalar.activation(sq[:, :], tok, ACT.Square, bias=bout_c[:, :]).then_inc(act_b.tell("sq2"), 1)
                yield
                inverse_root("v2", "ln2", "rs2", r, eps_col, 1.0)
                yield
                yield
                centred(3)
                yield
                inverse_root("v3", "ln3", "rs3", r, eps2_col, 1.0 + EPS)
                yield
                yield
                for name, dst, squares in (("q", q2T, sq), ("k", k2T, ksq)):
                    act.wait_ge(pe_b.sem, pe_b.at(g, name + "2"))
                    nc.scalar.copy(dst[:, :], tok).then_inc(act_b.tell(name + "2"), 1)
                    nc.scalar.activation(squares[:, :], tok, ACT.Square).then_inc(act_b.tell(name + "sq"), 1)
                    yield
                for name, rr in (("q", r), ("k", r2)):
                    if name == "k":
                        act.wait_ge(act_b.sem, act_b.at(g, "qrs"))
                    inverse_root(name + "ss", name + "ln", name + "rs", rr, eps12_col, 1.0)
                    yield
                yield
                act.wait_ge(pe_b.sem, pe_b.at(g, "vx"))
                nc.scalar.copy(v2[:, :, :], ps_b[0:PAIR, :].rearrange("p (n d) -> p n d", n=PAIRS)
                               ).then_inc(act_b.tell("vx"), 1)
                yield
                yield from nothing(2)
                for h in range(FHEADS):
                    act.wait_ge(dve_b.sem, dve_b.at(g, f"sub{h}"))
                    nc.scalar.activation(p2[:, h, :, :], s2[:, h, :, :], ACT.Exp).then_inc(act_b.tell(f"e{h}"), 1)
                yield
                yield from nothing(2)
                for h in range(FHEADS):
                    act.wait_ge(pe_b.sem, pe_b.at(g, f"pT{h}"))
                    nc.scalar.copy(p2T[:, h, :, :], ps_b[0:PAIR, 0:TOK].rearrange("p (n q) -> p n q", n=PAIRS)
                                   ).then_inc(act_b.tell(f"pT{h}"), 1)
                    yield
                act.wait_ge(pe_b.sem, pe_b.at(g, "av"))
                nc.scalar.copy(o2T[:, :], tok).then_inc(act_b.tell("o2T"), 1)
                yield
                act.wait_ge(pe_b.sem, pe_b.at(g, "wo"))
                act.wait_ge(pe_c.sem, pe_c.at(g, f"u{EXPERTS - 1}.{FCH - 1}", back=1))
                nc.scalar.copy(yT[:, :], tok).then_inc(act_b.tell("y"), 1)
                yield
                yield
                act.wait_ge(dve_b.sem, dve_b.at(g, "gsub"))
                nc.scalar.activation(gl[:, 1, :, :], gl[:, 0, :, :], ACT.Exp).then_inc(act_b.tell("gexp"), 1)
                yield
                yield

            def stage_c(g):
                banks = hidden_banks(g)
                for e in range(EXPERTS):
                    for j in range(FCH):
                        act.wait_ge(pe_c.sem, pe_c.at(g, f"u{e}.{j}"))
                        col = P_B1 + e * FCH + j
                        nc.scalar.activation(hid[:, j % 2, :], banks[j % len(banks)][:, 0:TOK], ACT.Gelu_apprx_tanh,
                                             bias=par[:, col:col + 1]).then_inc(act_c.tell(f"g{e}.{j}"), 1)
                        yield
                yield
                act.wait_ge(pe_c.sem, pe_c.at(g, "ot"))
                act.wait_ge(out_done, (g + 1) * 16)
                nc.scalar.copy(outs[:, :, :], ps_e[0:PAIR, :].rearrange("p (n d) -> p n d", n=PAIRS)
                               ).then_inc(act_c.tell("ot"), 1)
                yield

            def iteration(a, b, c):
                take_units((a, b, c), {"a": stage_a, "b": stage_b, "c": stage_c},
                           tables=lambda u: act.preload_act_table_set(
                               {"x": "natural_log_exp_and_others", "y": "gelu_apprx_tanh_and_others"}[u]))

            iteration(0, None, None)
            iteration(1, 0, None)
            with act.Fori(2, GROUPS) as i:
                iteration(i, i - 1, i - 2)
            iteration(None, GROUPS - 1, GROUPS - 2)
            iteration(None, None, GROUPS - 1)

        @block.vector
        def _(dve):
            start_at_one_group(dve, dve_a, dve_b, dve_c)
            told = [0]

            def then(ins):
                told[0] += 1
                ins.then_inc(dve_set, 1)
                dve.wait_ge(dve_set, told[0])

            def table_chunk(c):
                dve.wait_ge(idx_in[c % 2], 16 * (c // 2 + 1))
                if c:
                    dve.wait_ge(dve_table, 3 * c)
                nc.vector.tensor_copy(idx_b, idx_i[c % 2]).then_inc(dve_table, 1)
                dve.wait_ge(dve_table, 3 * c + 1)
                if c >= 2:
                    dve.wait_ge(pe_table, NSUB * (c - 1))
                for k in range(2):
                    nc.vector.tensor_scalar(onehot[c % 2][:, k, :], idx_b, cst[0:HALF, C_IOTA + k:C_IOTA + k + 1],
                                            None, ALU.is_equal).then_inc(dve_table, 1)

            dve.wait_ge(table_in, 2 * 16)
            rest = abt[:, :, :]
            for part in range(PARTS):
                then(nc.vector.tensor_copy(ab_parts[:, :, part, :], rest))
                if part < PARTS - 1:
                    then(nc.vector.tensor_tensor(ab_rest[:, part, :, :], rest, ab_parts[:, :, part, :], ALU.subtract))
                    rest = ab_rest[:, part, :, :]
            for c in range(NCHUNK):
                table_chunk(c)
            dve.wait_ge(consts_in, 5 * 16)
            for i, (n, col, w, wa) in enumerate(((KD, P_BNQ, HEADS, qwa), (KD, P_BNK, HEADS, kwa), (VD, P_BNV, HEADS, vwa),
                                                 (D, P_PROJ, 1, None))):
                dve.wait_ge(act_set, i + 1)
                root = bn[0:n, i, 0:w] if i < 3 else proj_s[:, 0:1]
                scale = bn[0:n, 3, 0:w] if i < 3 else proj_s[:, 1:2]
                prod = bn[0:n, 4, 0:w] if i < 3 else proj_s[:, 0:1]
                shift = bn[0:n, 5, 0:w] if i < 3 else proj_s[:, 2:3]
                gamma, beta, mu = (par[0:n, col + k * w:col + (k + 1) * w] for k in range(3))
                then(nc.vector.reciprocal(root, root))
                then(nc.vector.tensor_tensor(scale, gamma, root, ALU.mult))
                then(nc.vector.tensor_tensor(prod, mu, scale, ALU.mult))
                then(nc.vector.tensor_tensor(shift, beta, prod, ALU.subtract))
                if wa is not None:
                    then(nc.vector.tensor_tensor(wa[:, :, 0:CIN], wa[:, :, 0:CIN],
                                                 wide(scale, 2, CIN), ALU.mult))
                    then(nc.vector.tensor_copy(wa[:, :, CIN:CA], shift.unsqueeze(2)))
                else:
                    then(nc.vector.tensor_scalar(proj_s[:, 3:4], scale, 1.0 / 6.0, None, ALU.mult))
                    then(nc.vector.memset(den[:, :, :], 1.0))
            dve.wait_ge(act_set, 9)
            then(nc.vector.tensor_scalar(decq[:, :], decq[:, :], LHD ** -0.5, None, ALU.mult))
            then(nc.vector.tensor_scalar(kn_scale[:, :], par[:, P_KN:P_KN + 1], FHD ** 0.5, None, ALU.mult))
            for i in range(3):
                dve.wait_ge(pe_set, WEIGHT_BANKS + i + 1)
                then(nc.vector.tensor_copy(pwT[:, 2 * i:2 * i + 2, :],
                                           ps_s[2 if i % 2 == 0 else 1][:, 256:512].rearrange("p (n d) -> p n d", n=2)))
            dve.wait_ge(pe_set, WEIGHT_BANKS + 4)
            then(nc.vector.tensor_copy(bout_c[:, :], ps_s[0][:, 0:1]))
            then(nc.vector.memset(gl[:, 2, :, :], 0.0))
            dve.wait_ge(attn_w_in, 3 * 16)
            then(nc.vector.tensor_reduce(row_mean[:, 0:1], wout_s[:, :], AX.X, ALU.add))
            then(nc.vector.tensor_scalar(row_mean[:, 1:2], row_mean[:, 0:1], 1.0 / D, None, ALU.mult))
            then(nc.vector.tensor_scalar(wout_s[:, :], wout_s[:, :], row_mean[:, 1:2], None, ALU.subtract))
            dve.wait_ge(ones_set, 4)

            def whole_bias():
                dve.wait_ge(bias_in, 2 * PARTS * 16)
                dve.wait_ge(dve_a.sem, dve_a.at(0, f"qk{HEADS - 1}"))
                for part in (sneg, prob):
                    for t, m in ((slice(0, TILES - 1), MT), (slice(TILES - 1, TILES), tile_rows(TILES - 1))):
                        then(nc.vector.tensor_tensor(bias[0:m, t, :], bias[0:m, t, :], part[0:m, t, :], ALU.add))

            def stage_a(g):
                def negated_scores(b):
                    for t in range(TILES):
                        m = tile_rows(t)
                        if t % 2 == 0:
                            dve.wait_ge(pe_a.sem, pe_a.at(g, f"s{b}.{t // 2}"))
                            dve.sem_inc(dve_waited, 1)
                        nc.vector.tensor_tensor_reduce(
                            out=sneg[0:m, t, :], in0=ps_s[t // 2][0:m, (t % 2) * KPOS:(t % 2 + 1) * KPOS],
                            in1=bias[0:m, t, :], scale=-1.0, scalar=3.0e38, op0=ALU.add, op1=ALU.min,
                            accum_out=stat[0:m, 0, t:t + 1]).then_inc(dve_a.tell(f"neg{b}.{t}"), 1)

                for h in range(1, HEADS, 2):
                    dve.wait_ge(pe_a.sem, pe_a.at(g, f"qk{h}"))
                    nc.vector.tensor_copy(qp[:, :, h * QPOS:(h + 1) * QPOS],
                                          ps_t[1][0:CA, 0:TOK].rearrange("p (b q) -> p b q", b=NB)
                                          ).then_inc(dve_a.tell(f"qk{h}"), 1)
                    yield
                def normalised(b):
                    for part, tiles in enumerate(NORM_PARTS):
                        span = slice(tiles[0], tiles[-1] + 1)
                        dve.wait_ge(act_a.sem, act_a.at(g, f"exp{b}.{tiles[-1]}"))
                        nc.vector.reciprocal(stat[:, 2, span], stat[:, 1, span]).then_inc(dve_a.tell(f"rec{b}.{part}"), 1)
                        dve.wait_ge(dve_a.sem, dve_a.at(g, f"rec{b}.{part}"))
                        for t in tiles:
                            m = tile_rows(t)
                            nc.vector.tensor_scalar(prob[0:m, t, :], prob[0:m, t, :], stat[0:m, 2, t:t + 1], None,
                                                    ALU.mult).then_inc(dve_a.tell(f"norm{b}.{t}"), 1)

                if isinstance(g, int) and g == 0:
                    whole_bias()
                negated_scores(0)
                yield
                normalised(0)
                yield
                for b in range(NB):
                    dve.wait_ge(pe_a.sem, pe_a.at(g, f"tr{b}.1"))
                    nc.vector.tensor_copy(*pT_evac(1)).then_inc(dve_a.tell(f"pt{b}.1"), 1)
                    yield
                    if b + 1 < NB:
                        negated_scores(b + 1)
                        yield
                        normalised(b + 1)
                        yield
                    yield
                    dve.wait_ge(pe_a.sem, pe_a.at(g, f"t{b}.1"))
                    nc.vector.tensor_copy(*tT_evac(b, 1)).then_inc(dve_a.tell(f"tt{b}.1"), 1)
                    yield
                for j in range(HEADS // 2):
                    dve.wait_ge(act_a.sem, act_a.at(g, f"relu{j}"))
                    nc.vector.scalar_tensor_tensor(out=hs[:, j, :], in0=relu[:, j % 2, :], scalar=6.0,
                                                   in1=value_banks[j % len(value_banks)][:, 0:TOK], op0=ALU.min, op1=ALU.mult
                                                   ).then_inc(dve_a.tell(f"hs{j}"), 1)
                    yield

            def stage_b(g):
                tok = ps_b[:, 0:TOK]
                stt = nc.vector.scalar_tensor_tensor
                tt = nc.vector.tensor_tensor

                yield from nothing(3)
                dve.wait_ge(act_b.sem, act_b.at(g, "rs1"))
                tt(hnT[:, :], cT[:, :], r[:, :], ALU.mult).then_inc(dve_b.tell("hn"), 1)
                yield
                for name, e, p, dst in (("q", eq, pq, qd), ("k", ek, pk, kd)):
                    dve.wait_ge(act_b.sem, act_b.at(g, "p" + name))
                    stt(out=dst[:, :], in0=e[:, :], scalar=1.0, in1=p[:, :], op0=ALU.min, op1=ALU.add
                        ).then_inc(dve_b.tell(name), 1)
                    yield
                dve.wait_ge(pe_b.sem, pe_b.at(g, "v"))
                tt(v1[:, :, :, 0:LHD], ps_b[0:PAIR, :].rearrange("p (n h f) -> p n h f", n=PAIRS, h=LHEADS),
                   wide(bvs[:, :].rearrange("p (h f) -> p h f", h=LHEADS), 1, PAIRS), ALU.add
                   ).then_inc(dve_b.tell("v"), 1)
                yield
                for p in range(PAIRS):
                    for i in range(2):
                        dve.wait_ge(pe_b.sem, pe_b.at(g, f"a{p}.{i}"))
                        tt(aT[:, p % 2, 4 * i:4 * i + 4, :], ps_b[0:PAIR, 0:4 * PAIR].rearrange("p (h q) -> p h q", h=4),
                           wide(causal, 1, 4), ALU.mult).then_inc(dve_b.tell(f"a{p}.{i}"), 1)
                        yield
                    if p % 2:
                        n = p // 2
                        num = ps_b[0:PAIR, 0:16 * (LHD + 1)].rearrange("p (h f) -> p h f", h=16)
                        dve.wait_ge(pe_b.sem, pe_b.at(g, f"num{n}"))
                        nc.vector.tensor_scalar(den[:, 0, :].unsqueeze(2), num[:, :, LHD:LHD + 1], EPS, None, ALU.add
                                                ).then_inc(dve_b.tell(f"den{n}"), 1)
                        dve.wait_ge(dve_b.sem, dve_b.at(g, f"den{n}"))
                        nc.vector.reciprocal(den[:, 1, :], den[:, 0, :]).then_inc(dve_b.tell(f"rden{n}"), 1)
                        dve.wait_ge(dve_b.sem, dve_b.at(g, f"rden{n}"))
                        tt(lo[:, 2 * n:2 * n + 2, :].rearrange("p n (h f) -> p (n h) f", f=LHD), num[:, :, 0:LHD],
                           wide(den[:, 1, :], 2, LHD), ALU.mult).then_inc(dve_b.tell(f"o{n}"), 1)
                        yield
                yield from nothing(3)
                dve.wait_ge(act_b.sem, act_b.at(g, "rs2"))
                stt(out=ga[:, :], in0=cT[:, :], scalar=par[:, P_GAMMA:P_GAMMA + 1], in1=r[:, :], op0=ALU.mult,
                    op1=ALU.mult).then_inc(dve_b.tell("ga"), 1)
                dve.wait_ge(dve_b.sem, dve_b.at(g, "ga"))
                stt(out=h2T[:, :], in0=ga[:, :], scalar=par[:, P_BETA:P_BETA + 1], in1=h1T[:, :], op0=ALU.add,
                    op1=ALU.add).then_inc(dve_b.tell("h2"), 1)
                yield
                yield from nothing(2)
                dve.wait_ge(act_b.sem, act_b.at(g, "rs3"))
                stt(out=gx[:, :], in0=cT[:, :], scalar=par[:, P_FG:P_FG + 1], in1=r[:, :], op0=ALU.mult, op1=ALU.mult
                    ).then_inc(dve_b.tell("gx"), 1)
                dve.wait_ge(dve_b.sem, dve_b.at(g, "gx"))
                nc.vector.tensor_scalar(hxT[:, :], gx[:, :], par[:, P_FB:P_FB + 1], None, ALU.add
                                        ).then_inc(dve_b.tell("hx"), 1)
                yield
                yield from nothing(4)
                for name, src, rr, dst, col in (("q", q2T, r, q2n, par[:, P_QN:P_QN + 1]), ("k", k2T, r2, k2n, kn_scale[:, :])):
                    dve.wait_ge(act_b.sem, act_b.at(g, name + "rs"))
                    stt(out=dst[:, :], in0=src[:, :], scalar=col, in1=rr[:, :], op0=ALU.mult, op1=ALU.mult
                        ).then_inc(dve_b.tell(name + "2n"), 1)
                yield
                yield
                for h in range(FHEADS):
                    if h:
                        yield
                    dve.wait_ge(pe_b.sem, pe_b.at(g, f"s{h}"))
                    tt(s2[:, h, :, :], ps_b[0:PAIR, 0:TOK].rearrange("p (n k) -> p n k", n=PAIRS),
                       wide(addmask, 1, PAIRS), ALU.add).then_inc(dve_b.tell(f"sm{h}"), 1)
                    dve.wait_ge(dve_b.sem, dve_b.at(g, f"sm{h}"))
                    nc.vector.tensor_reduce(st2[:, 0, h, :], s2[:, h, :, :], AX.X, ALU.max).then_inc(dve_b.tell(f"mx{h}"), 1)
                    dve.wait_ge(dve_b.sem, dve_b.at(g, f"mx{h}"))
                    tt(s2[:, h, :, :], s2[:, h, :, :], wide(st2[:, 0, h, :], 2, PAIR), ALU.subtract
                       ).then_inc(dve_b.tell(f"sub{h}"), 1)
                yield
                yield
                for h in range(FHEADS):
                    dve.wait_ge(act_b.sem, act_b.at(g, f"e{h}"))
                    nc.vector.tensor_reduce(st2[:, 1, h, :], p2[:, h, :, :], AX.X, ALU.add).then_inc(dve_b.tell(f"sum{h}"), 1)
                    dve.wait_ge(dve_b.sem, dve_b.at(g, f"sum{h}"))
                    nc.vector.reciprocal(st2[:, 2, h, :], st2[:, 1, h, :]).then_inc(dve_b.tell(f"rc{h}"), 1)
                    dve.wait_ge(dve_b.sem, dve_b.at(g, f"rc{h}"))
                    tt(p2[:, h, :, :], p2[:, h, :, :], wide(st2[:, 2, h, :], 2, PAIR), ALU.mult
                       ).then_inc(dve_b.tell(f"pn{h}"), 1)
                    yield
                yield from nothing(4)
                dve.wait_ge(pe_b.sem, pe_b.at(g, "g"))
                tt(gl[:, 0, :, :], ps_b[0:PAIR, 0:PAIRS * EXPERTS].rearrange("p (n e) -> p n e", n=PAIRS),
                   wide(gbs[:, :], 1, PAIRS), ALU.add).then_inc(dve_b.tell("g"), 1)
                dve.wait_ge(dve_b.sem, dve_b.at(g, "g"))
                nc.vector.tensor_reduce(gst[:, 0, :], gl[:, 0, :, :], AX.X, ALU.max).then_inc(dve_b.tell("gmx"), 1)
                dve.wait_ge(dve_b.sem, dve_b.at(g, "gmx"))
                tt(gl[:, 0, :, :], gl[:, 0, :, :], wide(gst[:, 0, :], 2, EXPERTS), ALU.subtract
                   ).then_inc(dve_b.tell("gsub"), 1)
                yield
                dve.wait_ge(act_b.sem, act_b.at(g, "gexp"))
                nc.vector.tensor_reduce(gst[:, 1, :], gl[:, 1, :, :], AX.X, ALU.add).then_inc(dve_b.tell("gsum"), 1)
                dve.wait_ge(dve_b.sem, dve_b.at(g, "gsum"))
                nc.vector.reciprocal(gst[:, 2, :], gst[:, 1, :]).then_inc(dve_b.tell("grc"), 1)
                dve.wait_ge(dve_b.sem, dve_b.at(g, "grc"))
                tt(gl[:, 2, :, :], gl[:, 1, :, :], wide(gst[:, 2, :], 2, EXPERTS), ALU.mult
                   ).then_inc(dve_b.tell("gn"), 1)
                yield
                dve.wait_ge(pe_b.sem, pe_b.at(g, "gT"))
                dve.wait_ge(gate_out, (g + 1) * 16)
                nc.vector.tensor_copy(gT[:, :], ps_b[0:EXPERTS, 0:TOK]).then_inc(dve_b.tell("gT"), 1)
                yield

            def stage_c(g):
                def gated(e):
                    dve.wait_ge(pe_c.sem, pe_c.at(g, f"d{e}.{FCH - 1}"))
                    if e:
                        dve.wait_ge(dve_c.sem, dve_c.at(g, f"acc{e - 1}"))
                    nc.vector.scalar_tensor_tensor(out=tmp[:, :], in0=ps_e[:, 0:TOK], scalar=par[:, P_B2 + e:P_B2 + e + 1],
                                                   in1=gbc[:, e, :], op0=ALU.add, op1=ALU.mult
                                                   ).then_inc(dve_c.tell(f"m{e}"), 1)
                    dve.wait_ge(dve_c.sem, dve_c.at(g, f"m{e}"))
                    if e == 0:
                        dve.wait_ge(pe_c.sem, pe_c.at(g, "ot", back=1))
                    nc.vector.tensor_tensor(acc[:, :], acc[:, :] if e else h2T[:, :], tmp[:, :], ALU.add).then_inc(dve_c.tell(f"acc{e}"), 1)

                for e in range(EXPERTS):
                    if e == 1:
                        dve.wait_ge(gate_in, (g + 1) * 16)
                    if e:
                        gated(e - 1)
                    yield from nothing(FCH)
                gated(EXPERTS - 1)
                yield
                yield

            def iteration(a, b, c):
                take_units((a, b, c), {"a": stage_a, "b": stage_b, "c": stage_c})

            iteration(0, None, None)
            iteration(1, 0, None)
            with dve.Fori(2, GROUPS) as i:
                iteration(i, i - 1, i - 2)
            iteration(None, GROUPS - 1, GROUPS - 2)
            iteration(None, None, GROUPS - 1)

        @block.tensor
        def _(pe):
            start_at_one_group(pe, pe_a, pe_b, pe_c)
            mm = nc.tensor.matmul

            def table_chunk(c):
                pe.wait_ge(dve_table, 3 * (c + 1))
                for s in range(NSUB):
                    if s >= 2 or c:
                        pe.wait_ge(act_table, NSUB * c + s - 1)
                    for k in range(2):
                        last = mm((ps_b, ps_h)[s % 2][0:PARTS * HEADS, 0:SUB],
                                  ab_parts[:, k, :, :].rearrange("p i h -> p (i h)"),
                                  onehot[c % 2][:, k, s * SUB:(s + 1) * SUB], start=(k == 0), stop=(k == 1))
                    last.then_inc(pe_table, 1)

            pe.wait_ge(dve_set, SPLIT_STEPS)
            for c in range(NCHUNK):
                table_chunk(c)
            pe.wait_ge(dve_set, SPLIT_STEPS + 2 * BN_STEPS)
            for ps, heads in key_banks:
                for k, h in enumerate(heads):
                    last = mm(ps[0:CA, k * CA:(k + 1) * CA], qwa[:, h, :], kwa[:, h, :], start=True, stop=True)
                last.then_inc(pe_set, 1)
            pe.wait_ge(dve_set, SPLIT_STEPS + 3 * BN_STEPS)
            for ps, heads in value_weight_banks:
                for k, h in enumerate(heads):
                    last = nc.tensor.transpose(ps[0:CA, k * VD:(k + 1) * VD], vwa[:, h, :], ident[0:VD, 0:VD])
                last.then_inc(pe_set, 1)
            pe.wait_ge(act_set, 9 + WEIGHT_BANKS)
            for i in range(3):
                if i == 2:
                    pe.wait_ge(dve_set, PWT_READ)
                for k in range(2):
                    last = nc.tensor.transpose(ps_s[2 if i % 2 == 0 else 1][:, 256 + 128 * k:384 + 128 * k],
                                               pws[:, (2 * i + k) * 128:(2 * i + k + 1) * 128], ident)
                last.then_inc(pe_set, 1)
            mm(ps_s[0][:, 0:1], center, par[:, P_BOUT:P_BOUT + 1], start=True, stop=True).then_inc(pe_set, 1)
            pe.wait_ge(dve_set, SETUP_STEPS)
            pe.wait_ge(act_table, NSUB * NCHUNK)
            pe.wait_ge(ones_set, 4)

            def stage_a(g):
                def scores(b):
                    for j in range(3):
                        s = (act_a, dve_a, act_a)[j]
                        pe.wait_ge(s.sem, s.at(g, f"pt{b - 1}.{j}") if b else s.at(g, f"pt{NB - 1}.{j}", back=1))
                        for t in range(2 * j, min(2 * j + 2, TILES)):
                            m = tile_rows(t)
                            last = mm(ps_s[j][0:m, (t % 2) * KPOS:(t % 2 + 1) * KPOS], qp[:, b, MT * t:MT * t + m],
                                      xa[:, b, :], start=True, stop=True)
                        last.then_inc(pe_a.tell(f"s{b}.{j}"), 1)

                for b in range(NB):
                    pe.wait_ge(xa_in[b], (g + 1) * 16)
                for h in range(HEADS):
                    if h >= 2:
                        s = (act_a, dve_a)[h % 2]
                        pe.wait_ge(s.sem, s.at(g, f"qk{h - 2}"))
                    elif h == 0:
                        pe.wait_ge(dve_a.sem, dve_a.at(g, f"hs{HEADS // 2 - 1}", back=1))
                    xs = xa[:, :, :].rearrange("p b (i u j v) -> p b i u j v", i=OUT_RES, u=2, v=2)[:, :, :, 0, :, 0]
                    mm(ps_t[h % 2][0:CA, 0:TOK], mqk[:, h, :], xs, start=True, stop=True
                       ).then_inc(pe_a.tell(f"qk{h}"), 1)
                    if h % 2:
                        yield
                pe.wait_ge(act_a.sem, act_a.at(g, f"qk{HEADS - 2}"))
                pe.wait_ge(dve_a.sem, dve_a.at(g, f"qk{HEADS - 1}"))
                scores(0)
                yield
                yield
                for b in range(NB):
                    for j in range(3):
                        for t in range(2 * j, min(2 * j + 2, TILES)):
                            m = tile_rows(t)
                            pe.wait_ge(dve_a.sem, dve_a.at(g, f"norm{b}.{t}"))
                            for c in range(2):
                                col = (t % 2) * 2 * MT + c * MT
                                last = nc.tensor.transpose(ps_s[j][0:HALF, col:col + m],
                                                           prob[0:m, t, c * HALF:(c + 1) * HALF], ident[0:m, 0:m])
                        last.then_inc(pe_a.tell(f"tr{b}.{j}"), 1)
                    yield
                    if b + 1 < NB:
                        scores(b + 1)
                        yield
                        yield
                    pe.wait_ge(xp_in[b], (g + 1) * 16)
                    pe.wait_ge(act_a.sem, act_a.at(g, f"pt{b}.2"))
                    pe.wait_ge(dve_a.sem, dve_a.at(g, f"pt{b}.1"))
                    for n in range(2):
                        s = (act_a, dve_a)[n]
                        if b:
                            pe.wait_ge(s.sem, s.at(g, f"tt{b - 1}.{n}"))
                        for c in range(2):
                            last = mm(ps_t[n][0:CA, 0:6 * QPOS], xp[:, b, c, :],
                                      pT[:, c, 6 * QPOS * n:6 * QPOS * (n + 1)], start=(c == 0), stop=(c == 1))
                        last.then_inc(pe_a.tell(f"t{b}.{n}"), 1)
                        yield
                pe.wait_ge(act_a.sem, act_a.at(g, f"tt{NB - 1}.0"))
                pe.wait_ge(dve_a.sem, dve_a.at(g, f"tt{NB - 1}.1"))
                for j in range(HEADS // 2):
                    if j >= len(value_banks):
                        pe.wait_ge(dve_a.sem, dve_a.at(g, f"hs{j - len(value_banks)}"))
                    for i in range(2):
                        last = mm(value_banks[j % len(value_banks)][VD * i:VD * (i + 1), 0:TOK], wvT[:, 2 * j + i, :], tT[:, 2 * j + i, :],
                                  start=True, stop=True)
                    last.then_inc(pe_a.tell(f"wv{j}"), 1)
                    yield

            def stage_b(g):
                tok = ps_b[:, 0:TOK]

                def product(name, w, x):
                    mm(tok, w, x, start=True, stop=True).then_inc(pe_b.tell(name), 1)

                def token_rows(name, x, w, n):
                    for p in range(PAIRS):
                        last = mm(ps_b[0:PAIR, n * p:n * (p + 1)], x[:, p * PAIR:(p + 1) * PAIR], w, start=True, stop=True)
                    last.then_inc(pe_b.tell(name), 1)

                pe.wait_ge(dve_b.sem, dve_b.at(g, "gT", back=1))
                pe.wait_ge(dve_a.sem, dve_a.at(g, f"hs{HEADS // 2 - 1}"))
                for j in range(HEADS // 2):
                    last = mm(tok, pwT[:, j, :], hs[:, j, :], start=(j == 0), stop=(j == HEADS // 2 - 1))
                last.then_inc(pe_b.tell("proj"), 1)
                yield
                pe.wait_ge(act_b.sem, act_b.at(g, "h1"))
                product("c1", center, h1T[:, :])
                yield
                pe.wait_ge(act_b.sem, act_b.at(g, "sq1"))
                product("v1", mean, sq[:, :])
                yield
                yield
                pe.wait_ge(dve_b.sem, dve_b.at(g, "hn"))
                product("q", wqkv_s[:, 0:D], hnT[:, :])
                yield
                pe.wait_ge(act_b.sem, act_b.at(g, "pq"))
                product("k", wqkv_s[:, D:2 * D], hnT[:, :])
                yield
                pe.wait_ge(act_b.sem, act_b.at(g, "pk"))
                token_rows("v", hnT, wqkv_s[:, 2 * D:3 * D], D)
                yield
                pe.wait_ge(dve_b.sem, dve_b.at(g, "v"))
                pe.wait_ge(pool_b.sem, pool_b.at(g, "k"))
                for p in range(PAIRS):
                    pe.wait_ge(pool_b.sem, pool_b.at(g, f"qm{p}"))
                    for i in range(2):
                        if i:
                            pe.wait_ge(dve_b.sem, dve_b.at(g, f"a{p}.0"))
                        elif p == 2:
                            pe.wait_ge(dve_b.sem, dve_b.at(g, "o0"))
                        elif p:
                            pe.wait_ge(dve_b.sem, dve_b.at(g, f"a{p - 1}.1"))
                        mm(ps_b[0:PAIR, 0:4 * PAIR], kT[:, p * PAIR:(p + 1) * PAIR], qm[:, p % 2, 4 * i:4 * i + 4, :],
                           start=True, stop=True).then_inc(pe_b.tell(f"a{p}.{i}"), 1)
                        yield
                    if p % 2:
                        pe.wait_ge(dve_b.sem, dve_b.at(g, f"a{p}.1"))
                        for k in range(2):
                            for h in range(LHEADS):
                                col = (k * LHEADS + h) * (LHD + 1)
                                last = mm(ps_b[0:PAIR, col:col + LHD + 1], aT[:, k, h, :], v1[:, p - 1 + k, h, :],
                                          start=True, stop=True)
                        last.then_inc(pe_b.tell(f"num{p // 2}"), 1)
                        yield
                pe.wait_ge(dve_b.sem, dve_b.at(g, "o1"))
                for p in range(PAIRS):
                    last = nc.tensor.transpose(ps_b[:, p * PAIR:(p + 1) * PAIR], lo[:, p, :], ident[0:PAIR, 0:PAIR])
                last.then_inc(pe_b.tell("oT"), 1)
                yield
                pe.wait_ge(act_b.sem, act_b.at(g, "oT"))
                product("wout", wout_s[:, :], oT[:, :])
                yield
                pe.wait_ge(act_b.sem, act_b.at(g, "sq2"))
                product("v2", mean, sq[:, :])
                yield
                yield
                pe.wait_ge(dve_b.sem, dve_b.at(g, "h2"))
                product("c3", center, h2T[:, :])
                yield
                pe.wait_ge(act_b.sem, act_b.at(g, "sq3"))
                product("v3", mean, sq[:, :])
                yield
                yield
                pe.wait_ge(dve_b.sem, dve_b.at(g, "hx"))
                product("q2", fw[:, 0, :], hxT[:, :])
                yield
                pe.wait_ge(act_b.sem, act_b.at(g, "qsq"))
                product("k2", fw[:, 1, :], hxT[:, :])
                yield
                pe.wait_ge(act_b.sem, act_b.at(g, "ksq"))
                product("qss", headsum, sq[:, :])
                yield
                pe.wait_ge(act_b.sem, act_b.at(g, "qln"))
                product("kss", headsum, ksq[:, :])
                yield
                yield
                pe.wait_ge(act_b.sem, act_b.at(g, "kln"))
                token_rows("vx", hxT, fw[:, 2, :], D)
                yield
                pe.wait_ge(act_b.sem, act_b.at(g, "vx"))
                pe.wait_ge(dve_b.sem, dve_b.at(g, "k2n"))
                for h in range(FHEADS):
                    if h:
                        pe.wait_ge(dve_b.sem, dve_b.at(g, "sm0"))
                    f = slice(FHD * h, FHD * (h + 1))
                    for p in range(PAIRS):
                        t = slice(p * PAIR, (p + 1) * PAIR)
                        last = mm(ps_b[0:PAIR, t], q2n[f, t], k2n[f, t], start=True, stop=True)
                    last.then_inc(pe_b.tell(f"s{h}"), 1)
                    yield
                yield from nothing(3)
                for h in range(FHEADS):
                    if h:
                        pe.wait_ge(act_b.sem, act_b.at(g, "pT0"))
                    pe.wait_ge(dve_b.sem, dve_b.at(g, f"pn{h}"))
                    for p in range(PAIRS):
                        last = nc.tensor.transpose(ps_b[0:PAIR, p * PAIR:(p + 1) * PAIR], p2[:, h, p, :],
                                                   ident[0:PAIR, 0:PAIR])
                    last.then_inc(pe_b.tell(f"pT{h}"), 1)
                    yield
                pe.wait_ge(act_b.sem, act_b.at(g, "pT1"))
                for h in range(FHEADS):
                    for p in range(PAIRS):
                        last = mm(ps_b[FHD * h:FHD * (h + 1), p * PAIR:(p + 1) * PAIR], v2[:, p, FHD * h:FHD * (h + 1)],
                                  p2T[:, h, p, :], start=True, stop=True)
                last.then_inc(pe_b.tell("av"), 1)
                yield
                pe.wait_ge(act_b.sem, act_b.at(g, "o2T"))
                product("wo", fw[:, 3, :], o2T[:, :])
                yield
                pe.wait_ge(act_b.sem, act_b.at(g, "y"))
                token_rows("g", yT, gws[:, :], EXPERTS)
                yield
                yield
                pe.wait_ge(dve_b.sem, dve_b.at(g, "gn"))
                for p in range(PAIRS):
                    last = nc.tensor.transpose(ps_b[0:EXPERTS, p * PAIR:(p + 1) * PAIR], gl[:, 2, p, :],
                                               ident[0:PAIR, 0:PAIR])
                last.then_inc(pe_b.tell("gT"), 1)
                yield

            def stage_c(g):
                banks = hidden_banks(g)

                def up(e, j):
                    n = e * FCH + j - len(banks)
                    if n >= 0:
                        pe.wait_ge(act_c.sem, act_c.at(g, f"g{n // FCH}.{n % FCH}"))
                    mm(banks[j % len(banks)][:, 0:TOK], w1s[:, e, 128 * j:128 * (j + 1)], yT[:, :], start=True, stop=True
                       ).then_inc(pe_c.tell(f"u{e}.{j}"), 1)

                def down(e, j):
                    pe.wait_ge(act_c.sem, act_c.at(g, f"g{e}.{j}"))
                    if j == 0:
                        if e:
                            pe.wait_ge(dve_c.sem, dve_c.at(g, f"m{e - 1}"))
                        else:
                            pe.wait_ge(act_c.sem, act_c.at(g, "ot", back=1))
                    mm(ps_e[:, 0:TOK], w2s[:, e * FCH + j, :], hid[:, j % 2, :], start=(j == 0), stop=(j == FCH - 1)
                       ).then_inc(pe_c.tell(f"d{e}.{j}"), 1)

                pe.wait_ge(act_b.sem, act_b.at(g, "y"))
                before = None
                for e in range(EXPERTS):
                    for j in range(FCH):
                        up(e, j)
                        if before:
                            down(*before)
                        before = (e, j)
                        yield
                down(*before)
                yield
                pe.wait_ge(dve_c.sem, dve_c.at(g, f"acc{EXPERTS - 1}"))
                for p in range(PAIRS):
                    last = nc.tensor.transpose(ps_e[0:PAIR, p * D:(p + 1) * D], acc[:, p * PAIR:(p + 1) * PAIR], ident)
                last.then_inc(pe_c.tell("ot"), 1)
                yield

            def iteration(a, b, c):
                take_units((a, b, c), {"a": stage_a, "b": stage_b, "c": stage_c})

            iteration(0, None, None)
            pe.wait_ge(attn_w_in, 3 * 16)
            pe.wait_ge(ffn_w_in, 6 * 16)
            iteration(1, 0, None)
            pe.wait_ge(w1_in, 16)
            pe.wait_ge(w2_in, 16)
            with pe.Fori(2, GROUPS) as i:
                iteration(i, i - 1, i - 2)
            iteration(None, GROUPS - 1, GROUPS - 2)
            iteration(None, None, GROUPS - 1)


def shape_constants():
    c = np.zeros((128, NCONST), np.float32)
    i = np.arange(128)
    c[:, C_ID:C_ID + 128] = np.eye(128)
    c[:, C_CENTER:C_CENTER + 128] = np.eye(128) - 1.0 / D
    c[:, C_MEAN:C_MEAN + 128] = 1.0 / D
    c[:, C_HEADSUM:C_HEADSUM + 128] = i[:, None] // FHD == i[None, :] // FHD
    t = np.arange(PAIR)
    same = t[:, None] // QPOS == t[None, :] // QPOS
    c[:PAIR, C_CAUSAL:C_CAUSAL + PAIR] = same & (t[:, None] <= t[None, :])
    c[:PAIR, C_ADDMASK:C_ADDMASK + PAIR] = np.where(same & (t[None, :] <= t[:, None]), 0.0, NEG)
    c[:, C_HMASK:C_HMASK + LHEADS] = i[:, None] // LHD == np.arange(LHEADS)[None, :]
    c[:, C_T:C_T + QPOS] = np.arange(QPOS)
    c[:, C_IOTA] = i
    c[:, C_IOTA + 1] = i + HALF
    c[:, C_EPS:C_EPS + 5] = (EPS, EPS * EPS, 1e-12, 1.0, 3.0)
    return c


def kernel(**inputs):
    import concourse.bacc as _bacc
    from concourse.bass_utils import run_bass_kernel_spmd as _run

    a = {k.replace("L0_", ""): np.asarray(v) for k, v in inputs.items()}
    assert a["tok_attention_biases"].shape[1] == NOFF == 2 * HALF
    x = a["x"]
    kv = a["tok_kv_w"].reshape(HEADS, KD + VD, CIN)

    par = np.zeros((128, NPAR), np.float32)
    for k, s in enumerate("gbmv"):
        par[:, P_PROJ + k] = a["tok_proj_" + s]
        par[:KD, P_BNQ + HEADS * k:P_BNQ + HEADS * (k + 1)] = a["tok_q_" + s].reshape(HEADS, KD).T
        kvp = a["tok_kv_" + s].reshape(HEADS, KD + VD)
        par[:KD, P_BNK + HEADS * k:P_BNK + HEADS * (k + 1)] = kvp[:, :KD].T
        par[:VD, P_BNV + HEADS * k:P_BNV + HEADS * (k + 1)] = kvp[:, KD:].T
    par[:, P_BQ] = a["attn_bqkv"][0:D]
    par[:, P_BK] = a["attn_bqkv"][D:2 * D]
    for col, name in ((P_BOUT, "attn_bout"), (P_GAMMA, "attn_ln_gamma"), (P_BETA, "attn_ln_beta"), (P_FG, "ffn_ln_g"),
                      (P_FB, "ffn_ln_b")):
        par[:, col] = a[name]
    par[:, P_QN] = np.tile(a["ffn_qn_g"], FHEADS)
    par[:, P_KN] = np.tile(a["ffn_kn_g"], FHEADS)
    par[:, P_DEC] = np.repeat(a["attn_decay_logits"], LHD)
    par[:, P_B1:P_B1 + EXPERTS * FCH] = a["ffn_b1"].reshape(EXPERTS * FCH, 128).T
    par[:, P_B2:P_B2 + EXPERTS] = a["ffn_b2"].T

    arrays = {
        "xT": x.transpose(2, 0, 1).reshape(CIN, BATCH * KPOS),
        "xn": x.reshape(BATCH, 2, HALF, CIN).transpose(2, 0, 1, 3),
        "consts": shape_constants(),
        "params": par,
        "qw": a["tok_q_w"].reshape(HEADS, KD, CIN).transpose(1, 0, 2),
        "kw": kv[:, :KD].transpose(1, 0, 2),
        "vw": kv[:, KD:].transpose(1, 0, 2),
        "pw": a["tok_proj_w"],
        "ab": a["tok_attention_biases"].T.reshape(2, HALF, HEADS).transpose(1, 0, 2),
        "idxs": a["tok_bias_idxs"].reshape(NCHUNK, 1, CHUNK),
        "wqkv": a["attn_Wqkv"],
        "bqkv": a["attn_bqkv"].reshape(1, 3 * D),
        "wout": a["attn_Wout"],
        "fwq": a["ffn_Wq"], "fwk": a["ffn_Wk"], "fwv": a["ffn_Wv"], "fwo": a["ffn_Wo"],
        "gw": a["ffn_gate_W"],
        "gb": a["ffn_gate_b"].reshape(1, EXPERTS),
        "w1": a["ffn_W1"].transpose(1, 0, 2),
        "w2": a["ffn_W2"].reshape(EXPERTS * FCH, 128, D).transpose(1, 0, 2),
    }
    nc = _bacc.Bacc("TRN2", target_bir_lowering=False, num_devices=1)
    given, args = {}, []
    for name, v in arrays.items():
        v = np.ascontiguousarray(v)
        given[f"in_{name}"] = v
        args.append(nc.dram_tensor(f"in_{name}", v.shape, mybir.dt.from_np(v.dtype), kind="ExternalInput").ap())
    bias_dram = nc.dram_tensor("bias_rows_dram", (PARTS * HEADS, NCHUNK, CHUNK), F32, kind="Internal").ap()
    gate_dram = nc.dram_tensor("gate_rows_dram", (EXPERTS, TOK), F32, kind="Internal").ap()
    out = nc.dram_tensor("out_dram", (BATCH * QPOS, D), F32, kind="ExternalOutput").ap()
    audio_tower_kernel(nc, *args, bias_dram, gate_dram, out)
    r = _run(nc, [given], core_ids=[0])
    return r.results[0]["out_dram"].reshape(BATCH, QPOS, D)
```
